# Optimizing a Trainium2 kernel written in Bass

```python
import numpy as np
import jax
import jax.numpy as jnp

def _softmax(x, axis=-1):
    return jax.nn.softmax(x, axis=axis)

def _gelu(x):
    return jax.nn.gelu(x, approximate=True)

def _silu(x):
    return jax.nn.silu(x)

def _sigmoid(x):
    return jax.nn.sigmoid(x)

def _layernorm(x, axis=-1, eps=1e-05):
    m = jnp.mean(x, axis=axis, keepdims=True)
    v = jnp.var(x, axis=axis, keepdims=True)
    return (x - m) / jnp.sqrt(v + eps)

def _scatter_add(tgt, idx, src, axis=0):
    return tgt.at[idx].add(src)

def _segment_sum(src, seg, n):
    return jax.ops.segment_sum(src, seg, n)
kernel_name = 'mk_seq_postln_d1_jaxref_r4_4de256'

def setup_inputs(seed: int=0):
    np.random.seed(seed)
    _w = jnp.asarray

    def _L0_attn_setup():
        import jax, jax.numpy as jnp
        import numpy as np
        HIDDEN = 256
        HEADS = 16
        key = jax.random.key(seed)
        ks = jax.random.split(key, 7)
        s = 1.0 / np.sqrt(HIDDEN)
        return {'x': jax.random.normal(ks[0], (4, 1024, HIDDEN), dtype=jnp.float32), 'Wq': jax.random.uniform(ks[1], (HIDDEN, HIDDEN), jnp.float32, -s, s), 'bq': jax.random.uniform(ks[2], (HIDDEN,), jnp.float32, -s, s), 'Wk': jax.random.uniform(ks[3], (HIDDEN, HIDDEN), jnp.float32, -s, s), 'bk': jax.random.uniform(ks[4], (HIDDEN,), jnp.float32, -s, s), 'Wv': jax.random.uniform(ks[5], (HIDDEN, HIDDEN), jnp.float32, -s, s), 'bv': jax.random.uniform(ks[6], (HIDDEN,), jnp.float32, -s, s)}
    _L0_attn_in = _L0_attn_setup()

    def _L0_ffn_setup():
        import jax, jax.numpy as jnp
        import numpy as np
        TOP_K = 2
        E = 8
        D = 256
        F = 512
        B, S = (2, 256)
        key = jax.random.key(seed)
        ks = jax.random.split(key, 8)
        sc = 0.02
        return {'x_bsD': jax.random.normal(ks[0], (B, S, D), dtype=jnp.float32), 'router_DE': jax.random.normal(ks[1], (D, E), dtype=jnp.float32) * sc, 'w_in_shared_FD': jax.random.normal(ks[2], (F, D), dtype=jnp.float32) * sc, 'w_out_shared_DF': jax.random.normal(ks[3], (D, F), dtype=jnp.float32) * sc, 'w_swiglu_FD': jax.random.normal(ks[4], (F, D), dtype=jnp.float32) * sc, 'w_in_eDF': jax.random.normal(ks[5], (E, D, F), dtype=jnp.float32) * sc, 'w_swiglu_eDF': jax.random.normal(ks[6], (E, D, F), dtype=jnp.float32) * sc, 'w_out_eFD': jax.random.normal(ks[7], (E, F, D), dtype=jnp.float32) * sc}
    _L0_ffn_in = _L0_ffn_setup()
    _d = {'L0_attn_x': _L0_attn_in['x'], 'L0_attn_Wq': _L0_attn_in['Wq'], 'L0_attn_bq': _L0_attn_in['bq'], 'L0_attn_Wk': _L0_attn_in['Wk'], 'L0_attn_bk': _L0_attn_in['bk'], 'L0_attn_Wv': _L0_attn_in['Wv'], 'L0_attn_bv': _L0_attn_in['bv'], 'L0_ffn_router_DE': _L0_ffn_in['router_DE'], 'L0_ffn_w_in_shared_FD': _L0_ffn_in['w_in_shared_FD'], 'L0_ffn_w_out_shared_DF': _L0_ffn_in['w_out_shared_DF'], 'L0_ffn_w_swiglu_FD': _L0_ffn_in['w_swiglu_FD'], 'L0_ffn_w_in_eDF': _L0_ffn_in['w_in_eDF'], 'L0_ffn_w_swiglu_eDF': _L0_ffn_in['w_swiglu_eDF'], 'L0_ffn_w_out_eFD': _L0_ffn_in['w_out_eFD']}
    _x0 = _d['L0_attn_x']
    _d['L0_attn_x'] = jax.random.normal(jax.random.fold_in(jax.random.key(seed), 1), (16, 512, 256), dtype=_x0.dtype)
    del _x0
    return _d

def reference(L0_attn_x, L0_attn_Wq, L0_attn_bq, L0_attn_Wk, L0_attn_bk, L0_attn_Wv, L0_attn_bv, L0_ffn_router_DE, L0_ffn_w_in_shared_FD, L0_ffn_w_out_shared_DF, L0_ffn_w_swiglu_FD, L0_ffn_w_in_eDF, L0_ffn_w_swiglu_eDF, L0_ffn_w_out_eFD):

    def _L0_attn_ref(x, Wq, bq, Wk, bk, Wv, bv):
        import jax, jax.numpy as jnp
        import numpy as np
        HIDDEN = 256
        HEADS = 16
        batch, len_, hidden = x.shape
        xh = x.reshape(batch, HEADS, len_ // HEADS, hidden)
        q = jnp.einsum('bhcd,ed->bhce', xh, Wq) + bq
        k = jnp.einsum('bhcd,ed->bhce', xh, Wk) + bk
        v = jnp.einsum('bhcd,ed->bhce', xh, Wv) + bv
        score = jax.nn.softmax(jnp.einsum('bhce,bhke->bhck', q, k), axis=-1)
        out = jnp.einsum('bhck,bhke->bhce', score, v)
        return out.reshape(batch, len_, hidden)

    def _L0_ffn_ref(x_bsD, router_DE, w_in_shared_FD, w_out_shared_DF, w_swiglu_FD, w_in_eDF, w_swiglu_eDF, w_out_eFD):
        import jax, jax.numpy as jnp
        import numpy as np
        TOP_K = 2
        E = 8
        D = 256
        F = 512
        B, S = (2, 256)
        b, s, d = x_bsD.shape
        x_aD = x_bsD.reshape(-1, d)
        a = x_aD.shape[0]
        scores_aE = x_aD @ router_DE
        topv_aK, topi_aK = jax.lax.top_k(scores_aE, TOP_K)
        masked_aE = jnp.full_like(scores_aE, -jnp.inf)
        masked_aE = masked_aE.at[jnp.arange(a)[:, None], topi_aK].set(topv_aK)
        gates_Ea = jax.nn.sigmoid(masked_aE.astype(jnp.float32)).astype(x_aD.dtype).T
        routed_in_EaD = x_aD[None, :, :] * gates_Ea[:, :, None]
        routed_in_EaD = jax.lax.stop_gradient(routed_in_EaD)
        mid_EaF = jnp.einsum('ead,edf->eaf', routed_in_EaD, w_in_eDF)
        sw_EaF = jnp.einsum('ead,edf->eaf', routed_in_EaD, w_swiglu_eDF)
        h_EaF = jax.nn.silu(mid_EaF) * sw_EaF
        out_EaD = jnp.einsum('eaf,efd->ead', h_EaF, w_out_eFD)
        shared_aF = jax.nn.silu(x_aD @ w_in_shared_FD.T) * (x_aD @ w_swiglu_FD.T)
        shared_out_aD = jax.lax.stop_gradient(shared_aF @ w_out_shared_DF.T)
        out_aD = shared_out_aD + jnp.sum(out_EaD, axis=0)
        return out_aD.reshape(b, s, d)
    x = L0_attn_x
    x = _layernorm(x + _L0_attn_ref(x, L0_attn_Wq, L0_attn_bq, L0_attn_Wk, L0_attn_bk, L0_attn_Wv, L0_attn_bv), axis=-1)
    x = _layernorm(x + _L0_ffn_ref(x, L0_ffn_router_DE, L0_ffn_w_in_shared_FD, L0_ffn_w_out_shared_DF, L0_ffn_w_swiglu_FD, L0_ffn_w_in_eDF, L0_ffn_w_swiglu_eDF, L0_ffn_w_out_eFD), axis=-1)
    return x

_drawn_inputs = setup_inputs


def setup_inputs(seed=0):
    import zlib

    import numpy as np

    out = dict(_drawn_inputs(seed))
    spreads = {}
    factors = {'L0_attn_bk': 64.0,
     'L0_ffn_router_DE': 5.506,
     'L0_ffn_w_in_eDF': 4.782,
     'L0_ffn_w_swiglu_eDF': 4.761,
     'L0_ffn_w_out_eFD': 4.756,
     'L0_ffn_w_in_shared_FD': 7.612,
     'L0_ffn_w_out_shared_DF': 7.51,
     'L0_ffn_w_swiglu_FD': 7.511}
    for name, (base, spread) in spreads.items():
        noise = np.random.default_rng([zlib.crc32(name.encode()), seed]).standard_normal(out[name].shape)
        drawn = base * np.exp(spread * noise) if base else spread * noise
        out[name] = jnp.asarray(drawn.astype(out[name].dtype))
    for name, factor in factors.items():
        out[name] = (out[name] * factor).astype(out[name].dtype)
    return out
```

```python
from contextlib import ExitStack

import concourse.bass as bass
from concourse import mybir
from concourse.bass import IndirectOffsetOnAxis, ds

ALU = mybir.AluOpType
ACT = mybir.ActivationFunctionType
AX = mybir.AxisListType
F32 = mybir.dt.float32
BF16 = mybir.dt.bfloat16
I32 = mybir.dt.int32
U32 = mybir.dt.uint32

P = 128
D = 256
DC = D // P
F = 512
FC = F // P
E = 8
TOP_K = 2
TOKENS = 16 * 512
BLOCK = 32
NT = 4
GROUP = NT * P
GROUPS = TOKENS // GROUP
TILES = TOP_K * TOKENS // P + E
QBLOCKS = TOKENS // P + 1
QROWS = QBLOCKS * P
ROW = D + E
RING = 4
EPS = 1e-5
OFF_BLOCK = -1e30
BIG = 3e38
RSQRT_MAGIC = 0x5F3759DF
NEWTON = 3


def at_least(eng, sem, n):
    if not isinstance(n, int) or n > 0:
        eng.wait_ge(sem, n)


def build(nc, x, wqT, wkT, wvT, bq, bk, bv, router, w_in_shT, w_sw_shT, w_out_shT, w_in, w_sw, w_out,
          ident, mask, tri, experts, out):
    with ExitStack() as ctx:
        def sb(name, shape, dt=F32):
            return ctx.enter_context(nc.sbuf_tensor(name, shape, dt))

        def sem(name):
            return ctx.enter_context(nc.semaphore(name))

        bank = [ctx.enter_context(nc.psum_tensor(f"bank{i}", [P, 512], F32)) for i in range(8)]

        wi_sb = sb("wi_sb", [P, E * DC, F])
        ws_sb = sb("ws_sb", [P, E * DC, F])
        wo_sb = sb("wo_sb", [P, E * FC, D])
        shi_sb = sb("shi_sb", [P, DC, F])
        shs_sb = sb("shs_sb", [P, DC, F])
        sho_sb = sb("sho_sb", [P, FC, D])
        wq_sb = sb("wq_sb", [P, DC, D])
        wk_sb = sb("wk_sb", [P, DC, D])
        wv_sb = sb("wv_sb", [P, DC, D])
        bq_sb = sb("bq_sb", [P, DC])
        bk_sb = sb("bk_sb", [P, DC])
        bv_sb = sb("bv_sb", [P, D])
        router_sb = sb("router_sb", [P, DC, E])
        ident_sb = sb("ident_sb", [P, P])
        mask_sb = sb("mask_sb", [P, P])
        tri_sb = sb("tri_sb", [P, 2, P])
        trib = sb("trib", [P, 2, P], BF16)
        exp_sb = sb("exp_sb", [P, 2, E])

        x_sb = sb("x_sb", [P, NT, D])
        xb_sb = sb("xb_sb", [P, NT, D])
        xT = sb("xT", [P, DC, GROUP])
        qT = sb("qT", [P, DC, GROUP])
        keys_values = sb("keys_values", [P, 2 * NT * D])
        x1_scores = sb("x1_scores", [P, 2 * NT * D])
        hiddens = sb("hiddens", [P, FC * GROUP])
        kT = keys_values[:, 0:DC * GROUP].rearrange("p (k n) -> p k n", k=DC)
        v_sb = keys_values[:, NT * D:2 * NT * D].rearrange("p (t d) -> p t d", t=NT)
        x1T = x1_scores[:, 0:DC * GROUP].rearrange("p (k n) -> p k n", k=DC)
        s_sb = x1_scores[:, 1024:1536].rearrange("p (t k) -> p t k", t=NT)
        nmax = sb("nmax", [P, NT])
        p_sb = x1_scores[:, 1536:2048].rearrange("p (t k) -> p t k", t=NT)
        rsum = sb("rsum", [P, NT])
        rinv = sb("rinv", [P, NT])
        pT = sb("pT", [P, NT, P])
        y_sb = sb("y_sb", [P, NT, D])
        x1row = [sb(f"x1row{i}", [P, NT, ROW]) for i in range(2)]
        logit = sb("logit", [P, NT, E])
        en = sb("en", [P, NT, E])
        top = sb("top", [P, NT, 8])
        topi = sb("topi", [P, NT, 8], U32)
        topf = sb("topf", [P, TOP_K, NT])
        chosen = sb("chosen", [P, NT, E], BF16)
        count = sb("count", [P, E])
        place = sb("place", [P, NT, E])
        place2 = sb("place2", [P, TOP_K, NT, E])
        slot_i = sb("slot_i", [P, 2, TOP_K, NT], I32)
        sel = sb("sel", [P, GROUPS, TOP_K * NT, E])
        slot_f = sb("slot_f", [P, GROUPS, TOP_K * NT])

        stats = sb("stats", [P, NT, 6])
        mv = sb("mv", [P, NT, 2])
        veps = sb("veps", [P, NT])
        halfi = sb("halfi", [P, NT], I32)
        rs = sb("rs", [P, NT])
        rs_a = sb("rs_a", [P, NT])
        rs_b = sb("rs_b", [P, NT])
        rs_c = sb("rs_c", [P, NT])
        shift = sb("shift", [P, NT])

        cnt_i = sb("cnt_i", [P, E], I32)
        tiles_i = sb("tiles_i", [P, E], I32)
        tiles_f = sb("tiles_f", [P, 2, E + 4])
        pad_f = sb("pad_f", [P, E])
        pad_i = sb("pad_i", [P, E], I32)
        partno = sb("partno", [P, 1])
        zero_row = sb("zero_row", [P, ROW])
        tile_no = sb("tile_no", [P, TILES])
        past = hiddens[:, 0:TILES * (E + 1)].rearrange("p (t e) -> p t e", t=TILES)
        onehot = sb("onehot", [P, TILES, E])
        hop = sb("hop", [P, E])
        walk = x1_scores[:, 0:TILES * E].rearrange("p (t e) -> p t e", t=TILES)
        tile_e = sb("tile_e", [1, TILES])
        tile_b = sb("tile_b", [1, TILES])
        tile_ei = sb("tile_ei", [1, TILES], I32)
        tile_bi = sb("tile_bi", [1, TILES], I32)
        base_d = sb("base_d", [P, E])
        ysel = keys_values[:, 0:GROUPS * TOP_K * NT * E].rearrange("p (j e) -> p j e", e=E)
        yslot = sb("yslot", [P, GROUPS, TOP_K * NT])
        group_slots = [sb(f"group_slots{i}", [P, TOP_K * NT], I32) for i in range(2)]
        yslot_i = sb("yslot_i", [P, GROUPS * TOP_K * NT], I32)

        xs = [sb(f"xs{i}", [P, ROW]) for i in range(RING)]
        xsT = [sb(f"xsT{i}", [P, DC, P]) for i in range(2)]
        gate = [sb(f"gate{i}", [P, 1]) for i in range(2)]
        gate_j = sb("gate_j", [P, E])
        act2 = [hiddens[:, i * F:(i + 1) * F] for i in range(2)]
        h2 = [hiddens[:, (2 + i) * F:(3 + i) * F] for i in range(2)]
        h2T = [sb(f"h2T{i}", [P, FC, P]) for i in range(2)]
        y2 = [sb(f"y2_{i}", [P, D]) for i in range(RING)]

        queues = nc.dram_tensor("queues", [E * QROWS + P, ROW], F32, kind="Internal").ap()
        x1_dram = nc.dram_tensor("x1_dram", [TOKENS, D], F32, kind="Internal").ap()
        y_dram = nc.dram_tensor("y_dram", [TILES * P, D], F32, kind="Internal").ap()

        x_g = x.rearrange("b s d -> (b s) d").rearrange("(g t p) d -> g p t d", g=GROUPS, t=NT)
        x1_g = x1_dram.rearrange("(g t p) d -> g p t d", g=GROUPS, t=NT)
        out_g = out.rearrange("b s d -> (b s) d").rearrange("(g t p) d -> g p t d", g=GROUPS, t=NT)
        wi_g = w_in.rearrange("e (k p) f -> p (e k) f", k=DC)
        ws_g = w_sw.rearrange("e (k p) f -> p (e k) f", k=DC)
        wo_g = w_out.rearrange("e (c p) d -> p (e c) d", c=FC)

        z1 = [rows[:, :, 0:D] for rows in x1row]
        z1T = xT
        act3 = [qT[:, 0, :], qT[:, 1, :]]
        h3T = hiddens[:, :].rearrange("p (c n) -> p c n", c=FC)
        yg = [a[:, :].rearrange("p (j d) -> p j d", d=D) for a in (keys_values, x1_scores)]
        z_sb = y_sb
        o_sb = xb_sb

        const_in = sem("const_in")
        attn_in = sem("attn_in")
        x_in = sem("x_in")
        expert_in = sem("expert_in")
        shared_in = sem("shared_in")
        tri_ok = sem("tri_ok")
        start_ok = sem("start_ok")
        xT_ps = sem("xT_ps")
        xT_act = sem("xT_act")
        xT_dve = sem("xT_dve")
        xb_ok = sem("xb_ok")
        q_ps = sem("q_ps")
        q_ok = sem("q_ok")
        k_ps = sem("k_ps")
        k_ok = sem("k_ok")
        v_ps = sem("v_ps")
        v_ok = sem("v_ok")
        s_ps = sem("s_ps")
        s_ok = sem("s_ok")
        p_ok = sem("p_ok")
        pT_ps = sem("pT_ps")
        pT_ok = sem("pT_ok")
        rinv_ok = sem("rinv_ok")
        pv_ps = sem("pv_ps")
        y_ok = sem("y_ok")
        stats_ok = [sem(f"stats_ok{i}") for i in range(2)]
        mv_ok = [sem(f"mv_ok{i}") for i in range(2)]
        veps_ok = [sem(f"veps_ok{i}") for i in range(2)]
        half_ok = [sem(f"half_ok{i}") for i in range(2)]
        rs_ok = [[sem(f"rs_ok{j}_{i}") for i in range(NEWTON + 1)] for j in range(2)]
        rsa_ok = [[sem(f"rsa_ok{j}_{i}") for i in range(NEWTON)] for j in range(2)]
        rsb_ok = [[sem(f"rsb_ok{j}_{i}") for i in range(NEWTON)] for j in range(2)]
        shift_ok = [sem(f"shift_ok{i}") for i in range(2)]
        x1_ok = sem("x1_ok")
        x1T_ps = sem("x1T_ps")
        x1T_act = sem("x1T_act")
        x1T_dve = sem("x1T_dve")
        logit_ps = sem("logit_ps")
        logit_ok = sem("logit_ok")
        en_ok = sem("en_ok")
        en1_ok = sem("en1_ok")
        gates_ok = sem("gates_ok")
        top_ok = sem("top_ok")
        topi_ok = sem("topi_ok")
        topf_ok = sem("topf_ok")
        sel_ok = sem("sel_ok")
        chosen_ok = sem("chosen_ok")
        rank_ps = sem("rank_ps")
        place_ok = sem("place_ok")
        count_ok = sem("count_ok")
        place2_ok = sem("place2_ok")
        slotf_ok = sem("slotf_ok")
        slot_ok = sem("slot_ok")
        scattered = [sem(f"scattered{i}") for i in range(2)]
        x1_stored = [sem(f"x1_stored{i}") for i in range(2)]
        t_iota = sem("t_iota")
        t_step = sem("t_step")
        t_pad = sem("t_pad")
        padded = sem("padded")
        idle_padded = sem("idle_padded")
        tables_ok = sem("tables_ok")
        yslot_ok = sem("yslot_ok")
        xs_in = [sem(f"xs_in{i}") for i in range(RING)]
        xsT_ps = sem("xsT_ps")
        xsT_ok = sem("xsT_ok")
        gatej_ok = sem("gatej_ok")
        gate_ok = sem("gate_ok")
        mid_ps = sem("mid_ps")
        act_ok = sem("act_ok")
        sw_ps = sem("sw_ps")
        h_ok = sem("h_ok")
        hT_ps = sem("hT_ps")
        hT_ok = sem("hT_ok")
        y_ps = sem("y_ps")
        y2_ok = sem("y2_ok")
        y_stored = [sem(f"y_stored{i}") for i in range(RING)]
        z1_in = [sem(f"z1_in{i}") for i in range(2)]
        z1T_ps = sem("z1T_ps")
        z1T_act = sem("z1T_act")
        z1T_dve = sem("z1T_dve")
        mid3_ps = sem("mid3_ps")
        sw3_ps = sem("sw3_ps")
        act3_ok = sem("act3_ok")
        h3_ok = sem("h3_ok")
        o_ps = sem("o_ps")
        gathered = [sem(f"gathered{i}") for i in range(2)]
        slots_here = sem("slots_here")
        za_ok = sem("za_ok")
        zb_ok = sem("zb_ok")
        zc_ok = sem("zc_ok")
        o_ok = sem("o_ok")
        o_stored = sem("o_stored")

        block = ctx.enter_context(nc.Block())

        def wait_apart(eng, sem_, n):
            n = n if isinstance(n, int) else eng.snap(n)
            eng.wait_ge(const_in, 16)
            at_least(eng, sem_, n)

        def groups(eng, body, ahead):
            for g in range(ahead):
                body(g, g % 2)
            pairs = (GROUPS - ahead) // 2
            with eng.Fori(0, pairs) as i:
                for u in range(2):
                    body(i * 2 + (ahead + u), (ahead + u) % 2)
            for g in range(ahead + 2 * pairs, GROUPS):
                body(g, g % 2)

        @block.sync
        def _(sp):
            sp.dma_start(ident_sb[:, :], ident).then_inc(const_in, 16)
            sp.dma_start(x_sb[:, :, :], x_g[0]).then_inc(x_in, 16)
            for dst, src in ((wq_sb, wqT), (wk_sb, wkT), (wv_sb, wvT)):
                sp.dma_start(dst[:, :, :], src.rearrange("(k p) e -> p k e", p=P)).then_inc(attn_in, 16)
            sp.dma_start(bq_sb[:, :], bq).then_inc(const_in, 16)
            sp.dma_start(bk_sb[:, :], bk).then_inc(const_in, 16)
            sp.dma_start(bv_sb[:, :], bv).then_inc(const_in, 16)
            sp.dma_start(router_sb[:, :, :], router.rearrange("(k p) e -> p k e", p=P)).then_inc(const_in, 16)
            sp.dma_start(mask_sb[:, :], mask).then_inc(const_in, 16)
            sp.dma_start(tri_sb[:, :, :], tri).then_inc(const_in, 16)
            sp.dma_start(exp_sb[:, :, :], experts).then_inc(const_in, 16)
            sp.dma_start(shi_sb[:, :, :], w_in_shT.rearrange("(k p) f -> p k f", p=P)).then_inc(shared_in, 16)
            sp.dma_start(shs_sb[:, :, :], w_sw_shT.rearrange("(k p) f -> p k f", p=P)).then_inc(shared_in, 16)
            sp.dma_start(sho_sb[:, :, :], w_out_shT.rearrange("(c p) d -> p c d", p=P)).then_inc(shared_in, 16)

            def phase1(g, par):
                if not (isinstance(g, int) and g == 0):
                    at_least(sp, xT_ps, g)
                    at_least(sp, xb_ok, g)
                    sp.dma_start(x_sb[:, :, :], x_g[ds(g, 1)].rearrange("a p t d -> p (a t) d") if not isinstance(g, int) else x_g[g]).then_inc(x_in, 16)
                for dst, src, n in ((wi_sb, wi_g, 1), (ws_sb, ws_g, 1), (wo_sb, wo_g, 2)):
                    sp.dma_start(dst[:, ds(g * n, n), :], src[:, ds(g * n, n), :]).then_inc(expert_in, 16)
                if not (isinstance(g, int) and g == 0):
                    store_x1(g - 1, 1 - par)

            def store_x1(g, par):
                sp.wait_ge(x1_ok, g + 1)
                dst = x1_g[g] if isinstance(g, int) else x1_g[ds(g, 1)].rearrange("a p t d -> p (a t) d")
                sp.dma_start(dst, x1row[par][:, :, 0:D]).then_inc(x1_stored[par], 16)

            groups(sp, phase1, 2)
            store_x1(GROUPS - 1, (GROUPS - 1) % 2)

            sp.wait_ge(t_iota, 3)
            sp.dma_start(queues[E * QROWS:E * QROWS + P, :], zero_row[:, :]).then_inc(idle_padded, 16)
            for s in range(2):
                sp.wait_ge(scattered[s], 16 * TOP_K * NT * GROUPS // 2)
            sp.wait_ge(padded, 16 * E)
            sp.wait_ge(idle_padded, 16)
            sp.wait_ge(tables_ok, 1)

            def load_xs(t, r):
                if not (isinstance(t, int) and t < RING):
                    sp.wait_ge(xsT_ps, t - RING + 1)
                    sp.wait_ge(gate_ok, t - RING + 1)
                b = sp.value_load(tile_bi[0:1, ds(t, 1)], min_val=0, max_val=E * QBLOCKS)
                sp.dma_start(xs[r][:, :], queues[ds(b * P, P), :]).then_inc(xs_in[r], 16)

            def store_y(t, r):
                sp.wait_ge(y2_ok, t + 1)
                sp.dma_start(y_dram[ds(t * P, P), :], y2[r][:, :]).then_inc(y_stored[r], 16)

            for t in range(RING - 1):
                load_xs(t, t)
            load_xs(RING - 1, RING - 1)
            with sp.Fori(0, TILES // RING - 1) as i:
                for r in range(RING):
                    load_xs(i * RING + (r + RING), r)
                    store_y(i * RING + r, r)
            for r in range(RING):
                store_y(TILES - RING + r, r)

            def z_load(g, par):
                if not isinstance(g, int) or g >= 2:
                    sp.wait_ge(z1T_ps, g - 1)
                    sp.wait_ge(za_ok, g - 1)
                src = x1_g[g] if isinstance(g, int) else x1_g[ds(g, 1)].rearrange("a p t d -> p (a t) d")
                sp.dma_start(z1[par], src).then_inc(z1_in[par], 16)

            def z_store(g):
                sp.wait_ge(o_ok, g + 1)
                dst = out_g[g] if isinstance(g, int) else out_g[ds(g, 1)].rearrange("a p t d -> p (a t) d")
                sp.dma_start(dst, o_sb[:, :, :]).then_inc(o_stored, 16)

            def phase3(g, par):
                z_load(g, par)
                if not isinstance(g, int) or g >= 2:
                    z_store(g - 2)

            for s in range(2):
                sp.wait_ge(x1_stored[s], 16 * GROUPS // 2)
            groups(sp, phase3, 2)
            z_store(GROUPS - 2)
            z_store(GROUPS - 1)
            sp.wait_ge(o_stored, 16 * GROUPS)

        @block.gpsimd
        def _(pool):
            pool.memset(zero_row[:, :], 0.0).then_inc(t_iota, 1)
            pool.iota(tile_no[:, :], pattern=[[1, TILES]], base=0, channel_multiplier=0,
                      allow_small_or_imprecise_dtypes=True).then_inc(t_iota, 1)
            pool.iota(partno[:, :], pattern=[[0, 1]], base=0, channel_multiplier=1,
                      allow_small_or_imprecise_dtypes=True).then_inc(t_iota, 1)
            pool.wait_ge(const_in, 16 * 8)

            def add_bv(g):
                pool.wait_ge(x_in, g * 16 + 16)
                at_least(pool, y_ok, g)
                pool.tensor_tensor(xb_sb[:, :, :], x_sb[:, :, :],
                                   bv_sb[:, :].unsqueeze(1).to_broadcast([P, NT, D]), ALU.add).then_inc(xb_ok, 1)

            def scatter(g, par):
                wait_apart(pool, gates_ok, g + 2)
                for k in range(TOP_K):
                    for t in range(NT):
                        pool.indirect_dma_start(
                            out=queues, out_offset=IndirectOffsetOnAxis(ap=slot_i[:, par, k, t:t + 1], axis=0),
                            in_=x1row[par][:, t, :], in_offset=None).then_inc(scattered[par], 16)

            def phase1(g, par):
                add_bv(g)
                if not (isinstance(g, int) and g < 2):
                    scatter(g - 2, par)

            groups(pool, phase1, 2)
            scatter(GROUPS - 2, 0)
            scatter(GROUPS - 1, 1)

            pool.wait_ge(t_pad, 1)
            for e in range(E):
                pool.indirect_dma_start(
                    out=queues, out_offset=IndirectOffsetOnAxis(ap=pad_i[:, e:e + 1], axis=0),
                    in_=zero_row[:, :], in_offset=None).then_inc(padded, 16)

            pool.wait_ge(yslot_ok, 1)
            for r in range(RING):
                pool.wait_ge(y_stored[r], 16 * TILES // RING)

            def gather(g, par):
                pool.wait_ge(zc_ok, g + 1)
                pool.tensor_copy(group_slots[par][:, :], yslot_i[:, ds(g * (TOP_K * NT), TOP_K * NT)]).then_inc(slots_here, 1)
                wait_apart(pool, slots_here, g + 1)
                for j in range(TOP_K * NT):
                    ix = group_slots[par][:, j:j + 1]
                    pool.indirect_dma_start(
                        out=yg[par][:, j, :], out_offset=None, in_=y_dram,
                        in_offset=IndirectOffsetOnAxis(ap=ix, axis=0)).then_inc(gathered[par], 16)

            groups(pool, gather, 2)

        @block.tensor
        def _(pe):
            def group_transposes(rows, banks, g, done):
                for k in range(DC):
                    for t in range(NT):
                        mm = pe.transpose(banks[k][:, t * P:(t + 1) * P], rows[:, t, k * P:(k + 1) * P], ident_sb[:, :])
                mm.then_inc(done, 1)

            def project(w, dst, c, sig):
                for k in range(DC):
                    mm = pe.matmul(dst[:, :], w[:, k, c * P:(c + 1) * P], xT[:, k, :], start=(k == 0), stop=(k == DC - 1))
                mm.then_inc(sig, 1)

            def probs_T(g):
                pe.wait_ge(p_ok, g + 1)
                for t in range(NT):
                    mm = pe.transpose(bank[2][:, t * P:(t + 1) * P], p_sb[:, t, :], ident_sb[:, :])
                mm.then_inc(pT_ps, 1)

            def probs_v(g):
                pe.wait_ge(pT_ok, g + 1)
                pe.wait_ge(v_ok, g + 1)
                at_least(pe, x1T_act, g)
                at_least(pe, x1T_dve, g)
                for t in range(NT):
                    mm = pe.matmul(bank[5 + t // 2][:, (t % 2) * D:(t % 2 + 1) * D], pT[:, t, :], v_sb[:, t, :],
                                   start=True, stop=True)
                mm.then_inc(pv_ps, 1)

            def x1_T(g, par):
                pe.wait_ge(x1_ok, g + 1)
                group_transposes(x1row[par], (bank[5], bank[6]), g, x1T_ps)

            def logits(g):
                pe.wait_ge(x1T_act, g + 1)
                pe.wait_ge(x1T_dve, g + 1)
                at_least(pe, count_ok, g)
                at_least(pe, place_ok, g)
                for t in range(NT):
                    for k in range(DC):
                        mm = pe.matmul(bank[7][:, t * E:(t + 1) * E], x1T[:, k, t * P:(t + 1) * P], router_sb[:, k, :],
                                       start=(k == 0), stop=(k == DC - 1))
                mm.then_inc(logit_ps, 1)

            def ranks(g):
                pe.wait_ge(chosen_ok, g + 1)
                ch = chosen[:, :, :].rearrange("p t e -> p (t e)")
                rk = bank[7][:, 64:64 + NT * E]
                pe.matmul(rk, trib[:, 0, :], ch, start=True, stop=False, skip_group_check=True)
                for s in range(1, NT):
                    pe.matmul(bank[7][:, 64 + s * E:64 + NT * E], trib[:, 1, :], ch[:, 0:(NT - s) * E],
                              start=False, stop=(s == NT - 1), skip_group_check=True)
                for t in range(NT):
                    mm = pe.matmul(bank[7][:, 128:128 + E], trib[:, 1, :], ch[:, t * E:(t + 1) * E],
                                   start=(t == 0), stop=(t == NT - 1), skip_group_check=True)
                mm.then_inc(rank_ps, 1)

            def stage_a(g, par, prev):
                pe.wait_ge(x_in, g * 16 + 16)
                at_least(pe, k_ok, g)
                group_transposes(x_sb, (bank[0], bank[1]), g, xT_ps)
                at_least(pe, v_ok, g)
                pe.wait_ge(xT_act, g + 1)
                pe.wait_ge(xT_dve, g + 1)
                project(wq_sb, bank[3], 0, q_ps)
                if prev:
                    probs_T(g - 1)
                project(wq_sb, bank[4], 1, q_ps)
                if prev == 2:
                    ranks(g - 2)
                if prev:
                    probs_v(g - 1)
                project(wk_sb, bank[0], 0, k_ps)
                project(wk_sb, bank[1], 1, k_ps)
                pe.wait_ge(q_ok, g + 1)
                for t in range(NT):
                    for k in range(DC):
                        mm = pe.matmul(bank[3 + t // 2][:, (t % 2) * D:(t % 2 + 1) * D], xT[:, k, t * P:(t + 1) * P],
                                       wv_sb[:, k, :], start=(k == 0), stop=(k == DC - 1))
                mm.then_inc(v_ps, 1)
                if prev:
                    x1_T(g - 1, 1 - par)
                pe.wait_ge(k_ok, g + 1)
                at_least(pe, pT_ok, g)
                for t in range(NT):
                    for k in range(DC):
                        c = slice(t * P, (t + 1) * P)
                        mm = pe.matmul(bank[2][:, c], qT[:, k, c], kT[:, k, c], start=(k == 0), stop=(k == DC - 1))
                mm.then_inc(s_ps, 1)
                if prev:
                    logits(g - 1)

            pe.wait_ge(const_in, 16 * 8)
            pe.wait_ge(attn_in, 16 * 3)
            pe.wait_ge(tri_ok, 1)
            stage_a(0, 0, 0)
            stage_a(1, 1, 1)
            pairs = (GROUPS - 2) // 2
            with pe.Fori(0, pairs) as i:
                for u in range(2):
                    stage_a(i * 2 + (2 + u), u, 2)
            last = GROUPS - 1
            probs_T(last)
            ranks(last - 1)
            probs_v(last)
            x1_T(last, last % 2)
            logits(last)
            ranks(last)

            pe.wait_ge(count_ok, GROUPS)
            pe.wait_ge(place_ok, GROUPS)
            pe.wait_ge(expert_in, 16 * 3 * GROUPS)
            pe.wait_ge(tables_ok, 1)

            def xs_T(t, r):
                pe.wait_ge(xs_in[r], 16 * (t // RING + 1) if isinstance(t, int) else (t - r) * (16 // RING) + 16)
                at_least(pe, xsT_ok, t)
                for k in range(DC):
                    mm = pe.transpose(bank[0][:, k * P:(k + 1) * P], xs[r][:, k * P:(k + 1) * P], ident_sb[:, :])
                mm.then_inc(xsT_ps, 1)

            def hidden(t, r, w, dst, e, sig, free):
                at_least(pe, free, t)
                for k in range(DC):
                    mm = pe.matmul(dst[:, :], xsT[r % 2][:, k, :], w[:, ds(e * DC + k, 1), :].rearrange("p a f -> p (a f)"),
                                   start=(k == 0), stop=(k == DC - 1))
                mm.then_inc(sig, 1)

            def h_T(t, r):
                pe.wait_ge(h_ok, t + 1)
                at_least(pe, hT_ok, t)
                for c in range(FC):
                    mm = pe.transpose(bank[3][:, c * P:(c + 1) * P], h2[r % 2][:, c * P:(c + 1) * P], ident_sb[:, :])
                mm.then_inc(hT_ps, 1)

            def tile_out(t, r, e):
                pe.wait_ge(hT_ok, t + 1)
                if not isinstance(t, int) or t >= 2:
                    pe.wait_ge(y2_ok, t - 1)
                for c in range(FC):
                    mm = pe.matmul(bank[4 + r % 2][:, 0:D], h2T[r % 2][:, c, :],
                                   wo_sb[:, ds(e * FC + c, 1), :].rearrange("p a f -> p (a f)"),
                                   start=(c == 0), stop=(c == FC - 1))
                mm.then_inc(y_ps, 1)

            def expert_of(t):
                return pe.value_load(tile_ei[0:1, ds(t, 1)], min_val=0, max_val=E - 1)

            def tile(t, r, prev, ahead):
                if ahead:
                    xs_T(t + 1, (r + 1) % RING)
                e = expert_of(t)
                pe.wait_ge(xsT_ok, t + 1)
                hidden(t, r, wi_sb, bank[1], e, mid_ps, act_ok)
                if prev:
                    h_T(t - 1, r - 1)
                hidden(t, r, ws_sb, bank[2], e, sw_ps, h_ok)
                if prev:
                    tile_out(t - 1, (r - 1) % RING, expert_of(t - 1))

            xs_T(0, 0)
            for t in range(RING):
                tile(t, t, t > 0, True)
            with pe.Fori(1, TILES // RING - 1) as i:
                for r in range(RING):
                    tile(i * RING + r, r, True, True)
            for r in range(RING):
                tile(TILES - RING + r, r, True, r < RING - 1)
            h_T(TILES - 1, RING - 1)
            tile_out(TILES - 1, RING - 1, expert_of(TILES - 1))

            pe.wait_ge(y2_ok, TILES)
            pe.wait_ge(shared_in, 16 * 3)

            def z1_T(g, par):
                pe.wait_ge(z1_in[par], (g - par) * 8 + 16)
                at_least(pe, z1T_act, g)
                at_least(pe, z1T_dve, g)
                group_transposes(z1[par], (bank[0], bank[1]), g, z1T_ps)

            def shared_out(g):
                pe.wait_ge(h3_ok, g * FC + FC)
                at_least(pe, za_ok, g)
                for t in range(NT):
                    for c in range(FC):
                        mm = pe.matmul(bank[6 + t // 2][:, (t % 2) * D:(t % 2 + 1) * D], h3T[:, c, t * P:(t + 1) * P],
                                       sho_sb[:, c, :], start=(c == 0), stop=(c == FC - 1))
                mm.then_inc(o_ps, 1)

            def shared_hidden(g):
                pe.wait_ge(z1T_act, g + 1)
                pe.wait_ge(z1T_dve, g + 1)
                for c in range(FC):
                    for w, b, sig, free in ((shi_sb, 2, mid3_ps, act3_ok), (shs_sb, 4, sw3_ps, h3_ok)):
                        if not isinstance(g, int) or g * FC + c >= 2:
                            pe.wait_ge(free, g * FC + (c - 1))
                        for k in range(DC):
                            mm = pe.matmul(bank[b + c % 2][:, :], w[:, k, c * P:(c + 1) * P], z1T[:, k, :],
                                           start=(k == 0), stop=(k == DC - 1))
                        mm.then_inc(sig, 1)

            def phase3(g, par):
                z1_T(g, par)
                if not (isinstance(g, int) and g == 0):
                    shared_out(g - 1)
                shared_hidden(g)

            groups(pe, phase3, 2)
            shared_out(GROUPS - 1)

        @block.scalar
        def _(act):
            act.wait_ge(const_in, 16 * 8)

            def probs(g):
                act.wait_ge(s_ok, g + 1)
                at_least(act, pT_ps, g)
                at_least(act, rinv_ok, g)
                for t in range(NT):
                    a = act.activation(p_sb[:, t, :], s_sb[:, t, :], ACT.Exp, bias=nmax[:, t:t + 1], scale=-1.0,
                                       accum_out=rsum[:, t:t + 1])
                a.then_inc(p_ok, 1)

            def probs_T(g):
                act.wait_ge(pT_ps, g + 1)
                at_least(act, pv_ps, g)
                act.activation(pT[:, :, :].rearrange("p t k -> p (t k)"), bank[2][:, :], ACT.Copy).then_inc(pT_ok, 1)

            def x1_T(g):
                act.wait_ge(x1T_ps, g + 1)
                at_least(act, logit_ps, g)
                act.activation(x1T[:, 0, :], bank[5][:, :], ACT.Copy).then_inc(x1T_act, 1)

            def gate_exp(g):
                act.wait_ge(logit_ok, g + 1)
                at_least(act, en1_ok, g)
                act.activation(en[:, :, :], logit[:, :, :], ACT.Exp, scale=-1.0).then_inc(en_ok, 1)

            def stage_a(g, par, prev):
                act.wait_ge(xT_ps, g + 1)
                at_least(act, v_ps, g)
                act.activation(xT[:, 0, :], bank[0][:, :], ACT.Copy).then_inc(xT_act, 1)
                if prev:
                    gate_exp(g - 1) if prev == 3 else None
                act.wait_ge(q_ps, g * 2 + 1)
                at_least(act, s_ps, g)
                act.activation(qT[:, 0, :], bank[3][:, :], ACT.Identity, bias=bq_sb[:, 0:1])
                if prev:
                    probs_T(g - 1)
                act.wait_ge(q_ps, g * 2 + 2)
                act.activation(qT[:, 1, :], bank[4][:, :], ACT.Identity, bias=bq_sb[:, 1:2]).then_inc(q_ok, 1)
                if prev == 2:
                    gate_exp(g - 2)
                for c in range(DC):
                    act.wait_ge(k_ps, g * 2 + (c + 1))
                    a = act.activation(kT[:, c, :], bank[c][:, :], ACT.Identity, bias=bk_sb[:, c:c + 1])
                a.then_inc(k_ok, 1)
                act.wait_ge(v_ps, g + 1)
                at_least(act, pv_ps, g)
                for c in range(2):
                    a = act.activation(v_sb[:, 2 * c:2 * c + 2, :].rearrange("p t e -> p (t e)"), bank[3 + c][:, :], ACT.Copy)
                a.then_inc(v_ok, 1)
                if prev:
                    x1_T(g - 1)
                probs(g)

            stage_a(0, 0, 0)
            stage_a(1, 1, 1)
            with act.Fori(0, (GROUPS - 2) // 2) as i:
                for u in range(2):
                    stage_a(i * 2 + (2 + u), u, 2)
            last = GROUPS - 1
            probs_T(last)
            gate_exp(last - 1)
            x1_T(last)
            gate_exp(last)

            def tile(t, r, prev):
                act.wait_ge(mid_ps, t + 1)
                act.wait_ge(gate_ok, t + 1)
                if not isinstance(t, int) or t >= 2:
                    act.wait_ge(h_ok, t - 1)
                act.activation(act2[r % 2][:, :], bank[1][:, :], ACT.Silu, scale=gate[r % 2][:, 0:1]).then_inc(act_ok, 1)
                if prev:
                    t1, r1 = t - 1, (r - 1) % RING
                    act.wait_ge(hT_ps, t1 + 1)
                    if not isinstance(t, int) or t1 >= 2:
                        act.wait_ge(y_ps, t1 - 1)
                    act.activation(h2T[r1 % 2][:, :, :].rearrange("p c k -> p (c k)"), bank[3][:, :], ACT.Copy).then_inc(hT_ok, 1)
                    copy_out(t1, r1)

            def copy_out(t, r):
                act.wait_ge(y_ps, t + 1)
                if not isinstance(t, int) or t >= RING:
                    act.wait_ge(y_stored[r], (t - r) * (16 // RING) if not isinstance(t, int) else 16 * (t // RING))
                act.activation(y2[r][:, :], bank[4 + r % 2][:, 0:D], ACT.Copy).then_inc(y2_ok, 1)

            for t in range(RING):
                tile(t, t, t > 0)
            with act.Fori(1, TILES // RING) as i:
                for r in range(RING):
                    tile(i * RING + r, r, True)
            act.wait_ge(hT_ps, TILES)
            act.wait_ge(y_ps, TILES - 2)
            act.activation(h2T[1][:, :, :].rearrange("p c k -> p (c k)"), bank[3][:, :], ACT.Copy).then_inc(hT_ok, 1)
            copy_out(TILES - 1, RING - 1)

            def shared_act(g):
                act.wait_ge(z1T_ps, g + 1)
                at_least(act, sw3_ps, g * FC)
                act.activation(z1T[:, 0, :], bank[0][:, :], ACT.Copy).then_inc(z1T_act, 1)
                for c in range(FC):
                    act.wait_ge(mid3_ps, g * FC + (c + 1))
                    at_least(act, h3_ok, g * FC + (c - 1))
                    act.activation(act3[c % 2], bank[2 + c % 2][:, :], ACT.Silu).then_inc(act3_ok, 1)

            shared_act(0)
            with act.Fori(1, GROUPS) as g:
                shared_act(g)

        @block.vector
        def _(dve):
            dve.wait_ge(const_in, 16 * 8)
            dve.tensor_copy(trib[:, :, :], tri_sb[:, :, :]).then_inc(tri_ok, 1)
            dve.sem_inc(zc_ok, 2)
            dve.sem_inc(gates_ok, 1)

            def layer_norm(which, n, src, dst, read_ok, done):
                for t in range(NT):
                    i = dve.bn_stats(stats[:, t, :], src[:, t, :])
                i.then_inc(stats_ok[which], 1)
                wait_apart(dve, stats_ok[which], n)
                for t in range(NT):
                    i = dve.bn_aggr(mv[:, t, :], stats[:, t, :])
                i.then_inc(mv_ok[which], 1)
                dve.wait_ge(mv_ok[which], n)
                dve.tensor_scalar(veps[:, :], mv[:, :, 1], EPS, None, ALU.add).then_inc(veps_ok[which], 1)
                dve.wait_ge(veps_ok[which], n)
                dve.tensor_scalar(halfi[:, :], veps[:, :].bitcast(I32), 1, None, ALU.logical_shift_right).then_inc(half_ok[which], 1)
                dve.wait_ge(half_ok[which], n)
                dve.tensor_scalar(rs[:, :].bitcast(I32), halfi[:, :], -1.0, float(RSQRT_MAGIC), ALU.mult, ALU.add)\
                   .then_inc(rs_ok[which][0], 1)
                for s in range(NEWTON):
                    dve.wait_ge(rs_ok[which][s], n)
                    dve.tensor_tensor(rs_a[:, :], rs[:, :], rs[:, :], ALU.mult).then_inc(rsa_ok[which][s], 1)
                    dve.wait_ge(rsa_ok[which][s], n)
                    dve.scalar_tensor_tensor(out=rs_b[:, :], in0=rs_a[:, :], scalar=-0.5, in1=veps[:, :],
                                             op0=ALU.mult, op1=ALU.mult).then_inc(rsb_ok[which][s], 1)
                    dve.wait_ge(rsb_ok[which][s], n)
                    dve.scalar_tensor_tensor(out=rs[:, :], in0=rs_b[:, :], scalar=1.5, in1=rs[:, :],
                                             op0=ALU.add, op1=ALU.mult).then_inc(rs_ok[which][s + 1], 1)
                dve.wait_ge(rs_ok[which][NEWTON], n)
                dve.scalar_tensor_tensor(out=shift[:, :], in0=mv[:, :, 0], scalar=-1.0, in1=rs[:, :],
                                         op0=ALU.mult, op1=ALU.mult).then_inc(shift_ok[which], 1)
                dve.wait_ge(shift_ok[which], n)
                read_ok()
                for t in range(NT):
                    i = dve.tensor_scalar(dst[:, t, 0:D], src[:, t, :], rs[:, t:t + 1], shift[:, t:t + 1],
                                          ALU.mult, ALU.add)
                i.then_inc(done, 1)

            def attn_sum(g, par):
                dve.wait_ge(p_ok, g + 1)
                dve.reciprocal(rinv[:, :], rsum[:, :]).then_inc(rinv_ok, 1)
                dve.wait_ge(rinv_ok, g + 1)
                dve.wait_ge(xb_ok, g + 1)
                dve.wait_ge(pv_ps, g + 1)
                at_least(dve, x1_ok, g)
                for t in range(NT):
                    i = dve.scalar_tensor_tensor(out=y_sb[:, t, :], in0=bank[5 + t // 2][:, (t % 2) * D:(t % 2 + 1) * D],
                                                 scalar=rinv[:, t:t + 1], in1=xb_sb[:, t, :], op0=ALU.mult, op1=ALU.add)
                i.then_inc(y_ok, 1)
                dve.wait_ge(y_ok, g + 1)

                def row_free():
                    if not isinstance(g, int) or g >= 2:
                        dve.wait_ge(scattered[par], (g - par) * (8 * TOP_K * NT))
                        dve.wait_ge(x1_stored[par], (g - par) * 8)

                layer_norm(0, g + 1, y_sb, x1row[par], row_free, x1_ok)

            def x1_T(g):
                dve.wait_ge(x1T_ps, g + 1)
                at_least(dve, logit_ps, g)
                dve.tensor_copy(x1T[:, 1, :], bank[6][:, :]).then_inc(x1T_dve, 1)

            def choose(g, par):
                dve.wait_ge(logit_ps, g + 1)
                at_least(dve, en_ok, g)
                dve.tensor_copy(logit[:, :, :].rearrange("p t e -> p (t e)"), bank[7][:, 0:NT * E]).then_inc(logit_ok, 1)
                wait_apart(dve, logit_ok, g + 1)
                for t in range(NT):
                    i = dve.max(top[:, t, :], logit[:, t, :])
                i.then_inc(top_ok, 1)
                wait_apart(dve, top_ok, g + 1)
                for t in range(NT):
                    i = dve.max_index(topi[:, t, :], top[:, t, :], logit[:, t, :])
                i.then_inc(topi_ok, 1)
                dve.wait_ge(topi_ok, g + 1)
                dve.tensor_copy(topf[:, :, :], topi[:, :, 0:TOP_K].rearrange("p t k -> p k t")).then_inc(topf_ok, 1)
                dve.wait_ge(topf_ok, g + 1)
                sel_g = sel[:, ds(g, 1), :, :].rearrange("p a j e -> p (a j) e")
                dve.tensor_tensor(sel_g,
                                  exp_sb[:, 0, :].unsqueeze(1).to_broadcast([P, TOP_K * NT, E]),
                                  topf[:, :, :].rearrange("p k t -> p (k t)").unsqueeze(2).to_broadcast([P, TOP_K * NT, E]),
                                  ALU.is_equal).then_inc(sel_ok, 1)
                dve.wait_ge(sel_ok, g + 1)
                at_least(dve, rank_ps, g)
                dve.tensor_tensor(chosen[:, :, :], sel_g[:, 0:NT, :], sel_g[:, NT:2 * NT, :], ALU.add).then_inc(chosen_ok, 1)

            def gates(g, par):
                dve.wait_ge(en_ok, g + 1)
                dve.tensor_scalar(en[:, :, :], en[:, :, :], 1.0, None, ALU.add).then_inc(en1_ok, 1)
                dve.wait_ge(en1_ok, g + 1)
                dve.reciprocal(x1row[par][:, :, D:ROW], en[:, :, :]).then_inc(gates_ok, 1)

            def place_rows(g, par):
                dve.wait_ge(rank_ps, g + 1)
                at_least(dve, place2_ok, g)
                dve.tensor_tensor(place[:, :, :], bank[7][:, 64:64 + NT * E].rearrange("p (t e) -> p t e", t=NT),
                                  count[:, :].unsqueeze(1).to_broadcast([P, NT, E]), ALU.add).then_inc(place_ok, 1)
                dve.wait_ge(place_ok, g + 1)
                dve.tensor_tensor(count[:, :], bank[7][:, 128:128 + E], count[:, :], ALU.add).then_inc(count_ok, 1)
                sel_g = sel[:, ds(g, 1), :, :].rearrange("p a j e -> p (a j) e")
                for k in range(TOP_K):
                    i = dve.tensor_tensor(place2[:, k, :, :], sel_g[:, k * NT:(k + 1) * NT, :], place[:, :, :], ALU.mult)
                i.then_inc(place2_ok, 1)
                dve.wait_ge(place2_ok, g + 1)
                slot_g = slot_f[:, ds(g, 1), :].rearrange("p a j -> p (a j)")
                dve.tensor_reduce(slot_g, place2[:, :, :, :].rearrange("p k t e -> p (k t) e"), AX.X, ALU.add)\
                   .then_inc(slotf_ok, 1)
                dve.wait_ge(slotf_ok, g + 1)
                dve.tensor_scalar(slot_i[:, par, :, :].rearrange("p k t -> p (k t)"), slot_g, 0.0, None,
                                  ALU.add).then_inc(slot_ok, 1)
                dve.wait_ge(count_ok, g + 1)

            def stage_a(g, par, prev):
                dve.wait_ge(xT_ps, g + 1)
                at_least(dve, v_ps, g)
                dve.tensor_copy(xT[:, 1, :], bank[1][:, :]).then_inc(xT_dve, 1)
                if prev == 2:
                    place_rows(g - 2, par)
                    gates(g - 2, par)
                if prev:
                    attn_sum(g - 1, 1 - par)
                    x1_T(g - 1)
                wait_apart(dve, s_ps, g + 1)
                at_least(dve, p_ok, g)
                for t in range(NT):
                    i = dve.tensor_tensor_reduce(s_sb[:, t, :], bank[2][:, t * P:(t + 1) * P], mask_sb[:, :], -1.0, BIG,
                                                 ALU.add, ALU.min, nmax[:, t:t + 1])
                i.then_inc(s_ok, 1)
                if prev:
                    choose(g - 1, 1 - par)

            dve.tensor_copy(count[:, :], exp_sb[:, 1, :]).then_inc(start_ok, 1)
            dve.wait_ge(start_ok, 1)
            stage_a(0, 0, 0)
            stage_a(1, 1, 1)
            with dve.Fori(0, (GROUPS - 2) // 2) as i:
                for u in range(2):
                    stage_a(i * 2 + (2 + u), u, 2)
            last = GROUPS - 1
            place_rows(last - 1, 0)
            gates(last - 1, 0)
            attn_sum(last, 1)
            x1_T(last)
            choose(last, 1)
            place_rows(last, 1)
            gates(last, 1)

            steps = [0]

            def step(i):
                steps[0] += 1
                i.then_inc(t_step, 1)
                dve.wait_ge(t_step, steps[0])

            dve.wait_ge(t_iota, 3)
            step(dve.tensor_scalar(pad_f[:, :], count[:, :], partno[:, 0:1], None, ALU.add))
            dve.tensor_copy(pad_i[:, :], pad_f[:, :]).then_inc(t_pad, 1)
            step(dve.tensor_tensor(tiles_f[:, 0, 0:E], count[:, :], exp_sb[:, 1, :], ALU.subtract))
            step(dve.tensor_scalar(cnt_i[:, :], tiles_f[:, 0, 0:E], float(P - 1), None, ALU.add))
            step(dve.tensor_scalar(tiles_i[:, :], cnt_i[:, :], P.bit_length() - 1, None, ALU.logical_shift_right))
            step(dve.tensor_copy(hop[:, :], tiles_i[:, :]))
            end = [tiles_f[:, 0, 0:E], tiles_f[:, 1, 0:E]]
            step(dve.tensor_copy(end[0], hop[:, :]))
            n = 0
            s = 1
            while s < E:
                step(dve.tensor_copy(end[1 - n][:, 0:s], end[n][:, 0:s]))
                step(dve.tensor_tensor(end[1 - n][:, s:E], end[n][:, s:E], end[n][:, 0:E - s], ALU.add))
                n = 1 - n
                s *= 2
            ends = end[n]
            step(dve.tensor_tensor(base_d[:, :], ends, hop[:, :], ALU.subtract))
            step(dve.scalar_tensor_tensor(out=base_d[:, :], in0=base_d[:, :], scalar=float(P), in1=exp_sb[:, 1, :],
                                          op0=ALU.mult, op1=ALU.subtract))
            step(dve.memset(past[:, :, 0], 1.0))
            step(dve.tensor_tensor(past[:, :, 1:E + 1], tile_no[:, :].unsqueeze(2).to_broadcast([P, TILES, E]),
                                   ends.unsqueeze(1).to_broadcast([P, TILES, E]), ALU.is_ge))
            step(dve.tensor_tensor(onehot[:, :, :], past[:, :, 0:E], past[:, :, 1:E + 1], ALU.subtract))
            step(dve.tensor_reduce(tile_e[:, :], past[0:1, :, 1:E + 1], AX.X, ALU.add))
            step(dve.tensor_scalar(tile_ei[:, :], tile_e[:, :], float(E - 1), None, ALU.min))
            step(dve.tensor_scalar(hop[:, :], hop[:, :], -1.0, float(QBLOCKS), ALU.mult, ALU.add))
            step(dve.tensor_tensor(walk[0:1, :, :], past[0:1, :, 1:E + 1],
                                   hop[0:1, :].unsqueeze(1).to_broadcast([1, TILES, E]), ALU.mult))
            step(dve.tensor_reduce(tile_b[:, :], walk[0:1, :, :], AX.X, ALU.add))
            step(dve.tensor_tensor(tile_b[:, :], tile_b[:, :], tile_no[0:1, :], ALU.add))
            dve.tensor_scalar(tile_bi[:, :], tile_b[:, :], float(E * QBLOCKS), None, ALU.min).then_inc(tables_ok, 1)
            step(dve.tensor_tensor(ysel[:, :, :], sel[:, :, :, :].rearrange("p g j e -> p (g j) e"),
                                   base_d[:, :].unsqueeze(1).to_broadcast([P, GROUPS * TOP_K * NT, E]), ALU.mult))
            step(dve.tensor_reduce(yslot[:, :, :].rearrange("p g j -> p (g j)"), ysel[:, :, :], AX.X, ALU.add))
            dve.tensor_tensor(yslot_i[:, :], yslot[:, :, :].rearrange("p g j -> p (g j)"),
                              slot_f[:, :, :].rearrange("p g j -> p (g j)"), ALU.add).then_inc(yslot_ok, 1)

            def tile_in(t, r):
                dve.wait_ge(xs_in[r], 16 * (t // RING + 1) if isinstance(t, int) else (t - r) * (16 // RING) + 16)
                if not isinstance(t, int) or t >= 2:
                    dve.wait_ge(act_ok, t - 1)
                    dve.wait_ge(h_ok, t - 1)
                at_least(dve, gate_ok, t)
                dve.tensor_tensor(gate_j[:, :], xs[r][:, D:ROW], onehot[:, ds(t, 1), :].rearrange("p a e -> p (a e)"),
                                  ALU.mult).then_inc(gatej_ok, 1)
                dve.wait_ge(gatej_ok, t + 1)
                dve.tensor_reduce(gate[r % 2][:, 0:1], gate_j[:, :], AX.X, ALU.add).then_inc(gate_ok, 1)
                dve.wait_ge(xsT_ps, t + 1)
                if not isinstance(t, int) or t >= 2:
                    dve.wait_ge(sw_ps, t - 1)
                dve.tensor_copy(xsT[r % 2][:, :, :].rearrange("p k c -> p (k c)"), bank[0][:, 0:D]).then_inc(xsT_ok, 1)

            def product(t, r):
                dve.wait_ge(act_ok, t + 1)
                dve.wait_ge(sw_ps, t + 1)
                dve.wait_ge(gate_ok, t + 1)
                if not isinstance(t, int) or t >= 2:
                    dve.wait_ge(hT_ps, t - 1)
                dve.scalar_tensor_tensor(out=h2[r % 2][:, :], in0=bank[2][:, :], scalar=gate[r % 2][:, 0:1],
                                         in1=act2[r % 2][:, :], op0=ALU.mult, op1=ALU.mult).then_inc(h_ok, 1)

            tile_in(0, 0)
            for t in range(RING):
                tile_in(t + 1, (t + 1) % RING)
                product(t, t)
            with dve.Fori(1, TILES // RING - 1) as i:
                for r in range(RING):
                    tile_in(i * RING + (r + 1), (r + 1) % RING)
                    product(i * RING + r, r)
            for r in range(RING):
                if r < RING - 1:
                    tile_in(TILES - RING + r + 1, r + 1)
                product(TILES - RING + r, r)

            def combine(g, par):
                dve.wait_ge(o_ps, g + 1)
                dve.wait_ge(z1_in[par], (g - par) * 8 + 16)
                at_least(dve, o_ok, g)
                for c in range(2):
                    i = dve.tensor_tensor(z_sb[:, 2 * c:2 * c + 2, :], bank[6 + c][:, :].rearrange("p (t d) -> p t d", t=2),
                                          z1[par][:, 2 * c:2 * c + 2, :], ALU.add)
                i.then_inc(za_ok, 1)
                dve.wait_ge(za_ok, g + 1)
                if isinstance(g, int):
                    dve.wait_ge(gathered[par], 16 * TOP_K * NT * (g // 2 + 1))
                else:
                    dve.wait_ge(gathered[par], (g - par) * (8 * TOP_K * NT) + 16 * TOP_K * NT)
                dve.tensor_tensor(z_sb[:, :, :], z_sb[:, :, :], yg[par][:, 0:NT, :], ALU.add).then_inc(zb_ok, 1)
                dve.wait_ge(zb_ok, g + 1)
                dve.tensor_tensor(z_sb[:, :, :], z_sb[:, :, :], yg[par][:, NT:2 * NT, :], ALU.add).then_inc(zc_ok, 1)
                dve.wait_ge(zc_ok, g + 3)

                def out_free():
                    at_least(dve, o_stored, g * 16)

                layer_norm(1, g + 1, z_sb, o_sb, out_free, o_ok)

            def z1_T(g):
                dve.wait_ge(z1T_ps, g + 1)
                at_least(dve, sw3_ps, g * FC)
                dve.tensor_copy(z1T[:, 1, :], bank[1][:, :]).then_inc(z1T_dve, 1)

            def shared_product(g, c):
                dve.wait_ge(act3_ok, g * FC + (c + 1))
                dve.wait_ge(sw3_ps, g * FC + (c + 1))
                at_least(dve, o_ps, g)
                dve.tensor_tensor(h3T[:, c, :], bank[4 + c % 2][:, :], act3[c % 2], ALU.mult).then_inc(h3_ok, 1)

            def phase3(g, par, prev):
                z1_T(g)
                if prev:
                    shared_product(g, 0)
                    combine(g - 1, 1 - par)
                for c in range(1 if prev else 0, FC):
                    shared_product(g, c)

            phase3(0, 0, False)
            phase3(1, 1, True)
            with dve.Fori(0, (GROUPS - 2) // 2) as i:
                for u in range(2):
                    phase3(i * 2 + (2 + u), u, True)
            combine(GROUPS - 1, 1)


OUT_SHAPE = (16, 512, 256)


def kernel(L0_attn_x, L0_attn_Wq, L0_attn_bq, L0_attn_Wk, L0_attn_bk, L0_attn_Wv, L0_attn_bv, L0_ffn_router_DE,
           L0_ffn_w_in_shared_FD, L0_ffn_w_out_shared_DF, L0_ffn_w_swiglu_FD, L0_ffn_w_in_eDF, L0_ffn_w_swiglu_eDF,
           L0_ffn_w_out_eFD):
    import numpy as np
    import concourse.bacc as bacc
    from concourse.bass_utils import run_bass_kernel_spmd

    blocks = np.arange(P) // BLOCK
    feeds = {
        "x": L0_attn_x, "wqT": np.transpose(L0_attn_Wq), "wkT": np.transpose(L0_attn_Wk), "wvT": np.transpose(L0_attn_Wv),
        "bq": np.asarray(L0_attn_bq).reshape(DC, P).T, "bk": np.asarray(L0_attn_bk).reshape(DC, P).T, "bv": np.broadcast_to(np.asarray(L0_attn_bv)[None, :], (P, D)),
        "router": L0_ffn_router_DE, "w_in_shT": np.transpose(L0_ffn_w_in_shared_FD),
        "w_sw_shT": np.transpose(L0_ffn_w_swiglu_FD), "w_out_shT": np.transpose(L0_ffn_w_out_shared_DF),
        "w_in": L0_ffn_w_in_eDF, "w_sw": L0_ffn_w_swiglu_eDF, "w_out": L0_ffn_w_out_eFD,
        "ident": np.eye(P, dtype=np.float32),
        "mask": np.where(blocks[:, None] == blocks[None, :], 0.0, OFF_BLOCK).astype(np.float32),
        "tri": np.stack([np.triu(np.ones((P, P), np.float32), 1), np.ones((P, P), np.float32)], 1),
        "experts": np.broadcast_to(np.stack([np.arange(E), np.arange(E) * QROWS]).astype(np.float32)[None], (P, 2, E)),
    }
    nc = bacc.Bacc("TRN2", target_bir_lowering=False, num_devices=1)
    arrays, args = {}, {}
    for name, a in feeds.items():
        a = np.ascontiguousarray(a)
        arrays[f"in_{name}"] = a
        args[name] = nc.dram_tensor(f"in_{name}", a.shape, mybir.dt.from_np(a.dtype), kind="ExternalInput").ap()
    args["out"] = nc.dram_tensor("out_0", OUT_SHAPE, F32, kind="ExternalOutput").ap()
    build(nc, **args)
    return run_bass_kernel_spmd(nc, [arrays], core_ids=[0]).results[0]["out_0"]
```

```python
from contextlib import ExitStack

import concourse.bass as bass
from concourse import mybir
from concourse.bass import IndirectOffsetOnAxis, ds

ALU = mybir.AluOpType
ACT = mybir.ActivationFunctionType
AX = mybir.AxisListType
F32 = mybir.dt.float32
F32R = mybir.dt.float32r
BF16 = mybir.dt.bfloat16
I32 = mybir.dt.int32
U32 = mybir.dt.uint32

P = 128
D = 256
DC = D // P
F = 512
FC = F // P
HALF = 3 * F
E = 8
TOP_K = 2
TOKENS = 16 * 512
BLOCK = 32
HALVES = 2 * E
NT = 4
GROUP = NT * P
GROUPS = TOKENS // GROUP
TILES = TOP_K * TOKENS // P + E
QBLOCKS = TOKENS // P + 1
QROWS = QBLOCKS * P
ROW = D + E
RING = 4
EPS = 1e-5
OFF_BLOCK = -1e30
BIG = 3e38
RSQRT_MAGIC = 0x5F3759DF
NEWTON = 3


def at_least(eng, sem, n):
    if not isinstance(n, int) or n > 0:
        eng.wait_ge(sem, n)


def build(nc, x, wqT, wkT, wvT, bq, bk, bv, router, w_in_shT, w_sw_shT, w_out_shT, w_in, w_sw, w_out,
          ident, mask, tri, experts, out):
    with ExitStack() as ctx:
        ends = {}

        def sb(name, shape, dt=F32):
            a = ctx.enter_context(nc.sbuf_tensor(name, shape, dt))
            ends[name] = nc.sbuf_base
            return a

        def over(name, owner, shape, last, dt=F32R):
            size = 4
            for n in shape[1:]:
                size *= n
            return nc.alloc_sbuf_tensor_at(name, shape, dtype=dt, offset=ends[owner] - 4 * last - size)

        def sem(name):
            return ctx.enter_context(nc.semaphore(name))

        bank = [ctx.enter_context(nc.psum_tensor(f"bank{i}", [P, 512], F32)) for i in range(8)]

        w_hi = sb("w_hi", [P, HALVES, HALF], F32R)
        w_lo = sb("w_lo", [P, HALVES, HALF], BF16)
        w_raw = over("w_raw", "w_hi", [P, HALF], 0, F32)
        w_qkv_hi = sb("w_qkv_hi", [P, 3 * DC, D], F32R)
        w_qkv_lo = sb("w_qkv_lo", [P, 3 * DC, D], F32R)
        bq_sb = sb("bq_sb", [P, DC])
        bk_sb = sb("bk_sb", [P, DC])
        bv_sb = sb("bv_sb", [P, D])
        router_sb = sb("router_sb", [P, DC, E])
        ident_sb = sb("ident_sb", [P, P])
        mask_sb = sb("mask_sb", [P, P])
        trib = sb("trib", [P, 2, P], BF16)
        exp_sb = sb("exp_sb", [P, 2, E])

        x_rows = sb("x_rows", [P, 2, NT, D])
        x_sb = [x_rows[:, i, :, :] for i in range(2)]
        xT_hi = sb("xT_hi", [P, DC, GROUP], F32R)
        xT_lo = sb("xT_lo", [P, DC, GROUP], F32R)
        w_raw_last = over("w_raw_last", "xT_lo", [P, HALF], 0, F32)
        qT = sb("qT", [P, DC, GROUP])
        keys_values = sb("keys_values", [P, 2 * NT * D])
        kT = keys_values[:, 0:DC * GROUP].rearrange("p (k n) -> p k n", k=DC)
        v_sb = keys_values[:, NT * D:2 * NT * D].rearrange("p (t d) -> p t d", t=NT)
        x1T = kT
        s_sb = sb("s_sb", [P, NT, P])
        p_sb = s_sb
        nmax = sb("nmax", [P, NT])
        rsum = sb("rsum", [P, NT])
        rinv = sb("rinv", [P, NT])
        pT = sb("pT", [P, NT, P])
        x1row = [sb(f"x1row{i}", [P, NT, ROW]) for i in range(2)]
        tri_sb = x1row[0][:, 0, 0:2 * P].rearrange("p (a c) -> p a c", a=2)
        logit = sb("logit", [P, NT, E])
        en = sb("en", [P, NT, E])
        top = sb("top", [P, NT, 8])
        topi = sb("topi", [P, NT, 8], U32)
        topf = sb("topf", [P, TOP_K, NT])
        chosen = sb("chosen", [P, NT, E], BF16)
        count = sb("count", [P, E])
        place = sb("place", [P, NT, E])
        place2 = sb("place2", [P, TOP_K, NT, E])
        slot_i = sb("slot_i", [P, 2, TOP_K, NT], I32)
        sel = sb("sel", [P, GROUPS, TOP_K * NT, E], BF16)
        slot_f = sb("slot_f", [P, GROUPS, TOP_K * NT])

        stats = sb("stats", [P, NT, 6])
        mv = sb("mv", [P, NT, 2])
        veps = sb("veps", [P, NT])
        halfi = sb("halfi", [P, NT], I32)
        rs = sb("rs", [P, NT])
        rs_a = sb("rs_a", [P, NT])
        rs_b = sb("rs_b", [P, NT])
        rs_c = sb("rs_c", [P, NT])
        shift = sb("shift", [P, NT])

        cnt_i = sb("cnt_i", [P, E], I32)
        tiles_i = sb("tiles_i", [P, E], I32)
        tiles_f = sb("tiles_f", [P, 2, E + 4])
        pad_f = sb("pad_f", [P, E])
        pad_i = sb("pad_i", [P, E], I32)
        partno = sb("partno", [P, 1])
        zero_row = sb("zero_row", [P, ROW])
        tile_no = sb("tile_no", [P, TILES])
        spare = x_rows[:, :, :, :].rearrange("p i t d -> p (i t d)")
        past = spare[:, 0:TILES * (E + 1)].rearrange("p (t e) -> p t e", t=TILES)
        onehot = qT[:, :, :].rearrange("p k n -> p (k n)")[:, 0:TILES * E // 2].bitcast(BF16).rearrange("p (t e) -> p t e", t=TILES)
        hop = sb("hop", [P, E])
        walk = keys_values[:, 0:TILES * E].rearrange("p (t e) -> p t e", t=TILES)
        tile_e = spare[0:1, TILES * (E + 1):TILES * (E + 2)]
        tile_b = spare[0:1, TILES * (E + 2):TILES * (E + 3)]
        tile_ei = pT[0:1, 2:4, :].rearrange("p a b -> p (a b)")[:, 0:TILES].bitcast(I32)
        tile_bi = tile_no[0:1, :].bitcast(I32)
        base_d = sb("base_d", [P, E])
        ysel = keys_values[:, 0:GROUPS * TOP_K * NT * E].rearrange("p (j e) -> p j e", e=E)
        group_slots = [sb(f"group_slots{i}", [P, TOP_K * NT], I32) for i in range(2)]
        yslot_i = qT[:, :, :].rearrange("p k n -> p (k n)")[:, 800:800 + GROUPS * TOP_K * NT].bitcast(I32)

        def flat(a):
            return a.rearrange("p a b -> p (a b)")

        def f32(a):
            return a.bitcast(F32)

        xs = [x1row[0][:, i, :] for i in range(RING)]
        y2 = [x1row[1][:, i, 0:D] for i in range(RING)]
        xs_hi = [xT_hi[:, i, 0:D].rearrange("p (k c) -> p k c", k=DC) for i in range(2)]
        xs_lo = [xT_hi[:, i, D:2 * D].rearrange("p (k c) -> p k c", k=DC) for i in range(2)]
        xs_b = [flat(qT[:, :, :])[:, 544 + i * P:544 + (i + 1) * P].bitcast(BF16).rearrange("p (k c) -> p k c", k=DC)
                for i in range(2)]
        h_hi = over("h_hi", "x_rows", [P, FC, P], 0)
        h_lo = over("h_lo", "x_rows", [P, FC, P], F)
        h_b = flat(pT[:, 0:2, :]).bitcast(BF16).rearrange("p (c k) -> p c k", c=FC)
        gate = [sb(f"gate{i}", [P, 1]) for i in range(2)]
        gate_j = sb("gate_j", [P, E])
        act2 = over("act2", "xT_lo", [P, F], 0, F32)[:, :]
        h2 = over("h2", "xT_lo", [P, F], F, F32)[:, :]
        shared_raw = s_sb[:, :, :].rearrange("p t k -> p (t k)")

        queues = nc.dram_tensor("queues", [E * QROWS + P, ROW], F32, kind="Internal").ap()
        x1_dram = nc.dram_tensor("x1_dram", [TOKENS, D], F32, kind="Internal").ap()
        y_dram = nc.dram_tensor("y_dram", [TILES * P, D], F32, kind="Internal").ap()

        x_g = x.rearrange("b s d -> (b s) d").rearrange("(g t p) d -> g p t d", g=GROUPS, t=NT)
        x1_g = x1_dram.rearrange("(g t p) d -> g p t d", g=GROUPS, t=NT)
        out_g = out.rearrange("b s d -> (b s) d").rearrange("(g t p) d -> g p t d", g=GROUPS, t=NT)
        wi_g = w_in.rearrange("e (k p) f -> p (e k) f", k=DC)
        ws_g = w_sw.rearrange("e (k p) f -> p (e k) f", k=DC)
        wo_g = w_out.rearrange("e (h c p) d -> p (e h) c d", h=2, c=FC // 2)

        z1 = [rows[:, :, 0:D] for rows in x1row]
        free = flat(w_hi[:, :, :])
        z1_hi = free[:, 0:DC * GROUP].rearrange("p (k n) -> p k n", k=DC)
        z1_lo = free[:, DC * GROUP:2 * DC * GROUP].rearrange("p (k n) -> p k n", k=DC)
        h3_hi = free[:, 2048:2048 + FC * GROUP].rearrange("p (c n) -> p c n", c=FC)
        h3_lo = free[:, 4096:4096 + FC * GROUP].rearrange("p (c n) -> p c n", c=FC)
        rows_of = flat(w_lo[:, :, :]).bitcast(F32)
        h3 = [rows_of[:, 7168 + i * GROUP:7168 + (i + 1) * GROUP] for i in range(2)]
        act3 = [rows_of[:, 6144 + i * GROUP:6144 + (i + 1) * GROUP] for i in range(2)]
        yg = [rows_of[:, i * 2048:(i + 1) * 2048].rearrange("p (j d) -> p j d", d=D) for i in range(2)]
        z_sb, o_sb = (rows_of[:, 4096 + i * NT * D:4096 + (i + 1) * NT * D].rearrange("p (t d) -> p t d", d=D) for i in range(2))
        shared_hi = [over("shi_hi", "keys_values", [P, DC, F], 0), over("shs_hi", "w_qkv_lo", [P, DC, F], 0),
                     over("sho_hi", "w_qkv_lo", [P, FC, D], 2 * DC * F)]
        shared_lo = [over("shi_lo", "keys_values", [P, DC, F], DC * F), over("shs_lo", "w_qkv_lo", [P, DC, F], DC * F),
                     over("sho_lo", "x_rows", [P, FC, D], FC * D)]

        const_in = sem("const_in")
        ident_in = sem("ident_in")
        attn_in = [sem(f"attn_in{i}") for i in range(3)]
        x_in = [sem(f"x_in{i}") for i in range(2)]
        expert_in = sem("expert_in")
        w_hi_ok = sem("w_hi_ok")
        w_lo_ok = sem("w_lo_ok")
        shared_in = sem("shared_in")
        shared_hi_ok = sem("shared_hi_ok")
        shared_lo_ok = sem("shared_lo_ok")
        tri_ok = sem("tri_ok")
        start_ok = sem("start_ok")
        xT_ps = sem("xT_ps")
        qkv_hi_ok = sem("qkv_hi_ok")
        qkv_lo_ok = sem("qkv_lo_ok")
        x_hi_ok = sem("x_hi_ok")
        x_lo_ok = sem("x_lo_ok")
        q_ps = sem("q_ps")
        q_ok = sem("q_ok")
        k_ps = sem("k_ps")
        k_ok = sem("k_ok")
        v_ps = sem("v_ps")
        v_ok = sem("v_ok")
        s_ps = sem("s_ps")
        s_ok = sem("s_ok")
        p_ok = sem("p_ok")
        pT_ps = sem("pT_ps")
        pT_ok = sem("pT_ok")
        rinv_ok = sem("rinv_ok")
        pv_ps = sem("pv_ps")
        y_ok = sem("y_ok")
        stats_ok = [sem(f"stats_ok{i}") for i in range(2)]
        mv_ok = [sem(f"mv_ok{i}") for i in range(2)]
        veps_ok = [sem(f"veps_ok{i}") for i in range(2)]
        half_ok = [sem(f"half_ok{i}") for i in range(2)]
        rs_ok = [[sem(f"rs_ok{j}_{i}") for i in range(NEWTON + 1)] for j in range(2)]
        rsa_ok = [[sem(f"rsa_ok{j}_{i}") for i in range(NEWTON)] for j in range(2)]
        rsb_ok = [[sem(f"rsb_ok{j}_{i}") for i in range(NEWTON)] for j in range(2)]
        shift_ok = [sem(f"shift_ok{i}") for i in range(2)]
        x1_act = sem("x1_act")
        x1_dve = sem("x1_dve")
        x1T_ps = sem("x1T_ps")
        x1T_act = sem("x1T_act")
        x1T_dve = sem("x1T_dve")
        logit_ps = sem("logit_ps")
        logit_ok = sem("logit_ok")
        en_ok = sem("en_ok")
        en1_ok = sem("en1_ok")
        gates_ok = sem("gates_ok")
        top_ok = sem("top_ok")
        topi_ok = sem("topi_ok")
        topf_ok = sem("topf_ok")
        sel_ok = sem("sel_ok")
        chosen_ok = sem("chosen_ok")
        rank_ps = sem("rank_ps")
        place_ok = sem("place_ok")
        count_ok = sem("count_ok")
        place2_ok = sem("place2_ok")
        slotf_ok = sem("slotf_ok")
        slot_ok = sem("slot_ok")
        scattered = [sem(f"scattered{i}") for i in range(2)]
        x1_stored = [sem(f"x1_stored{i}") for i in range(2)]
        t_iota = sem("t_iota")
        t_step = sem("t_step")
        t_pad = sem("t_pad")
        padded = sem("padded")
        idle_padded = sem("idle_padded")
        tables_ok = sem("tables_ok")
        yslot_ok = sem("yslot_ok")
        xs_in = [sem(f"xs_in{i}") for i in range(RING)]
        xsT_ps = sem("xsT_ps")
        xs_hi_ok = sem("xs_hi_ok")
        xs_lo_ok = sem("xs_lo_ok")
        gatej_ok = sem("gatej_ok")
        gate_ok = sem("gate_ok")
        mid_ps = sem("mid_ps")
        act_ok = sem("act_ok")
        sw_ps = sem("sw_ps")
        h_ok = sem("h_ok")
        hT_ps = sem("hT_ps")
        h_hi_ok = sem("h_hi_ok")
        h_lo_ok = sem("h_lo_ok")
        h_b_ok = sem("h_b_ok")
        y_ps = sem("y_ps")
        y2_ok = sem("y2_ok")
        y_stored = [sem(f"y_stored{i}") for i in range(RING)]
        z1_in = [sem(f"z1_in{i}") for i in range(2)]
        z1T_ps = sem("z1T_ps")
        z1_hi_ok = sem("z1_hi_ok")
        z1_lo_ok = sem("z1_lo_ok")
        mid3_ps = sem("mid3_ps")
        sw3_ps = sem("sw3_ps")
        act3_ok = sem("act3_ok")
        h3_ok = sem("h3_ok")
        h3_hi_ok = sem("h3_hi_ok")
        h3_lo_ok = sem("h3_lo_ok")
        o_ps = sem("o_ps")
        gathered = [sem(f"gathered{i}") for i in range(2)]
        slots_here = sem("slots_here")
        za_ok = sem("za_ok")
        pair_ok = sem("pair_ok")
        zc_ok = sem("zc_ok")
        o_ok = sem("o_ok")
        o_stored = sem("o_stored")

        block = ctx.enter_context(nc.Block())

        def wait_apart(eng, sem_, n):
            n = n if isinstance(n, int) else eng.snap(n)
            eng.wait_ge(ident_in, 16)
            at_least(eng, sem_, n)

        def groups(eng, body, ahead):
            for g in range(ahead):
                body(g, g % 2)
            pairs = (GROUPS - ahead) // 2
            with eng.Fori(0, pairs) as i:
                for u in range(2):
                    body(i * 2 + (ahead + u), (ahead + u) % 2)
            for g in range(ahead + 2 * pairs, GROUPS):
                body(g, g % 2)

        @block.sync
        def _(sp):
            sp.dma_start(ident_sb[:, :], ident).then_inc(ident_in, 16)
            sp.dma_start(x_sb[0], x_g[0]).then_inc(x_in[0], 16)
            for i, src in enumerate((wqT, wkT, wvT)):
                sp.dma_start(w_raw[:, i * DC * D:(i + 1) * DC * D].rearrange("p (k e) -> p k e", k=DC),
                             src.rearrange("(k p) e -> p k e", p=P)).then_inc(attn_in[i], 16)
            sp.dma_start(x_sb[1], x_g[1]).then_inc(x_in[1], 16)
            sp.dma_start(bq_sb[:, :], bq).then_inc(const_in, 16)
            sp.dma_start(bk_sb[:, :], bk).then_inc(const_in, 16)
            sp.dma_start(bv_sb[:, :], bv).then_inc(const_in, 16)
            sp.dma_start(router_sb[:, :, :], router.rearrange("(k p) e -> p k e", p=P)).then_inc(const_in, 16)
            sp.dma_start(mask_sb[:, :], mask).then_inc(const_in, 16)
            sp.dma_start(tri_sb, tri).then_inc(const_in, 16)
            sp.dma_start(exp_sb[:, :, :], experts).then_inc(const_in, 16)

            def phase1(g, par):
                if not (isinstance(g, int) and g < 2):
                    store_x1(g - 2, par)
                if not (isinstance(g, int) and g == 0):
                    if not (isinstance(g, int) and g + 1 == GROUPS):
                        sp.wait_ge(y_ok, g)
                        sp.dma_start(x_sb[1 - par], x_g[g + 1] if isinstance(g, int) else x_g[ds(g + 1, 1)].rearrange("a p t d -> p (a t) d"))\
                          .then_inc(x_in[1 - par], 16)
                    load_half(g - 1, w_raw)

            def load_half(g, raw):
                at_least(sp, w_lo_ok, g)
                for i, src in enumerate((wi_g, ws_g)):
                    sp.dma_start(raw[:, i * F:(i + 1) * F], src[:, ds(g, 1), :].rearrange("p a f -> p (a f)")).then_inc(expert_in, 16)
                sp.dma_start(raw[:, 2 * F:3 * F].rearrange("p (c d) -> p c d", d=D),
                             wo_g[:, ds(g, 1), :, :].rearrange("p a c d -> p (a c) d")).then_inc(expert_in, 16)

            def store_x1(g, par):
                sp.wait_ge(x1_act, g + 1)
                sp.wait_ge(x1_dve, g + 1)
                dst = x1_g[g] if isinstance(g, int) else x1_g[ds(g, 1)].rearrange("a p t d -> p (a t) d")
                sp.dma_start(dst, x1row[par][:, :, 0:D]).then_inc(x1_stored[par], 16)

            sp.wait_ge(qkv_lo_ok, 3)
            phase1(0, 0)
            phase1(1, 1)
            with sp.Fori(0, (GROUPS - 4) // 2) as i:
                for u in range(2):
                    phase1(i * 2 + (2 + u), u)
            phase1(GROUPS - 2, 0)
            phase1(GROUPS - 1, 1)
            store_x1(GROUPS - 2, 0)
            sp.wait_ge(v_ps, GROUPS)
            load_half(GROUPS - 1, w_raw_last)
            store_x1(GROUPS - 1, 1)

            sp.wait_ge(t_iota, 3)
            sp.dma_start(queues[E * QROWS:E * QROWS + P, :], zero_row[:, :]).then_inc(idle_padded, 16)
            for s in range(2):
                sp.wait_ge(scattered[s], 16 * TOP_K * NT * GROUPS // 2)
            sp.wait_ge(padded, 16 * E)
            sp.wait_ge(idle_padded, 16)
            sp.wait_ge(tables_ok, 1)
            for s in range(2):
                sp.wait_ge(x1_stored[s], 16 * GROUPS // 2)

            def load_xs(t, r):
                if not (isinstance(t, int) and t < RING):
                    sp.wait_ge(xsT_ps, t - RING + 1)
                    sp.wait_ge(gate_ok, t - RING + 1)
                b = sp.value_load(tile_bi[0:1, ds(t, 1)], min_val=0, max_val=E * QBLOCKS)
                sp.dma_start(xs[r], queues[ds(b * P, P), :]).then_inc(xs_in[r], 16)

            def store_y(t, r):
                sp.wait_ge(y2_ok, t + 1)
                sp.dma_start(y_dram[ds(t * P, P), :], y2[r]).then_inc(y_stored[r], 16)

            for t in range(RING):
                load_xs(t, t)
            with sp.Fori(0, TILES // RING - 1) as i:
                for r in range(RING):
                    load_xs(i * RING + (r + RING), r)
                    store_y(i * RING + r, r)
            for r in range(RING - 1):
                store_y(TILES - RING + r, r)

            def z_load(g, par):
                if not isinstance(g, int) or g >= 2:
                    sp.wait_ge(z1T_ps, g - 1)
                    sp.wait_ge(za_ok, g - 1)
                src = x1_g[g] if isinstance(g, int) else x1_g[ds(g, 1)].rearrange("a p t d -> p (a t) d")
                sp.dma_start(z1[par], src).then_inc(z1_in[par], 16)

            def z_store(g):
                sp.wait_ge(o_ok, g + 1)
                dst = out_g[g] if isinstance(g, int) else out_g[ds(g, 1)].rearrange("a p t d -> p (a t) d")
                sp.dma_start(dst, o_sb[:, :, :]).then_inc(o_stored, 16)

            def phase3(g, par):
                z_load(g, par)
                if not isinstance(g, int) or g >= 2:
                    z_store(g - 2)

            sp.wait_ge(xsT_ps, TILES)
            sp.wait_ge(gate_ok, TILES)
            phase3(0, 0)
            store_y(TILES - 1, RING - 1)
            for r in range(RING):
                sp.wait_ge(y_stored[r], 16 * TILES // RING)
            phase3(1, 1)
            with sp.Fori(0, (GROUPS - 2) // 2) as i:
                for u in range(2):
                    phase3(i * 2 + (2 + u), u)
            z_store(GROUPS - 2)
            z_store(GROUPS - 1)
            sp.wait_ge(o_stored, 16 * GROUPS)

        @block.gpsimd
        def _(pool):
            pool.memset(zero_row[:, :], 0.0).then_inc(t_iota, 1)
            pool.iota(tile_no[:, :], pattern=[[1, TILES]], base=0, channel_multiplier=0,
                      allow_small_or_imprecise_dtypes=True).then_inc(t_iota, 1)
            pool.iota(partno[:, :], pattern=[[0, 1]], base=0, channel_multiplier=1,
                      allow_small_or_imprecise_dtypes=True).then_inc(t_iota, 1)
            pool.wait_ge(ident_in, 16)

            def scatter(g, par):
                wait_apart(pool, gates_ok, g + 1)
                for k in range(TOP_K):
                    for t in range(NT):
                        pool.indirect_dma_start(
                            out=queues, out_offset=IndirectOffsetOnAxis(ap=slot_i[:, par, k, t:t + 1], axis=0),
                            in_=x1row[par][:, t, :], in_offset=None).then_inc(scattered[par], 16)

            def split_expert(g, raw=w_raw):
                pool.wait_ge(w_hi_ok, g + 1)
                pool.tensor_tensor(w_lo[:, ds(g, 1), :].rearrange("p a n -> p (a n)"), raw[:, :],
                                   f32(w_hi[:, ds(g, 1), :].rearrange("p a n -> p (a n)")), ALU.subtract).then_inc(w_lo_ok, 1)

            def phase1(g, par):
                if not (isinstance(g, int) and g < 2):
                    split_expert(g - 2)
                    scatter(g - 2, par)

            groups(pool, phase1, 2)
            split_expert(GROUPS - 2)
            scatter(GROUPS - 2, 0)
            scatter(GROUPS - 1, 1)

            pool.wait_ge(t_pad, 1)
            for e in range(E):
                pool.indirect_dma_start(
                    out=queues, out_offset=IndirectOffsetOnAxis(ap=pad_i[:, e:e + 1], axis=0),
                    in_=zero_row[:, :], in_offset=None).then_inc(padded, 16)

            split_expert(GROUPS - 1, w_raw_last)

            pool.wait_ge(yslot_ok, 1)
            n = 0
            for m, src in enumerate((w_in_shT, w_sw_shT, w_out_shT)):
                k = src.shape[0] // P
                for half in range(2):
                    c = slice(half * k // 2, (half + 1) * k // 2)
                    rows = shared_raw.rearrange("p (k n) -> p k n", k=k // 2)
                    if n > 0:
                        pool.wait_ge(shared_lo_ok, n)
                    pool.dma_start(rows,
                                   src.rearrange("(h k p) n -> h p k n", h=2, p=P)[half]).then_inc(shared_in, 16)
                    n += 1
                    pool.wait_ge(shared_in, 16 * n)
                    pool.tensor_copy(shared_hi[m][:, c, :], rows).then_inc(shared_hi_ok, 1)
                    pool.wait_ge(shared_hi_ok, n)
                    pool.tensor_tensor(shared_lo[m][:, c, :], rows, f32(shared_hi[m][:, c, :]), ALU.subtract).then_inc(shared_lo_ok, 1)

            for r in range(RING):
                pool.wait_ge(y_stored[r], 16 * TILES // RING)

            def gather(g, par):
                pool.wait_ge(zc_ok, g + 1)
                pool.tensor_copy(group_slots[par][:, :], yslot_i[:, ds(g * (TOP_K * NT), TOP_K * NT)]).then_inc(slots_here, 1)
                wait_apart(pool, slots_here, g + 1)
                for j in range(TOP_K * NT):
                    ix = group_slots[par][:, j:j + 1]
                    pool.indirect_dma_start(
                        out=yg[par][:, j, :], out_offset=None, in_=y_dram,
                        in_offset=IndirectOffsetOnAxis(ap=ix, axis=0)).then_inc(gathered[par], 16)

            def pair(g, par):
                if isinstance(g, int):
                    pool.wait_ge(gathered[par], 16 * TOP_K * NT * (g // 2 + 1))
                else:
                    pool.wait_ge(gathered[par], (g - par) * (8 * TOP_K * NT) + 16 * TOP_K * NT)
                pool.tensor_tensor(yg[par][:, 0:NT, :], yg[par][:, 0:NT, :], yg[par][:, NT:2 * NT, :], ALU.add).then_inc(pair_ok, 1)

            def gather_and_pair(g, par):
                gather(g, par)
                if not (isinstance(g, int) and g == 0):
                    pair(g - 1, 1 - par)

            groups(pool, gather_and_pair, 2)
            pair(GROUPS - 1, 1)

        @block.tensor
        def _(pe):
            def group_transposes(rows, banks, g, done):
                for k in range(DC):
                    for t in range(NT):
                        mm = pe.transpose(banks[k][:, t * P:(t + 1) * P], rows[:, t, k * P:(k + 1) * P], ident_sb[:, :])
                mm.then_inc(done, 1)

            def project(w, dst, c, sig, w_ready):
                if w_ready:
                    pe.wait_ge(qkv_lo_ok, w + 1)
                for n, (wp, rows) in enumerate(((w_qkv_hi, xT_hi), (w_qkv_lo, xT_hi), (w_qkv_hi, xT_lo))):
                    for k in range(DC):
                        mm = pe.matmul(dst[:, :], wp[:, w * DC + k, c * P:(c + 1) * P], rows[:, k, :],
                                       start=(n == 0 and k == 0), stop=(n == 2 and k == DC - 1))
                mm.then_inc(sig, 1)

            def probs_T(g):
                pe.wait_ge(p_ok, g + 1)
                for t in range(NT):
                    mm = pe.transpose(bank[2][:, t * P:(t + 1) * P], p_sb[:, t, :], ident_sb[:, :])
                mm.then_inc(pT_ps, 1)

            def probs_v(g):
                pe.wait_ge(pT_ok, g + 1)
                pe.wait_ge(v_ok, g + 1)
                for t in range(NT):
                    mm = pe.matmul(bank[5 + t // 2][:, (t % 2) * D:(t % 2 + 1) * D], pT[:, t, :], v_sb[:, t, :],
                                   start=True, stop=True)
                mm.then_inc(pv_ps, 1)

            def x1_T(g, par):
                pe.wait_ge(x1_act, g + 1)
                pe.wait_ge(x1_dve, g + 1)
                group_transposes(x1row[par], (bank[5], bank[6]), g, x1T_ps)

            def logits(g):
                pe.wait_ge(x1T_act, g + 1)
                pe.wait_ge(x1T_dve, g + 1)
                for t in range(NT):
                    for k in range(DC):
                        mm = pe.matmul(bank[7][:, t * E:(t + 1) * E], x1T[:, k, t * P:(t + 1) * P], router_sb[:, k, :],
                                       start=(k == 0), stop=(k == DC - 1))
                mm.then_inc(logit_ps, 1)

            def ranks(g):
                pe.wait_ge(chosen_ok, g + 1)
                ch = chosen[:, :, :].rearrange("p t e -> p (t e)")
                rk = bank[7][:, 64:64 + NT * E]
                pe.matmul(rk, trib[:, 0, :], ch, start=True, stop=False, skip_group_check=True)
                for s in range(1, NT):
                    pe.matmul(bank[7][:, 64 + s * E:64 + NT * E], trib[:, 1, :], ch[:, 0:(NT - s) * E],
                              start=False, stop=(s == NT - 1), skip_group_check=True)
                for t in range(NT):
                    mm = pe.matmul(bank[7][:, 128:128 + E], trib[:, 1, :], ch[:, t * E:(t + 1) * E],
                                   start=(t == 0), stop=(t == NT - 1), skip_group_check=True)
                mm.then_inc(rank_ps, 1)

            def stage(g, par, prev):
                pe.wait_ge(x_in[par], (g - par) * 8 + 16)
                at_least(pe, k_ok, g)
                group_transposes(x_sb[par], (bank[0], bank[1]), g, xT_ps)
                if prev == 2:
                    logits(g - 2)
                pe.wait_ge(x_lo_ok, g + 1)
                at_least(pe, v_ok, g)
                project(0, bank[3], 0, q_ps, not prev)
                if prev:
                    probs_T(g - 1)
                project(0, bank[4], 1, q_ps, not prev)
                if prev == 2:
                    ranks(g - 2)
                if prev:
                    probs_v(g - 1)
                project(1, bank[0], 0, k_ps, not prev)
                project(1, bank[1], 1, k_ps, not prev)
                pe.wait_ge(q_ok, g + 1)
                if not prev:
                    pe.wait_ge(qkv_lo_ok, 3)
                for t in range(NT):
                    for n, (rows, w) in enumerate(((xT_hi, w_qkv_hi), (xT_hi, w_qkv_lo), (xT_lo, w_qkv_hi))):
                        for k in range(DC):
                            mm = pe.matmul(bank[3 + t // 2][:, (t % 2) * D:(t % 2 + 1) * D], rows[:, k, t * P:(t + 1) * P],
                                           w[:, 2 * DC + k, :], start=(n == 0 and k == 0), stop=(n == 2 and k == DC - 1))
                mm.then_inc(v_ps, 1)
                pe.wait_ge(k_ok, g + 1)
                at_least(pe, pT_ok, g)
                for t in range(NT):
                    for k in range(DC):
                        c = slice(t * P, (t + 1) * P)
                        mm = pe.matmul(bank[2][:, c], qT[:, k, c], kT[:, k, c], start=(k == 0), stop=(k == DC - 1))
                mm.then_inc(s_ps, 1)
                if prev:
                    x1_T(g - 1, 1 - par)

            pe.wait_ge(ident_in, 16)
            stage(0, 0, 0)
            pe.wait_ge(const_in, 16 * 7)
            pe.wait_ge(tri_ok, 1)
            stage(1, 1, 1)
            with pe.Fori(0, (GROUPS - 2) // 2) as i:
                for u in range(2):
                    stage(i * 2 + (2 + u), u, 2)
            last = GROUPS - 1
            logits(last - 1)
            probs_T(last)
            ranks(last - 1)
            probs_v(last)
            x1_T(last, last % 2)
            logits(last)
            ranks(last)

            pe.wait_ge(count_ok, GROUPS)
            pe.wait_ge(place_ok, GROUPS)
            pe.wait_ge(w_lo_ok, GROUPS)
            pe.wait_ge(tables_ok, 1)

            def xs_T(t, r):
                pe.wait_ge(xs_in[r], 16 * (t // RING + 1) if isinstance(t, int) else (t - r) * (16 // RING) + 16)
                at_least(pe, xs_lo_ok, t)
                for k in range(DC):
                    mm = pe.transpose(bank[0][:, k * P:(k + 1) * P], xs[r][:, k * P:(k + 1) * P], ident_sb[:, :])
                mm.then_inc(xsT_ps, 1)

            def hidden(t, r, first, dst, e, sig, free):
                at_least(pe, free, t)
                for n, (rows, w) in enumerate(((xs_hi, w_hi), (xs_lo, w_hi), (xs_b, w_lo))):
                    for k in range(DC):
                        mm = pe.matmul(dst[:, :], rows[r % 2][:, k, :],
                                       w[:, ds(e * 2 + k, 1), first:first + F].rearrange("p a f -> p (a f)"),
                                       start=(n == 0 and k == 0), stop=(n == 2 and k == DC - 1))
                mm.then_inc(sig, 1)

            def h_T(t):
                pe.wait_ge(h_ok, t + 1)
                at_least(pe, h_lo_ok, t)
                for c in range(FC):
                    mm = pe.transpose(bank[3][:, c * P:(c + 1) * P], h2[:, c * P:(c + 1) * P], ident_sb[:, :])
                mm.then_inc(hT_ps, 1)

            def tile_out(t, r, e):
                pe.wait_ge(h_hi_ok, t + 1)
                if not isinstance(t, int) or t >= 2:
                    pe.wait_ge(y2_ok, t - 1)
                for n, (rows, w) in enumerate(((h_hi, w_hi), (h_lo, w_hi), (h_b, w_lo))):
                    if n > 0:
                        pe.wait_ge((h_lo_ok, h_b_ok)[n - 1], t + 1)
                    for c in range(FC):
                        first = 2 * F + (c % 2) * D
                        mm = pe.matmul(bank[4 + r % 2][:, 0:D], rows[:, c, :],
                                       w[:, ds(e * 2 + c // 2, 1), first:first + D].rearrange("p a f -> p (a f)"),
                                       start=(n == 0 and c == 0), stop=(n == 2 and c == FC - 1))
                mm.then_inc(y_ps, 1)

            def expert_of(t):
                return pe.value_load(tile_ei[0:1, ds(t, 1)], min_val=0, max_val=E - 1)

            def tile(t, r, e, e_prev, prev, ahead):
                if prev:
                    h_T(t - 1)
                hidden(t, r, F, bank[2], e, sw_ps, h_ok)
                e_next = expert_of(t + 1) if ahead > 0 else None
                if prev:
                    tile_out(t - 1, (r - 1) % RING, e_prev)
                if ahead > 1:
                    xs_T(t + 2, (r + 2) % RING)
                if ahead > 0:
                    hidden_in(t + 1, (r + 1) % RING, e_next)
                return e_next

            def hidden_in(t, r, e):
                pe.wait_ge(xs_lo_ok, t + 1)
                hidden(t, r, 0, bank[1], e, mid_ps, act_ok)

            def tiles(first, prev, left):
                e_prev = expert_of(first - 1) if prev else None
                e = expert_of(first)
                for r in range(RING):
                    e_next = tile(first + r, r, e, e_prev, prev or r > 0, left + RING - 1 - r)
                    e_prev, e = e, e_next

            xs_T(0, 0)
            xs_T(1, 1)
            hidden_in(0, 0, expert_of(0))
            tiles(0, False, 2)
            with pe.Fori(1, TILES // RING - 1) as i:
                tiles(i * RING, True, 2)
            tiles(TILES - RING, True, 0)
            h_T(TILES - 1)
            tile_out(TILES - 1, RING - 1, expert_of(TILES - 1))


            def z1_T(g, par):
                pe.wait_ge(z1_in[par], (g - par) * 8 + 16)
                at_least(pe, z1_lo_ok, g)
                group_transposes(z1[par], (bank[0], bank[1]), g, z1T_ps)

            def shared_out(g):
                at_least(pe, za_ok, g)
                for t in range(NT):
                    for c in range(FC):
                        if t == 0:
                            pe.wait_ge(h3_lo_ok, g * FC + (c + 1))
                        for n, (rows, w) in enumerate(((h3_hi, shared_hi), (h3_hi, shared_lo), (h3_lo, shared_hi))):
                            mm = pe.matmul(bank[6 + t // 2][:, (t % 2) * D:(t % 2 + 1) * D], rows[:, c, t * P:(t + 1) * P],
                                           w[2][:, c, :], start=(c == 0 and n == 0), stop=(c == FC - 1 and n == 2))
                mm.then_inc(o_ps, 1)

            def shared_hidden(g):
                pe.wait_ge(z1_lo_ok, g + 1)
                for c in range(FC):
                    for m, b, sig, free in ((0, 2, mid3_ps, act3_ok), (1, 4, sw3_ps, h3_ok)):
                        if not isinstance(g, int) or g * FC + c >= 2:
                            pe.wait_ge(free, g * FC + (c - 1))
                        for n, (w, rows) in enumerate(((shared_hi, z1_hi), (shared_lo, z1_hi), (shared_hi, z1_lo))):
                            for k in range(DC):
                                mm = pe.matmul(bank[b + c % 2][:, :], w[m][:, k, c * P:(c + 1) * P], rows[:, k, :],
                                               start=(n == 0 and k == 0), stop=(n == 2 and k == DC - 1))
                        mm.then_inc(sig, 1)

            def phase3(g, par):
                z1_T(g, par)
                if isinstance(g, int) and g == 0:
                    pe.wait_ge(y2_ok, TILES)
                    pe.wait_ge(shared_lo_ok, 6)
                if not (isinstance(g, int) and g == 0):
                    shared_out(g - 1)
                shared_hidden(g)

            groups(pe, phase3, 2)
            shared_out(GROUPS - 1)

        @block.scalar
        def _(act):
            def probs(g):
                act.wait_ge(s_ok, g + 1)
                at_least(act, pT_ps, g)
                at_least(act, rinv_ok, g)
                for t in range(NT):
                    a = act.activation(p_sb[:, t, :], s_sb[:, t, :], ACT.Exp, bias=nmax[:, t:t + 1], scale=-1.0,
                                       accum_out=rsum[:, t:t + 1])
                a.then_inc(p_ok, 1)

            def probs_T(g):
                act.wait_ge(pT_ps, g + 1)
                at_least(act, pv_ps, g)
                act.activation(pT[:, :, :].rearrange("p t k -> p (t k)"), bank[2][:, :], ACT.Copy).then_inc(pT_ok, 1)

            def x1_T(g):
                act.wait_ge(x1T_ps, g + 1)
                act.activation(x1T[:, 0, :], bank[5][:, :], ACT.Copy).then_inc(x1T_act, 1)

            def gate_exp(g):
                act.wait_ge(logit_ok, g + 1)
                at_least(act, en1_ok, g)
                act.activation(en[:, :, :], logit[:, :, :], ACT.Exp, scale=-1.0).then_inc(en_ok, 1)

            def split_expert(g, raw=w_raw):
                act.wait_ge(expert_in, g * 48 + 48)
                act.activation(w_hi[:, ds(g, 1), :].rearrange("p a n -> p (a n)"), raw[:, :], ACT.Copy).then_inc(w_hi_ok, 1)

            def norm_apply1(g, par):
                act.wait_ge(shift_ok[0], g + 1)
                for t in range(NT // 2):
                    a = act.activation(x1row[par][:, t, 0:D], x1row[par][:, t, 0:D], ACT.Identity,
                                       bias=shift[:, t:t + 1], scale=rs[:, t:t + 1])
                a.then_inc(x1_act, 1)

            def stage(g, par, prev):
                act.wait_ge(xT_ps, g + 1)
                for k in range(DC):
                    a = act.activation(xT_hi[:, k, :], bank[k][:, :], ACT.Copy)
                a.then_inc(x_hi_ok, 1)
                if prev:
                    probs(g - 1)
                if prev == 2:
                    gate_exp(g - 2)
                for c in range(DC):
                    act.wait_ge(q_ps, g * 2 + (c + 1))
                    a = act.activation(qT[:, c, :], bank[3 + c][:, :], ACT.Identity, bias=bq_sb[:, c:c + 1])
                    if prev and c == 0:
                        probs_T(g - 1)
                a.then_inc(q_ok, 1)
                if prev == 2:
                    split_expert(g - 2)
                for c in range(DC):
                    act.wait_ge(k_ps, g * 2 + (c + 1))
                    a = act.activation(kT[:, c, :], bank[c][:, :], ACT.Identity, bias=bk_sb[:, c:c + 1])
                a.then_inc(k_ok, 1)
                if prev:
                    norm_apply1(g - 1, 1 - par)
                    x1_T(g - 1)

            for i in range(3):
                c = slice(i * DC * D, (i + 1) * DC * D)
                act.wait_ge(attn_in[i], 16)
                act.activation(flat(w_qkv_hi[:, :, :])[:, c], w_raw[:, c], ACT.Copy).then_inc(qkv_hi_ok, 1)
            act.wait_ge(const_in, 16 * 7)
            stage(0, 0, 0)
            stage(1, 1, 1)
            with act.Fori(0, (GROUPS - 2) // 2) as i:
                for u in range(2):
                    stage(i * 2 + (2 + u), u, 2)
            last = GROUPS - 1
            probs(last)
            probs_T(last)
            gate_exp(last - 1)
            split_expert(last - 1)
            norm_apply1(last, 1)
            x1_T(last)
            gate_exp(last)
            split_expert(last, w_raw_last)

            def rows_hi(t, r):
                act.wait_ge(xsT_ps, t + 1)
                act.activation(xs_hi[r % 2][:, :, :].rearrange("p k c -> p (k c)"), bank[0][:, 0:D], ACT.Copy).then_inc(xs_hi_ok, 1)

            def silu(t, r):
                act.wait_ge(mid_ps, t + 1)
                act.wait_ge(gate_ok, t + 1)
                at_least(act, h_ok, t)
                act.activation(act2, bank[1][:, :], ACT.Silu, scale=gate[r % 2][:, 0:1]).then_inc(act_ok, 1)

            def hidden_hi(t, r):
                act.wait_ge(hT_ps, t + 1)
                act.activation(h_hi[:, :, :].rearrange("p c k -> p (c k)"), bank[3][:, :], ACT.Copy).then_inc(h_hi_ok, 1)

            def copy_out(t, r):
                act.wait_ge(y_ps, t + 1)
                if not isinstance(t, int) or t >= RING:
                    act.wait_ge(y_stored[r], (t - r) * (16 // RING))
                act.activation(y2[r], bank[4 + r % 2][:, 0:D], ACT.Copy).then_inc(y2_ok, 1)

            def tile(t, r, prev, ahead):
                if ahead:
                    rows_hi(t + 1, (r + 1) % RING)
                silu(t, r)
                if prev:
                    hidden_hi(t - 1, (r - 1) % RING)
                    copy_out(t - 1, (r - 1) % RING)

            rows_hi(0, 0)
            for t in range(RING):
                tile(t, t, t > 0, True)
            with act.Fori(1, TILES // RING - 1) as i:
                for r in range(RING):
                    tile(i * RING + r, r, True, True)
            for r in range(RING):
                tile(TILES - RING + r, r, True, r < RING - 1)
            hidden_hi(TILES - 1, RING - 1)
            copy_out(TILES - 1, RING - 1)

            def shared_act(g):
                act.wait_ge(z1T_ps, g + 1)
                for k in range(DC):
                    a = act.activation(z1_hi[:, k, :], bank[k][:, :], ACT.Copy)
                a.then_inc(z1_hi_ok, 1)
                if not (isinstance(g, int) and g < 2):
                    norm_apply(g - 2)
                for c in range(FC):
                    act.wait_ge(mid3_ps, g * FC + (c + 1))
                    if not isinstance(g, int) or g * FC + c >= 2:
                        act.wait_ge(h3_ok, g * FC + (c - 1))
                    act.activation(act3[c % 2], bank[2 + c % 2][:, :], ACT.Silu).then_inc(act3_ok, 1)
                    if c > 0:
                        shared_h_hi(g, c - 1)
                shared_h_hi(g, FC - 1)

            def shared_h_hi(g, c):
                act.wait_ge(h3_ok, g * FC + (c + 1))
                act.activation(h3_hi[:, c, :], h3[c % 2], ACT.Copy).then_inc(h3_hi_ok, 1)

            def norm_apply(g):
                act.wait_ge(shift_ok[1], g + 1)
                at_least(act, o_stored, g * 16)
                for t in range(NT):
                    a = act.activation(o_sb[:, t, :], z_sb[:, t, :], ACT.Identity, bias=shift[:, t:t + 1], scale=rs[:, t:t + 1])
                a.then_inc(o_ok, 1)

            shared_act(0)
            shared_act(1)
            with act.Fori(2, GROUPS) as g:
                shared_act(g)
            norm_apply(GROUPS - 2)
            norm_apply(GROUPS - 1)

        @block.vector
        def _(dve):
            for i in range(3):
                c = slice(i * DC * D, (i + 1) * DC * D)
                dve.wait_ge(qkv_hi_ok, i + 1)
                dve.tensor_tensor(flat(w_qkv_lo[:, :, :])[:, c], w_raw[:, c], f32(flat(w_qkv_hi[:, :, :])[:, c]), ALU.subtract)\
                   .then_inc(qkv_lo_ok, 1)
            dve.wait_ge(const_in, 16 * 7)
            dve.tensor_copy(trib[:, :, :], tri_sb).then_inc(tri_ok, 1)
            dve.sem_inc(zc_ok, 2)

            def norm_stats(which, n, src):
                for t in range(NT):
                    i = dve.bn_stats(stats[:, t, :], src[:, t, :])
                i.then_inc(stats_ok[which], 1)
                wait_apart(dve, stats_ok[which], n)
                for t in range(NT):
                    i = dve.bn_aggr(mv[:, t, :], stats[:, t, :])
                i.then_inc(mv_ok[which], 1)

            def norm_root(which, n):
                dve.wait_ge(mv_ok[which], n)
                dve.tensor_scalar(veps[:, :], mv[:, :, 1], EPS, None, ALU.add).then_inc(veps_ok[which], 1)
                dve.wait_ge(veps_ok[which], n)
                dve.tensor_scalar(halfi[:, :], veps[:, :].bitcast(I32), 1, None, ALU.logical_shift_right).then_inc(half_ok[which], 1)
                dve.wait_ge(half_ok[which], n)
                dve.tensor_scalar(rs[:, :].bitcast(I32), halfi[:, :], -1.0, float(RSQRT_MAGIC), ALU.mult, ALU.add)\
                   .then_inc(rs_ok[which][0], 1)
                for s in range(NEWTON):
                    dve.wait_ge(rs_ok[which][s], n)
                    dve.tensor_tensor(rs_a[:, :], rs[:, :], rs[:, :], ALU.mult).then_inc(rsa_ok[which][s], 1)
                    dve.wait_ge(rsa_ok[which][s], n)
                    dve.scalar_tensor_tensor(out=rs_b[:, :], in0=rs_a[:, :], scalar=-0.5, in1=veps[:, :],
                                             op0=ALU.mult, op1=ALU.mult).then_inc(rsb_ok[which][s], 1)
                    dve.wait_ge(rsb_ok[which][s], n)
                    dve.scalar_tensor_tensor(out=rs[:, :], in0=rs_b[:, :], scalar=1.5, in1=rs[:, :],
                                             op0=ALU.add, op1=ALU.mult).then_inc(rs_ok[which][s + 1], 1)
                dve.wait_ge(rs_ok[which][NEWTON], n)
                dve.scalar_tensor_tensor(out=shift[:, :], in0=mv[:, :, 0], scalar=-1.0, in1=rs[:, :],
                                         op0=ALU.mult, op1=ALU.mult).then_inc(shift_ok[which], 1)

            def attn_sum(g, par):
                dve.wait_ge(rinv_ok, g + 1)
                dve.wait_ge(pv_ps, g + 1)
                if not isinstance(g, int) or g >= 2:
                    dve.wait_ge(scattered[par], (g - par) * (8 * TOP_K * NT))
                    dve.wait_ge(x1_stored[par], (g - par) * 8)
                for t in range(NT):
                    i = dve.scalar_tensor_tensor(out=x1row[par][:, t, 0:D], in0=bank[5 + t // 2][:, (t % 2) * D:(t % 2 + 1) * D],
                                                 scalar=rinv[:, t:t + 1], in1=x_sb[par][:, t, :], op0=ALU.mult, op1=ALU.add)
                i.then_inc(y_ok, 1)
                dve.wait_ge(y_ok, g + 1)
                norm_stats(0, g + 1, x1row[par][:, :, 0:D])
                norm_root(0, g + 1)
                dve.wait_ge(shift_ok[0], g + 1)
                for t in range(NT // 2, NT):
                    i = dve.tensor_scalar(x1row[par][:, t, 0:D], x1row[par][:, t, 0:D], rs[:, t:t + 1], shift[:, t:t + 1],
                                          ALU.mult, ALU.add)
                i.then_inc(x1_dve, 1)

            def values(g):
                dve.wait_ge(v_ps, g + 1)
                for c in range(2):
                    i = dve.tensor_tensor(v_sb[:, 2 * c:2 * c + 2, :], bank[3 + c][:, :].rearrange("p (t e) -> p t e", t=2),
                                          bv_sb[:, :].unsqueeze(1).to_broadcast([P, 2, D]), ALU.add)
                i.then_inc(v_ok, 1)

            def x1_T(g):
                dve.wait_ge(x1T_ps, g + 1)
                dve.tensor_copy(x1T[:, 1, :], bank[6][:, :]).then_inc(x1T_dve, 1)

            def choose(g, par):
                dve.wait_ge(logit_ps, g + 1)
                at_least(dve, en_ok, g)
                dve.tensor_copy(logit[:, :, :].rearrange("p t e -> p (t e)"), bank[7][:, 0:NT * E]).then_inc(logit_ok, 1)
                wait_apart(dve, logit_ok, g + 1)
                for t in range(NT):
                    i = dve.max(top[:, t, :], logit[:, t, :])
                i.then_inc(top_ok, 1)
                wait_apart(dve, top_ok, g + 1)
                for t in range(NT):
                    i = dve.max_index(topi[:, t, :], top[:, t, :], logit[:, t, :])
                i.then_inc(topi_ok, 1)
                dve.wait_ge(topi_ok, g + 1)
                dve.tensor_copy(topf[:, :, :], topi[:, :, 0:TOP_K].rearrange("p t k -> p k t")).then_inc(topf_ok, 1)
                dve.wait_ge(topf_ok, g + 1)
                sel_g = sel[:, ds(g, 1), :, :].rearrange("p a j e -> p (a j) e")
                dve.tensor_tensor(sel_g,
                                  exp_sb[:, 0, :].unsqueeze(1).to_broadcast([P, TOP_K * NT, E]),
                                  topf[:, :, :].rearrange("p k t -> p (k t)").unsqueeze(2).to_broadcast([P, TOP_K * NT, E]),
                                  ALU.is_equal).then_inc(sel_ok, 1)
                dve.wait_ge(sel_ok, g + 1)
                at_least(dve, rank_ps, g)
                dve.tensor_tensor(chosen[:, :, :], sel_g[:, 0:NT, :], sel_g[:, NT:2 * NT, :], ALU.add).then_inc(chosen_ok, 1)

            def gates(g, par):
                dve.wait_ge(en_ok, g + 1)
                dve.tensor_scalar(en[:, :, :], en[:, :, :], 1.0, None, ALU.add).then_inc(en1_ok, 1)
                dve.wait_ge(en1_ok, g + 1)
                dve.reciprocal(x1row[par][:, :, D:ROW], en[:, :, :]).then_inc(gates_ok, 1)

            def place_rows(g, par):
                dve.wait_ge(rank_ps, g + 1)
                at_least(dve, place2_ok, g)
                dve.tensor_tensor(place[:, :, :], bank[7][:, 64:64 + NT * E].rearrange("p (t e) -> p t e", t=NT),
                                  count[:, :].unsqueeze(1).to_broadcast([P, NT, E]), ALU.add).then_inc(place_ok, 1)
                dve.wait_ge(place_ok, g + 1)
                dve.tensor_tensor(count[:, :], bank[7][:, 128:128 + E], count[:, :], ALU.add).then_inc(count_ok, 1)
                sel_g = sel[:, ds(g, 1), :, :].rearrange("p a j e -> p (a j) e")
                for k in range(TOP_K):
                    i = dve.tensor_tensor(place2[:, k, :, :], sel_g[:, k * NT:(k + 1) * NT, :], place[:, :, :], ALU.mult)
                i.then_inc(place2_ok, 1)
                dve.wait_ge(place2_ok, g + 1)
                slot_g = slot_f[:, ds(g, 1), :].rearrange("p a j -> p (a j)")
                dve.tensor_reduce(slot_g, place2[:, :, :, :].rearrange("p k t e -> p (k t) e"), AX.X, ALU.add)\
                   .then_inc(slotf_ok, 1)
                dve.wait_ge(slotf_ok, g + 1)
                dve.tensor_scalar(slot_i[:, par, :, :].rearrange("p k t -> p (k t)"), slot_g, 0.0, None,
                                  ALU.add).then_inc(slot_ok, 1)
                dve.wait_ge(count_ok, g + 1)

            def scores(g):
                wait_apart(dve, s_ps, g + 1)
                at_least(dve, pT_ps, g)
                for t in range(NT):
                    i = dve.tensor_tensor_reduce(s_sb[:, t, :], bank[2][:, t * P:(t + 1) * P], mask_sb[:, :], -1.0, BIG,
                                                 ALU.add, ALU.min, nmax[:, t:t + 1])
                i.then_inc(s_ok, 1)

            def stage(g, par, prev):
                dve.wait_ge(x_hi_ok, g + 1)
                for k in range(DC):
                    i = dve.tensor_tensor(xT_lo[:, k, :], bank[k][:, :], f32(xT_hi[:, k, :]), ALU.subtract)
                i.then_inc(x_lo_ok, 1)
                if prev == 2:
                    choose(g - 2, par)
                if prev:
                    dve.wait_ge(p_ok, g)
                    dve.reciprocal(rinv[:, :], rsum[:, :]).then_inc(rinv_ok, 1)
                if prev == 2:
                    place_rows(g - 2, par)
                    gates(g - 2, par)
                if prev:
                    attn_sum(g - 1, 1 - par)
                scores(g)
                if prev:
                    x1_T(g - 1)
                values(g)

            dve.tensor_copy(count[:, :], exp_sb[:, 1, :]).then_inc(start_ok, 1)
            dve.wait_ge(start_ok, 1)
            stage(0, 0, 0)
            stage(1, 1, 1)
            with dve.Fori(0, (GROUPS - 2) // 2) as i:
                for u in range(2):
                    stage(i * 2 + (2 + u), u, 2)
            last = GROUPS - 1
            dve.wait_ge(p_ok, GROUPS)
            dve.reciprocal(rinv[:, :], rsum[:, :]).then_inc(rinv_ok, 1)
            choose(last - 1, 0)
            place_rows(last - 1, 0)
            gates(last - 1, 0)
            attn_sum(last, 1)
            x1_T(last)
            choose(last, 1)
            place_rows(last, 1)
            gates(last, 1)

            steps = [0]

            def step(i):
                steps[0] += 1
                i.then_inc(t_step, 1)
                dve.wait_ge(t_step, steps[0])

            dve.wait_ge(t_iota, 3)
            step(dve.tensor_scalar(pad_f[:, :], count[:, :], partno[:, 0:1], None, ALU.add))
            dve.tensor_copy(pad_i[:, :], pad_f[:, :]).then_inc(t_pad, 1)
            step(dve.tensor_tensor(tiles_f[:, 0, 0:E], count[:, :], exp_sb[:, 1, :], ALU.subtract))
            step(dve.tensor_scalar(cnt_i[:, :], tiles_f[:, 0, 0:E], float(P - 1), None, ALU.add))
            step(dve.tensor_scalar(tiles_i[:, :], cnt_i[:, :], P.bit_length() - 1, None, ALU.logical_shift_right))
            step(dve.tensor_copy(hop[:, :], tiles_i[:, :]))
            end = [tiles_f[:, 0, 0:E], tiles_f[:, 1, 0:E]]
            step(dve.tensor_copy(end[0], hop[:, :]))
            n = 0
            s = 1
            while s < E:
                step(dve.tensor_copy(end[1 - n][:, 0:s], end[n][:, 0:s]))
                step(dve.tensor_tensor(end[1 - n][:, s:E], end[n][:, s:E], end[n][:, 0:E - s], ALU.add))
                n = 1 - n
                s *= 2
            ends = end[n]
            step(dve.tensor_tensor(base_d[:, :], ends, hop[:, :], ALU.subtract))
            step(dve.scalar_tensor_tensor(out=base_d[:, :], in0=base_d[:, :], scalar=float(P), in1=exp_sb[:, 1, :],
                                          op0=ALU.mult, op1=ALU.subtract))
            step(dve.memset(past[:, :, 0], 1.0))
            step(dve.tensor_tensor(past[:, :, 1:E + 1], tile_no[:, :].unsqueeze(2).to_broadcast([P, TILES, E]),
                                   ends.unsqueeze(1).to_broadcast([P, TILES, E]), ALU.is_ge))
            step(dve.tensor_tensor(onehot, past[:, :, 0:E], past[:, :, 1:E + 1], ALU.subtract))
            step(dve.tensor_reduce(tile_e, past[0:1, :, 1:E + 1], AX.X, ALU.add))
            step(dve.tensor_scalar(tile_ei, tile_e, float(E - 1), None, ALU.min))
            step(dve.tensor_scalar(hop[:, :], hop[:, :], -1.0, float(QBLOCKS), ALU.mult, ALU.add))
            step(dve.tensor_tensor(walk[0:1, :, :], past[0:1, :, 1:E + 1],
                                   hop[0:1, :].unsqueeze(1).to_broadcast([1, TILES, E]), ALU.mult))
            step(dve.tensor_reduce(tile_b, walk[0:1, :, :], AX.X, ALU.add))
            step(dve.tensor_tensor(tile_b, tile_b, tile_no[0:1, :], ALU.add))
            dve.tensor_scalar(tile_bi, tile_b, float(E * QBLOCKS), None, ALU.min).then_inc(tables_ok, 1)
            step(dve.tensor_tensor(ysel[:, :, :], sel[:, :, :, :].rearrange("p g j e -> p (g j) e"),
                                   base_d[:, :].unsqueeze(1).to_broadcast([P, GROUPS * TOP_K * NT, E]), ALU.mult))
            yslot = s_sb[:, 0, :]
            step(dve.tensor_reduce(yslot, ysel[:, :, :], AX.X, ALU.add))
            dve.tensor_tensor(yslot_i, yslot,
                              slot_f[:, :, :].rearrange("p g j -> p (g j)"), ALU.add).then_inc(yslot_ok, 1)

            def gate_of(t, r):
                dve.wait_ge(xs_in[r], 16 * (t // RING + 1) if isinstance(t, int) else (t - r) * (16 // RING) + 16)
                at_least(dve, gate_ok, t)
                dve.tensor_tensor(gate_j[:, :], xs[r][:, D:ROW], onehot[:, ds(t, 1), :].rearrange("p a e -> p (a e)"),
                                  ALU.mult).then_inc(gatej_ok, 1)
                dve.wait_ge(gatej_ok, t + 1)
                dve.tensor_reduce(gate[r % 2][:, 0:1], gate_j[:, :], AX.X, ALU.add).then_inc(gate_ok, 1)

            def rows_lo(t, r):
                dve.wait_ge(xs_hi_ok, t + 1)
                dve.tensor_tensor(xs_lo[r % 2][:, :, :].rearrange("p k c -> p (k c)"), bank[0][:, 0:D],
                                  f32(xs_hi[r % 2][:, :, :].rearrange("p k c -> p (k c)")), ALU.subtract)
                dve.tensor_copy(xs_b[r % 2][:, :, :].rearrange("p k c -> p (k c)"),
                                f32(xs_hi[r % 2][:, :, :].rearrange("p k c -> p (k c)"))).then_inc(xs_lo_ok, 1)

            def hidden_lo(t, r):
                dve.wait_ge(h_hi_ok, t + 1)
                dve.tensor_tensor(h_lo[:, :, :].rearrange("p c k -> p (c k)"), bank[3][:, :],
                                  f32(h_hi[:, :, :].rearrange("p c k -> p (c k)")), ALU.subtract).then_inc(h_lo_ok, 1)
                dve.tensor_copy(h_b.rearrange("p c k -> p (c k)"),
                                f32(h_hi[:, :, :].rearrange("p c k -> p (c k)"))).then_inc(h_b_ok, 1)

            def product(t, r):
                dve.wait_ge(act_ok, t + 1)
                dve.wait_ge(sw_ps, t + 1)
                dve.wait_ge(gate_ok, t + 1)
                at_least(dve, hT_ps, t)
                dve.scalar_tensor_tensor(out=h2, in0=bank[2][:, :], scalar=gate[r % 2][:, 0:1],
                                         in1=act2, op0=ALU.mult, op1=ALU.mult).then_inc(h_ok, 1)

            def tile(t, r, prev, ahead):
                if ahead:
                    gate_of(t + 1, (r + 1) % RING)
                    rows_lo(t + 1, (r + 1) % RING)
                if prev:
                    hidden_lo(t - 1, (r - 1) % RING)
                product(t, r)

            gate_of(0, 0)
            rows_lo(0, 0)
            for t in range(RING):
                tile(t, t, t > 0, True)
            with dve.Fori(1, TILES // RING - 1) as i:
                for r in range(RING):
                    tile(i * RING + r, r, True, True)
            for r in range(RING):
                tile(TILES - RING + r, r, True, r < RING - 1)
            hidden_lo(TILES - 1, RING - 1)

            def add_shared(g, par):
                dve.wait_ge(o_ps, g + 1)
                dve.wait_ge(z1_in[par], (g - par) * 8 + 16)
                at_least(dve, o_ok, g)
                for c in range(2):
                    i = dve.tensor_tensor(z_sb[:, 2 * c:2 * c + 2, :], bank[6 + c][:, :].rearrange("p (t d) -> p t d", t=2),
                                          z1[par][:, 2 * c:2 * c + 2, :], ALU.add)
                i.then_inc(za_ok, 1)

            def add_experts(g, par):
                dve.wait_ge(za_ok, g + 1)
                dve.wait_ge(pair_ok, g + 1)
                dve.tensor_tensor(z_sb[:, :, :], z_sb[:, :, :], yg[par][:, 0:NT, :], ALU.add).then_inc(zc_ok, 1)

            def stats_of_sum(g):
                dve.wait_ge(zc_ok, g + 3)
                norm_stats(1, g + 1, z_sb)

            def z1_lo_of(g):
                dve.wait_ge(z1_hi_ok, g + 1)
                for k in range(DC):
                    i = dve.tensor_tensor(z1_lo[:, k, :], bank[k][:, :], f32(z1_hi[:, k, :]), ALU.subtract)
                i.then_inc(z1_lo_ok, 1)

            def shared_product(g, c):
                dve.wait_ge(act3_ok, g * FC + (c + 1))
                dve.wait_ge(sw3_ps, g * FC + (c + 1))
                dve.tensor_tensor(h3[c % 2], bank[4 + c % 2][:, :], act3[c % 2], ALU.mult).then_inc(h3_ok, 1)

            def shared_lo_of(g, c):
                dve.wait_ge(h3_hi_ok, g * FC + (c + 1))
                dve.tensor_tensor(h3_lo[:, c, :], h3[c % 2], f32(h3_hi[:, c, :]), ALU.subtract).then_inc(h3_lo_ok, 1)

            def phase3(g, par, prev):
                z1_lo_of(g)
                if prev:
                    add_shared(g - 1, 1 - par)
                    add_experts(g - 1, 1 - par)
                for c in range(FC):
                    shared_product(g, c)
                    if prev and c == 0:
                        stats_of_sum(g - 1)
                    shared_lo_of(g, c)
                if prev:
                    norm_root(1, g)

            phase3(0, 0, False)
            phase3(1, 1, True)
            with dve.Fori(0, (GROUPS - 2) // 2) as i:
                for u in range(2):
                    phase3(i * 2 + (2 + u), u, True)
            add_shared(GROUPS - 1, 1)
            add_experts(GROUPS - 1, 1)
            stats_of_sum(GROUPS - 1)
            norm_root(1, GROUPS)


OUT_SHAPE = (16, 512, 256)


def kernel(L0_attn_x, L0_attn_Wq, L0_attn_bq, L0_attn_Wk, L0_attn_bk, L0_attn_Wv, L0_attn_bv, L0_ffn_router_DE,
           L0_ffn_w_in_shared_FD, L0_ffn_w_out_shared_DF, L0_ffn_w_swiglu_FD, L0_ffn_w_in_eDF, L0_ffn_w_swiglu_eDF,
           L0_ffn_w_out_eFD):
    import numpy as np
    import concourse.bacc as bacc
    from concourse.bass_utils import run_bass_kernel_spmd

    blocks = np.arange(P) // BLOCK
    feeds = {
        "x": L0_attn_x, "wqT": np.transpose(L0_attn_Wq), "wkT": np.transpose(L0_attn_Wk), "wvT": np.transpose(L0_attn_Wv),
        "bq": np.asarray(L0_attn_bq).reshape(DC, P).T, "bk": np.asarray(L0_attn_bk).reshape(DC, P).T, "bv": np.broadcast_to(np.asarray(L0_attn_bv)[None, :], (P, D)),
        "router": L0_ffn_router_DE, "w_in_shT": np.transpose(L0_ffn_w_in_shared_FD),
        "w_sw_shT": np.transpose(L0_ffn_w_swiglu_FD), "w_out_shT": np.transpose(L0_ffn_w_out_shared_DF),
        "w_in": L0_ffn_w_in_eDF, "w_sw": L0_ffn_w_swiglu_eDF, "w_out": L0_ffn_w_out_eFD,
        "ident": np.eye(P, dtype=np.float32),
        "mask": np.where(blocks[:, None] == blocks[None, :], 0.0, OFF_BLOCK).astype(np.float32),
        "tri": np.stack([np.triu(np.ones((P, P), np.float32), 1), np.ones((P, P), np.float32)], 1),
        "experts": np.broadcast_to(np.stack([np.arange(E), np.arange(E) * QROWS]).astype(np.float32)[None], (P, 2, E)),
    }
    nc = bacc.Bacc("TRN2", target_bir_lowering=False, num_devices=1)
    arrays, args = {}, {}
    for name, a in feeds.items():
        a = np.ascontiguousarray(a)
        arrays[f"in_{name}"] = a
        args[name] = nc.dram_tensor(f"in_{name}", a.shape, mybir.dt.from_np(a.dtype), kind="ExternalInput").ap()
    args["out"] = nc.dram_tensor("out_0", OUT_SHAPE, F32, kind="ExternalOutput").ap()
    build(nc, **args)
    return run_bass_kernel_spmd(nc, [arrays], core_ids=[0]).results[0]["out_0"]
```

```python
from contextlib import ExitStack

import concourse.bass as bass
from concourse import mybir
from concourse.bass import IndirectOffsetOnAxis, ds

ALU = mybir.AluOpType
ACT = mybir.ActivationFunctionType
AX = mybir.AxisListType
F32 = mybir.dt.float32
F32R = mybir.dt.float32r
BF16 = mybir.dt.bfloat16
I32 = mybir.dt.int32
U32 = mybir.dt.uint32

P = 128
D = 256
DC = D // P
F = 512
FC = F // P
HALF = 3 * F
E = 8
TOP_K = 2
TOKENS = 16 * 512
BLOCK = 32
HALVES = 2 * E
NT = 4
GROUP = NT * P
GROUPS = TOKENS // GROUP
TILES = (TOP_K * TOKENS + E * (P - 1)) // P
QBLOCKS = TOKENS // P + 1
QROWS = QBLOCKS * P
ROW = D + E
RING = 4
TAIL = (TILES - 1) // RING * RING
EPS = 1e-5
OFF_BLOCK = -1e30
BIG = 3e38
RSQRT_MAGIC = 0x5F3759DF
NEWTON = 3


def at_least(eng, sem, n):
    if not isinstance(n, int) or n > 0:
        eng.wait_ge(sem, n)


def build(nc, x, wqT, wkT, wvT, bq, bk, bv, router, w_in_shT, w_sw_shT, w_out_shT, w_in, w_sw, w_out,
          ident, mask, tri, experts, out):
    with ExitStack() as ctx:
        ends = {}

        def sb(name, shape, dt=F32):
            a = ctx.enter_context(nc.sbuf_tensor(name, shape, dt))
            ends[name] = nc.sbuf_base
            return a

        def over(name, owner, shape, last, dt=F32R):
            size = 4
            for n in shape[1:]:
                size *= n
            return nc.alloc_sbuf_tensor_at(name, shape, dtype=dt, offset=ends[owner] - 4 * last - size)

        def sem(name):
            return ctx.enter_context(nc.semaphore(name))

        bank = [ctx.enter_context(nc.psum_tensor(f"bank{i}", [P, 512], F32)) for i in range(8)]

        w_hi = sb("w_hi", [P, HALVES, HALF], F32R)
        w_lo = sb("w_lo", [P, HALVES, HALF], BF16)
        w_raw = over("w_raw", "w_hi", [P, HALF], 0, F32)
        w_qkv_hi = sb("w_qkv_hi", [P, 3 * DC, D], F32R)
        w_qkv_lo = sb("w_qkv_lo", [P, 3 * DC, D], F32R)
        bq_sb = sb("bq_sb", [P, DC])
        bk_sb = sb("bk_sb", [P, DC])
        bv_sb = sb("bv_sb", [P, D])
        router_sb = sb("router_sb", [P, DC, E])
        ident_sb = sb("ident_sb", [P, P])
        mask_sb = sb("mask_sb", [P, P])
        trib = sb("trib", [P, 2, P], BF16)
        exp_sb = sb("exp_sb", [P, 2, E])

        x_rows = sb("x_rows", [P, 2, NT, D])
        x_sb = [x_rows[:, i, :, :] for i in range(2)]
        xT_hi = sb("xT_hi", [P, DC, GROUP], F32R)
        xT_lo = sb("xT_lo", [P, DC, GROUP], F32R)
        w_raw_last = over("w_raw_last", "xT_lo", [P, HALF], 0, F32)
        qT = sb("qT", [P, DC, GROUP])
        keys_values = sb("keys_values", [P, 2 * NT * D])
        kT = keys_values[:, 0:DC * GROUP].rearrange("p (k n) -> p k n", k=DC)
        v_sb = keys_values[:, NT * D:2 * NT * D].rearrange("p (t d) -> p t d", t=NT)
        x1T = kT
        s_sb = sb("s_sb", [P, NT, P])
        p_sb = s_sb
        nmax = sb("nmax", [P, NT])
        rsum = sb("rsum", [P, NT])
        rinv = sb("rinv", [P, NT])
        pT = sb("pT", [P, NT, P])
        x1row = [sb(f"x1row{i}", [P, NT, ROW]) for i in range(2)]
        tri_sb = x1row[0][:, 0, 0:2 * P].rearrange("p (a c) -> p a c", a=2)
        logit = sb("logit", [P, NT, E])
        en = sb("en", [P, NT, E])
        top = sb("top", [P, NT, 8])
        topi = sb("topi", [P, NT, 8], U32)
        topf = sb("topf", [P, TOP_K, NT])
        chosen = sb("chosen", [P, NT, E], BF16)
        count = sb("count", [P, E])
        place = sb("place", [P, NT, E])
        place2 = sb("place2", [P, TOP_K, NT, E])
        slot_i = sb("slot_i", [P, 2, TOP_K, NT], I32)
        sel = sb("sel", [P, GROUPS, TOP_K * NT, E], BF16)
        slot_f = sb("slot_f", [P, GROUPS, TOP_K * NT])

        stats = sb("stats", [P, NT, 6])
        mv = sb("mv", [P, NT, 2])
        veps = sb("veps", [P, NT])
        halfi = sb("halfi", [P, NT], I32)
        rs = sb("rs", [P, NT])
        rs_a = sb("rs_a", [P, NT])
        rs_b = sb("rs_b", [P, NT])
        shift = sb("shift", [P, NT])

        cnt_i = sb("cnt_i", [P, E], I32)
        tiles_i = sb("tiles_i", [P, E], I32)
        tiles_f = sb("tiles_f", [P, 2, E])
        end_i = sb("end_i", [P, E], I32)
        zero_row = sb("zero_row", [P, ROW])
        tile_no = sb("tile_no", [P, TILES])
        spare = x_rows[:, :, :, :].rearrange("p i t d -> p (i t d)")
        past = spare[:, 0:TILES * (E + 1)].rearrange("p (t e) -> p t e", t=TILES)
        q_place = qT[:, :, :].rearrange("p k n -> p (k n)")
        onehot = q_place[:, 0:TILES * E // 2].bitcast(BF16).rearrange("p (t e) -> p t e", t=TILES)
        hop = sb("hop", [P, E])
        walk = keys_values[:, 0:TILES * E].rearrange("p (t e) -> p t e", t=TILES)
        tile_e = spare[0:1, TILES * (E + 1):TILES * (E + 2)]
        tile_b = spare[0:1, TILES * (E + 2):TILES * (E + 3)]
        tile_ei = pT[0:1, 2:4, :].rearrange("p a b -> p (a b)")[:, 0:TILES].bitcast(I32)
        tile_bi = tile_no[0:1, :].bitcast(I32)
        base_d = sb("base_d", [P, E])
        ysel = keys_values[:, 0:GROUPS * TOP_K * NT * E].rearrange("p (j e) -> p j e", e=E)
        group_slots = [sb(f"group_slots{i}", [P, TOP_K * NT], I32) for i in range(2)]
        yslot_i = q_place[:, TILES * E // 2 + 2 * P:TILES * E // 2 + 2 * P + GROUPS * TOP_K * NT].bitcast(I32)

        def flat(a):
            return a.rearrange("p a b -> p (a b)")

        def f32(a):
            return a.bitcast(F32)

        xs = [x1row[0][:, i, :] for i in range(RING)]
        y2 = [x1row[1][:, i, 0:D] for i in range(RING)]
        xs_hi = [xT_hi[:, i, 0:D].rearrange("p (k c) -> p k c", k=DC) for i in range(2)]
        xs_lo = [xT_hi[:, i, D:2 * D].rearrange("p (k c) -> p k c", k=DC) for i in range(2)]
        xs_b = [q_place[:, TILES * E // 2 + i * P:TILES * E // 2 + (i + 1) * P].bitcast(BF16)
                .rearrange("p (k c) -> p k c", k=DC) for i in range(2)]
        h_hi = over("h_hi", "x_rows", [P, FC, P], 0)
        h_lo = over("h_lo", "x_rows", [P, FC, P], F)
        h_b = flat(pT[:, 0:2, :]).bitcast(BF16).rearrange("p (c k) -> p c k", c=FC)
        gate = [sb(f"gate{i}", [P, 1]) for i in range(2)]
        gate_j = sb("gate_j", [P, E])
        act2 = over("act2", "xT_lo", [P, F], 0, F32)[:, :]
        h2 = over("h2", "xT_lo", [P, F], F, F32)[:, :]
        shared_raw = s_sb[:, :, :].rearrange("p t k -> p (t k)")

        queues = nc.dram_tensor("queues", [E * QROWS + P, ROW], F32, kind="Internal").ap()
        x1_dram = nc.dram_tensor("x1_dram", [TOKENS, D], F32, kind="Internal").ap()
        y_dram = nc.dram_tensor("y_dram", [TILES * P, D], F32, kind="Internal").ap()

        x_g = x.rearrange("b s d -> (b s) d").rearrange("(g t p) d -> g p t d", g=GROUPS, t=NT)
        x1_g = x1_dram.rearrange("(g t p) d -> g p t d", g=GROUPS, t=NT)
        out_g = out.rearrange("b s d -> (b s) d").rearrange("(g t p) d -> g p t d", g=GROUPS, t=NT)
        wi_g = w_in.rearrange("e (k p) f -> p (e k) f", k=DC)
        ws_g = w_sw.rearrange("e (k p) f -> p (e k) f", k=DC)
        wo_g = w_out.rearrange("e (h c p) d -> p (e h) c d", h=2, c=FC // 2)

        z1 = [rows[:, :, 0:D] for rows in x1row]
        def take(place, used, n, d):
            first = used[0]
            used[0] += n * d
            return place[:, first:first + n * d].rearrange("p (n d) -> p n d", d=d)

        hi_place, hi_used = flat(w_hi[:, :, :]), [0]
        z1_hi = take(hi_place, hi_used, DC, GROUP)
        z1_lo = take(hi_place, hi_used, DC, GROUP)
        h3_hi = take(hi_place, hi_used, FC, GROUP)
        h3_lo = take(hi_place, hi_used, FC, GROUP)
        lo_place, lo_used = flat(w_lo[:, :, :]).bitcast(F32), [0]
        yg = [take(lo_place, lo_used, TOP_K * NT, D) for _ in range(2)]
        z_sb = take(lo_place, lo_used, NT, D)
        o_sb = take(lo_place, lo_used, NT, D)
        act3 = [take(lo_place, lo_used, 1, GROUP)[:, 0, :] for _ in range(2)]
        h3 = [take(lo_place, lo_used, 1, GROUP)[:, 0, :] for _ in range(2)]
        shared_hi = [over("shi_hi", "keys_values", [P, DC, F], 0), over("shs_hi", "w_qkv_lo", [P, DC, F], 0),
                     over("sho_hi", "w_qkv_lo", [P, FC, D], 2 * DC * F)]
        shared_lo = [over("shi_lo", "keys_values", [P, DC, F], DC * F), over("shs_lo", "w_qkv_lo", [P, DC, F], DC * F),
                     over("sho_lo", "x_rows", [P, FC, D], FC * D)]

        const_in = sem("const_in")
        ident_in = sem("ident_in")
        attn_in = [sem(f"attn_in{i}") for i in range(3)]
        x_in = [sem(f"x_in{i}") for i in range(2)]
        expert_in = sem("expert_in")
        w_hi_ok = sem("w_hi_ok")
        w_lo_ok = sem("w_lo_ok")
        shared_in = sem("shared_in")
        shared_hi_ok = sem("shared_hi_ok")
        shared_lo_ok = sem("shared_lo_ok")
        tri_ok = sem("tri_ok")
        start_ok = sem("start_ok")
        xT_ps = sem("xT_ps")
        qkv_hi_ok = sem("qkv_hi_ok")
        qkv_lo_ok = sem("qkv_lo_ok")
        x_bias_ok = sem("x_bias_ok")
        x_hi_ok = sem("x_hi_ok")
        x_lo_ok = sem("x_lo_ok")
        q_ps = sem("q_ps")
        q_ok = sem("q_ok")
        k_ps = sem("k_ps")
        k_ok = sem("k_ok")
        v_ps = sem("v_ps")
        v_ok = sem("v_ok")
        s_ps = sem("s_ps")
        s_ok = sem("s_ok")
        p_ok = sem("p_ok")
        pT_ps = sem("pT_ps")
        pT_ok = sem("pT_ok")
        rinv_ok = sem("rinv_ok")
        pv_ps = sem("pv_ps")
        y_ok = sem("y_ok")
        stats_ok = [sem(f"stats_ok{i}") for i in range(2)]
        mv_ok = [sem(f"mv_ok{i}") for i in range(2)]
        veps_ok = [sem(f"veps_ok{i}") for i in range(2)]
        half_ok = [sem(f"half_ok{i}") for i in range(2)]
        rs_ok = [[sem(f"rs_ok{j}_{i}") for i in range(NEWTON + 1)] for j in range(2)]
        rsa_ok = [[sem(f"rsa_ok{j}_{i}") for i in range(NEWTON)] for j in range(2)]
        rsb_ok = [[sem(f"rsb_ok{j}_{i}") for i in range(NEWTON)] for j in range(2)]
        shift_ok = [sem(f"shift_ok{i}") for i in range(2)]
        x1_act = sem("x1_act")
        x1_dve = sem("x1_dve")
        x1T_ps = sem("x1T_ps")
        x1T_act = sem("x1T_act")
        x1T_dve = sem("x1T_dve")
        logit_ps = sem("logit_ps")
        logit_ok = sem("logit_ok")
        en_ok = sem("en_ok")
        en1_ok = sem("en1_ok")
        gates_ok = sem("gates_ok")
        top_ok = sem("top_ok")
        topi_ok = sem("topi_ok")
        topf_ok = sem("topf_ok")
        sel_ok = sem("sel_ok")
        chosen_ok = sem("chosen_ok")
        rank_ps = sem("rank_ps")
        place_ok = sem("place_ok")
        count_ok = sem("count_ok")
        place2_ok = sem("place2_ok")
        slotf_ok = sem("slotf_ok")
        slot_ok = sem("slot_ok")
        scattered = [sem(f"scattered{i}") for i in range(2)]
        x1_stored = [sem(f"x1_stored{i}") for i in range(2)]
        t_iota = sem("t_iota")
        t_step = sem("t_step")
        t_pad = sem("t_pad")
        padded = sem("padded")
        idle_padded = sem("idle_padded")
        tables_ok = sem("tables_ok")
        yslot_ok = sem("yslot_ok")
        xs_in = [sem(f"xs_in{i}") for i in range(RING)]
        xsT_ps = sem("xsT_ps")
        xs_hi_ok = sem("xs_hi_ok")
        xs_lo_ok = sem("xs_lo_ok")
        gatej_ok = sem("gatej_ok")
        gate_ok = sem("gate_ok")
        mid_ps = sem("mid_ps")
        act_ok = sem("act_ok")
        sw_ps = sem("sw_ps")
        h_ok = sem("h_ok")
        hT_ps = sem("hT_ps")
        h_hi_ok = sem("h_hi_ok")
        h_lo_ok = sem("h_lo_ok")
        h_b_ok = sem("h_b_ok")
        y_ps = sem("y_ps")
        y2_ok = sem("y2_ok")
        y_stored = [sem(f"y_stored{i}") for i in range(RING)]
        z1_in = [sem(f"z1_in{i}") for i in range(2)]
        z1T_ps = sem("z1T_ps")
        z1_hi_ok = sem("z1_hi_ok")
        z1_lo_ok = sem("z1_lo_ok")
        mid3_ps = sem("mid3_ps")
        sw3_ps = sem("sw3_ps")
        act3_ok = sem("act3_ok")
        h3_ok = sem("h3_ok")
        h3_hi_ok = sem("h3_hi_ok")
        h3_lo_ok = sem("h3_lo_ok")
        o_ps = sem("o_ps")
        gathered = [sem(f"gathered{i}") for i in range(2)]
        slots_here = sem("slots_here")
        summed_ok = sem("summed_ok")
        pair_ok = sem("pair_ok")
        added_ok = sem("added_ok")
        o_ok = sem("o_ok")
        o_stored = sem("o_stored")
        o_half_ok = sem("o_half_ok")

        block = ctx.enter_context(nc.Block())

        def wait_apart(eng, sem_, n):
            n = n if isinstance(n, int) else eng.snap(n)
            eng.wait_ge(ident_in, 16)
            at_least(eng, sem_, n)

        def groups(eng, body, ahead):
            for g in range(ahead):
                body(g, g % 2)
            pairs = (GROUPS - ahead) // 2
            with eng.Fori(0, pairs) as i:
                for u in range(2):
                    body(i * 2 + (ahead + u), (ahead + u) % 2)
            for g in range(ahead + 2 * pairs, GROUPS):
                body(g, g % 2)

        def stages(eng, stage):
            stage(0, 0, 0, True)
            stage(1, 1, 1, True)
            for u in range(2):
                stage(2 + u, u, 2, True)
            with eng.Fori(0, (GROUPS - 6) // 2) as i:
                for u in range(2):
                    stage(i * 2 + (4 + u), u, 2, True)
            stage(GROUPS - 2, 0, 2, True)
            stage(GROUPS - 1, 1, 2, False)

        @block.sync
        def _(sp):
            sp.dma_start(ident_sb[:, :], ident).then_inc(ident_in, 16)
            sp.dma_start(x_sb[0], x_g[0]).then_inc(x_in[0], 16)
            for i, src in enumerate((wqT, wkT, wvT)):
                sp.dma_start(w_raw[:, i * DC * D:(i + 1) * DC * D].rearrange("p (k e) -> p k e", k=DC),
                             src.rearrange("(k p) e -> p k e", p=P)).then_inc(attn_in[i], 16)
            sp.dma_start(x_sb[1], x_g[1]).then_inc(x_in[1], 16)
            sp.dma_start(bq_sb[:, :], bq).then_inc(const_in, 16)
            sp.dma_start(bk_sb[:, :], bk).then_inc(const_in, 16)
            sp.dma_start(bv_sb[:, :], bv).then_inc(const_in, 16)
            sp.dma_start(router_sb[:, :, :], router.rearrange("(k p) e -> p k e", p=P)).then_inc(const_in, 16)
            sp.dma_start(mask_sb[:, :], mask).then_inc(const_in, 16)
            sp.dma_start(tri_sb, tri).then_inc(const_in, 16)
            sp.dma_start(exp_sb[:, :, :], experts).then_inc(const_in, 16)

            def phase1(g, par):
                if not (isinstance(g, int) and g < 2):
                    store_x1(g - 2, par)
                if not (isinstance(g, int) and g == 0):
                    if not (isinstance(g, int) and g + 1 == GROUPS):
                        sp.wait_ge(y_ok, g)
                        sp.dma_start(x_sb[1 - par], x_g[g + 1] if isinstance(g, int) else x_g[ds(g + 1, 1)].rearrange("a p t d -> p (a t) d"))\
                          .then_inc(x_in[1 - par], 16)
                    load_half(g - 1, w_raw)

            def load_half(g, raw):
                at_least(sp, w_lo_ok, g)
                for i, src in enumerate((wi_g, ws_g)):
                    sp.dma_start(raw[:, i * F:(i + 1) * F], src[:, ds(g, 1), :].rearrange("p a f -> p (a f)")).then_inc(expert_in, 16)
                sp.dma_start(raw[:, 2 * F:3 * F].rearrange("p (c d) -> p c d", d=D),
                             wo_g[:, ds(g, 1), :, :].rearrange("p a c d -> p (a c) d")).then_inc(expert_in, 16)

            def store_x1(g, par):
                sp.wait_ge(x1_act, g + 1)
                sp.wait_ge(x1_dve, g + 1)
                dst = x1_g[g] if isinstance(g, int) else x1_g[ds(g, 1)].rearrange("a p t d -> p (a t) d")
                sp.dma_start(dst, x1row[par][:, :, 0:D]).then_inc(x1_stored[par], 16)

            sp.wait_ge(qkv_lo_ok, 3)
            phase1(0, 0)
            phase1(1, 1)
            with sp.Fori(0, (GROUPS - 4) // 2) as i:
                for u in range(2):
                    phase1(i * 2 + (2 + u), u)
            phase1(GROUPS - 2, 0)
            phase1(GROUPS - 1, 1)
            store_x1(GROUPS - 2, 0)
            sp.wait_ge(v_ps, GROUPS)
            load_half(GROUPS - 1, w_raw_last)
            store_x1(GROUPS - 1, 1)

            sp.wait_ge(t_iota, 2)
            sp.dma_start(queues[E * QROWS:E * QROWS + P, :], zero_row[:, :]).then_inc(idle_padded, 16)
            sp.wait_ge(t_pad, 1)
            for e in range(E):
                end = sp.value_load(end_i[0:1, e:e + 1], min_val=e * QROWS, max_val=e * QROWS + TOKENS)
                sp.dma_start(queues[ds(end, P), :], zero_row[:, :]).then_inc(padded, 16)
            for s in range(2):
                sp.wait_ge(scattered[s], 16 * TOP_K * NT * GROUPS // 2)
            sp.wait_ge(padded, 16 * E)
            sp.wait_ge(idle_padded, 16)
            sp.wait_ge(tables_ok, 1)
            for s in range(2):
                sp.wait_ge(x1_stored[s], 16 * GROUPS // 2)

            def load_xs(t, r):
                if not (isinstance(t, int) and t < RING):
                    sp.wait_ge(xsT_ps, t - RING + 1)
                    sp.wait_ge(gate_ok, t - RING + 1)
                b = sp.value_load(tile_bi[0:1, ds(t, 1)], min_val=0, max_val=E * QBLOCKS)
                sp.dma_start(xs[r], queues[ds(b * P, P), :]).then_inc(xs_in[r], 16)

            def store_y(t, r):
                sp.wait_ge(y2_ok, t + 1)
                sp.dma_start(y_dram[ds(t * P, P), :], y2[r]).then_inc(y_stored[r], 16)

            for t in range(RING):
                load_xs(t, t)
            with sp.Fori(0, TAIL // RING - 1) as i:
                for r in range(RING):
                    load_xs(i * RING + (r + RING), r)
                    store_y(i * RING + r, r)
            for t in range(TAIL, TILES):
                load_xs(t, t % RING)
                store_y(t - RING, t % RING)
            for t in range(TILES - RING, TILES - 1):
                store_y(t, t % RING)

            def z_load(g, par):
                if not isinstance(g, int) or g >= 2:
                    sp.wait_ge(z1T_ps, g - 1)
                    sp.wait_ge(summed_ok, g - 1)
                src = x1_g[g] if isinstance(g, int) else x1_g[ds(g, 1)].rearrange("a p t d -> p (a t) d")
                sp.dma_start(z1[par], src).then_inc(z1_in[par], 16)

            def z_store(g):
                sp.wait_ge(o_ok, g + 1)
                dst = out_g[g] if isinstance(g, int) else out_g[ds(g, 1)].rearrange("a p t d -> p (a t) d")
                sp.dma_start(dst, o_sb[:, :, :]).then_inc(o_stored, 16)

            def phase3(g, par):
                z_load(g, par)
                if not isinstance(g, int) or g >= 2:
                    z_store(g - 2)

            sp.wait_ge(xsT_ps, TILES)
            sp.wait_ge(gate_ok, TILES)
            phase3(0, 0)
            store_y(TILES - 1, (TILES - 1) % RING)
            for r in range(RING):
                sp.wait_ge(y_stored[r], 16 * len(range(r, TILES, RING)))
            phase3(1, 1)
            with sp.Fori(0, (GROUPS - 2) // 2) as i:
                for u in range(2):
                    phase3(i * 2 + (2 + u), u)
            z_store(GROUPS - 2)
            for half, ok in ((slice(NT // 2, NT), (o_half_ok, 1)), (slice(0, NT // 2), (o_ok, GROUPS))):
                sp.wait_ge(*ok)
                sp.dma_start(out_g[GROUPS - 1][:, half, :], o_sb[:, half, :]).then_inc(o_stored, 16)
            sp.wait_ge(o_stored, 16 * (GROUPS + 1))

        @block.gpsimd
        def _(pool):
            pool.memset(zero_row[:, :], 0.0).then_inc(t_iota, 1)
            pool.iota(tile_no[:, :], pattern=[[1, TILES]], base=0, channel_multiplier=0,
                      allow_small_or_imprecise_dtypes=True).then_inc(t_iota, 1)
            pool.wait_ge(const_in, 16 * 7)

            def scatter(g, par):
                wait_apart(pool, gates_ok, g + 1)
                for k in range(TOP_K):
                    for t in range(NT):
                        pool.indirect_dma_start(
                            out=queues, out_offset=IndirectOffsetOnAxis(ap=slot_i[:, par, k, t:t + 1], axis=0),
                            in_=x1row[par][:, t, :], in_offset=None).then_inc(scattered[par], 16)

            def split_expert(g, raw=w_raw):
                pool.wait_ge(w_hi_ok, g + 1)
                pool.tensor_tensor(w_lo[:, ds(g, 1), :].rearrange("p a n -> p (a n)"), raw[:, :],
                                   f32(w_hi[:, ds(g, 1), :].rearrange("p a n -> p (a n)")), ALU.subtract).then_inc(w_lo_ok, 1)

            def add_bias(g, par):
                pool.wait_ge(xT_ps, g * DC + DC)
                pool.tensor_tensor(x_sb[par], x_sb[par], bv_sb[:, :].unsqueeze(1).to_broadcast([P, NT, D]),
                                   ALU.add).then_inc(x_bias_ok, 1)

            def phase1(g, par):
                add_bias(g, par)
                if not (isinstance(g, int) and g < 2):
                    split_expert(g - 2)
                    scatter(g - 2, par)

            groups(pool, phase1, 2)
            split_expert(GROUPS - 2)
            scatter(GROUPS - 2, 0)
            scatter(GROUPS - 1, 1)

            split_expert(GROUPS - 1, w_raw_last)

            pool.wait_ge(yslot_ok, 1)
            n = 0
            for m, src in enumerate((w_in_shT, w_sw_shT, w_out_shT)):
                k = src.shape[0] // P
                for half in range(2):
                    c = slice(half * k // 2, (half + 1) * k // 2)
                    rows = shared_raw.rearrange("p (k n) -> p k n", k=k // 2)
                    if n > 0:
                        pool.wait_ge(shared_lo_ok, n)
                    pool.dma_start(rows,
                                   src.rearrange("(h k p) n -> h p k n", h=2, p=P)[half]).then_inc(shared_in, 16)
                    n += 1
                    pool.wait_ge(shared_in, 16 * n)
                    pool.tensor_copy(shared_hi[m][:, c, :], rows).then_inc(shared_hi_ok, 1)
                    pool.wait_ge(shared_hi_ok, n)
                    pool.tensor_tensor(shared_lo[m][:, c, :], rows, f32(shared_hi[m][:, c, :]), ALU.subtract).then_inc(shared_lo_ok, 1)

            for r in range(RING):
                pool.wait_ge(y_stored[r], 16 * len(range(r, TILES, RING)))

            def gather(g, par):
                pool.wait_ge(added_ok, g + 1)
                pool.tensor_copy(group_slots[par][:, :], yslot_i[:, ds(g * (TOP_K * NT), TOP_K * NT)]).then_inc(slots_here, 1)
                wait_apart(pool, slots_here, g + 1)
                for j in range(TOP_K * NT):
                    ix = group_slots[par][:, j:j + 1]
                    pool.indirect_dma_start(
                        out=yg[par][:, j, :], out_offset=None, in_=y_dram,
                        in_offset=IndirectOffsetOnAxis(ap=ix, axis=0)).then_inc(gathered[par], 16)

            def pair(g, par):
                if isinstance(g, int):
                    pool.wait_ge(gathered[par], 16 * TOP_K * NT * (g // 2 + 1))
                else:
                    pool.wait_ge(gathered[par], (g - par) * (8 * TOP_K * NT) + 16 * TOP_K * NT)
                pool.tensor_tensor(yg[par][:, 0:NT, :], yg[par][:, 0:NT, :], yg[par][:, NT:2 * NT, :], ALU.add).then_inc(pair_ok, 1)

            def gather_and_pair(g, par):
                gather(g, par)
                if not (isinstance(g, int) and g == 0):
                    pair(g - 1, 1 - par)

            groups(pool, gather_and_pair, 2)
            pair(GROUPS - 1, 1)

        @block.tensor
        def _(pe):
            def chunk_transposes(rows, dst, k):
                for t in range(NT):
                    mm = pe.transpose(dst[:, t * P:(t + 1) * P], rows[:, t, k * P:(k + 1) * P], ident_sb[:, :])
                return mm

            def project(w, dst, c, sig, w_ready):
                if w_ready:
                    pe.wait_ge(qkv_lo_ok, w + 1)
                for n, (wp, rows) in enumerate(((w_qkv_hi, xT_hi), (w_qkv_lo, xT_hi), (w_qkv_hi, xT_lo))):
                    for k in range(DC):
                        mm = pe.matmul(dst[:, :], wp[:, w * DC + k, c * P:(c + 1) * P], rows[:, k, :],
                                       start=(n == 0 and k == 0), stop=(n == 2 and k == DC - 1))
                mm.then_inc(sig, 1)

            def probs_T(g):
                pe.wait_ge(p_ok, g + 1)
                for t in range(NT):
                    mm = pe.transpose(bank[2][:, t * P:(t + 1) * P], p_sb[:, t, :], ident_sb[:, :])
                mm.then_inc(pT_ps, 1)

            def probs_v(g):
                pe.wait_ge(pT_ok, g + 1)
                pe.wait_ge(v_ok, g + 1)
                for t in range(NT):
                    mm = pe.matmul(bank[5 + t // 2][:, (t % 2) * D:(t % 2 + 1) * D], pT[:, t, :], v_sb[:, t, :],
                                   start=True, stop=True)
                    if t % 2:
                        mm.then_inc(pv_ps, 1)

            def x1_T(g, par):
                pe.wait_ge(x1_act, g + 1)
                pe.wait_ge(x1_dve, g + 1)
                for k in range(DC):
                    mm = chunk_transposes(x1row[par], bank[5 + k], k)
                mm.then_inc(x1T_ps, 1)

            def logits(g):
                pe.wait_ge(x1T_act, g + 1)
                pe.wait_ge(x1T_dve, g + 1)
                for t in range(NT):
                    for k in range(DC):
                        mm = pe.matmul(bank[7][:, t * E:(t + 1) * E], x1T[:, k, t * P:(t + 1) * P], router_sb[:, k, :],
                                       start=(k == 0), stop=(k == DC - 1))
                mm.then_inc(logit_ps, 1)

            def ranks(g):
                pe.wait_ge(chosen_ok, g + 1)
                ch = chosen[:, :, :].rearrange("p t e -> p (t e)")
                rk = bank[7][:, 64:64 + NT * E]
                pe.matmul(rk, trib[:, 0, :], ch, start=True, stop=False, skip_group_check=True)
                for s in range(1, NT):
                    pe.matmul(bank[7][:, 64 + s * E:64 + NT * E], trib[:, 1, :], ch[:, 0:(NT - s) * E],
                              start=False, stop=(s == NT - 1), skip_group_check=True)
                for t in range(NT):
                    mm = pe.matmul(bank[7][:, 128:128 + E], trib[:, 1, :], ch[:, t * E:(t + 1) * E],
                                   start=(t == 0), stop=(t == NT - 1), skip_group_check=True)
                mm.then_inc(rank_ps, 1)

            def stage(g, par, prev, more):
                if prev == 1:
                    pe.wait_ge(const_in, 16 * 7)
                    pe.wait_ge(tri_ok, 1)
                if prev == 2:
                    logits(g - 2)
                pe.wait_ge(x_lo_ok, g + 1)
                at_least(pe, v_ok, g)
                project(0, bank[3], 0, q_ps, not prev)
                if prev:
                    probs_T(g - 1)
                project(0, bank[4], 1, q_ps, not prev)
                if prev == 2:
                    ranks(g - 2)
                if prev:
                    probs_v(g - 1)
                project(1, bank[0], 0, k_ps, not prev)
                project(1, bank[1], 1, k_ps, not prev)
                pe.wait_ge(q_ok, g + 1)
                if not prev:
                    pe.wait_ge(qkv_lo_ok, 3)
                for t in range(NT):
                    for n, (rows, w) in enumerate(((xT_hi, w_qkv_hi), (xT_hi, w_qkv_lo), (xT_lo, w_qkv_hi))):
                        for k in range(DC):
                            mm = pe.matmul(bank[3 + t // 2][:, (t % 2) * D:(t % 2 + 1) * D], rows[:, k, t * P:(t + 1) * P],
                                           w[:, 2 * DC + k, :], start=(n == 0 and k == 0), stop=(n == 2 and k == DC - 1))
                mm.then_inc(v_ps, 1)
                pe.wait_ge(k_ok, g + 1)
                at_least(pe, pT_ok, g)
                for t in range(NT):
                    for k in range(DC):
                        c = slice(t * P, (t + 1) * P)
                        mm = pe.matmul(bank[2][:, c], qT[:, k, c], kT[:, k, c], start=(k == 0), stop=(k == DC - 1))
                mm.then_inc(s_ps, 1)
                if more:
                    x_T(g + 1, 1 - par, 0)
                if prev:
                    x1_T(g - 1, 1 - par)
                if more:
                    x_T(g + 1, 1 - par, 1)

            def x_T(g, par, k):
                pe.wait_ge(x_in[par], (g - par) * 8 + 16)
                chunk_transposes(x_sb[par], bank[k], k).then_inc(xT_ps, 1)

            pe.wait_ge(ident_in, 16)
            x_T(0, 0, 0)
            x_T(0, 0, 1)
            stages(pe, stage)
            last = GROUPS - 1
            logits(last - 1)
            probs_T(last)
            probs_v(last)
            ranks(last - 1)
            x1_T(last, last % 2)
            logits(last)
            ranks(last)

            pe.wait_ge(count_ok, GROUPS)
            pe.wait_ge(place_ok, GROUPS)
            pe.wait_ge(w_lo_ok, GROUPS)
            pe.wait_ge(tables_ok, 1)

            def xs_T(t, r):
                pe.wait_ge(xs_in[r], 16 * (t // RING + 1) if isinstance(t, int) else (t - r) * (16 // RING) + 16)
                at_least(pe, xs_lo_ok, t)
                for k in range(DC):
                    mm = pe.transpose(bank[0][:, k * P:(k + 1) * P], xs[r][:, k * P:(k + 1) * P], ident_sb[:, :])
                mm.then_inc(xsT_ps, 1)

            def hidden(t, r, first, dst, e, sig, free):
                at_least(pe, free, t)
                for n, (rows, w) in enumerate(((xs_hi, w_hi_e), (xs_lo, w_hi_e), (xs_b, w_lo_e))):
                    for k in range(DC):
                        c = k * HALF + first
                        mm = pe.matmul(dst[:, :], rows[r % 2][:, k, :], w[:, ds(e, 1), c:c + F].rearrange("p a f -> p (a f)"),
                                       start=(n == 0 and k == 0), stop=(n == 2 and k == DC - 1))
                mm.then_inc(sig, 1)

            def h_T(t):
                pe.wait_ge(h_ok, t + 1)
                at_least(pe, h_lo_ok, t)
                for c in range(FC):
                    mm = pe.transpose(bank[3][:, c * P:(c + 1) * P], h2[:, c * P:(c + 1) * P], ident_sb[:, :])
                mm.then_inc(hT_ps, 1)

            def tile_out(t, r, e):
                pe.wait_ge(h_hi_ok, t + 1)
                if not isinstance(t, int) or t >= 2:
                    pe.wait_ge(y2_ok, t - 1)
                for n, (rows, w) in enumerate(((h_hi, w_hi_e), (h_lo, w_hi_e), (h_b, w_lo_e))):
                    if n > 0:
                        pe.wait_ge((h_lo_ok, h_b_ok)[n - 1], t + 1)
                    for c in range(FC):
                        first = c // 2 * HALF + 2 * F + (c % 2) * D
                        mm = pe.matmul(bank[4 + r % 2][:, 0:D], rows[:, c, :],
                                       w[:, ds(e, 1), first:first + D].rearrange("p a f -> p (a f)"),
                                       start=(n == 0 and c == 0), stop=(n == 2 and c == FC - 1))
                mm.then_inc(y_ps, 1)

            w_hi_e, w_lo_e = (w[:, :, :].rearrange("p (e h) n -> p e (h n)", h=2) for w in (w_hi, w_lo))

            def experts_of(t):
                both = pe.value_load(tile_ei[0:1, ds(t, 1)], min_val=0, max_val=E * E - 1)
                return ((both >> (E.bit_length() - 1)).with_bounds(min_val=0, max_val=E - 1),
                        (both & (E - 1)).with_bounds(min_val=0, max_val=E - 1))

            def tile(t, r, e, e_prev, prev, ahead):
                if prev:
                    h_T(t - 1)
                if e is None:
                    e_prev, e = experts_of(t)
                hidden(t, r, F, bank[2], e, sw_ps, h_ok)
                e_next = experts_of(t + 1)[1] if ahead > 0 else None
                if prev:
                    tile_out(t - 1, (r - 1) % RING, e_prev)
                if ahead > 1:
                    xs_T(t + 2, (r + 2) % RING)
                if ahead > 0:
                    hidden_in(t + 1, (r + 1) % RING, e_next)
                return e, e_next

            def hidden_in(t, r, e):
                pe.wait_ge(xs_lo_ok, t + 1)
                hidden(t, r, 0, bank[1], e, mid_ps, act_ok)

            def tiles(first, n, prev, left):
                e = e_prev = None
                for r in range(n):
                    e_prev, e = tile(first + r, r, e, e_prev, prev or r > 0, left + n - 1 - r)

            xs_T(0, 0)
            xs_T(1, 1)
            hidden_in(0, 0, experts_of(0)[1])
            tiles(0, RING, False, 2)
            with pe.Fori(1, TAIL // RING) as i:
                tiles(i * RING, RING, True, 2)
            tiles(TAIL, TILES - TAIL, True, 0)
            h_T(TILES - 1)
            tile_out(TILES - 1, (TILES - 1) % RING, experts_of(TILES - 1)[1])


            def z1_T(g, par):
                pe.wait_ge(z1_in[par], (g - par) * 8 + 16)
                at_least(pe, z1_lo_ok, g)
                for k in range(DC):
                    mm = chunk_transposes(z1[par], bank[k], k)
                mm.then_inc(z1T_ps, 1)

            def shared_out(g):
                at_least(pe, summed_ok, g)
                for half in range(2):
                    for c in range(FC):
                        if half == 0:
                            pe.wait_ge(h3_lo_ok, g * FC + (c + 1))
                        for t in (half, 2 + half):
                            for n, (rows, w) in enumerate(((h3_hi, shared_hi), (h3_hi, shared_lo), (h3_lo, shared_hi))):
                                mm = pe.matmul(bank[6 + t // 2][:, half * D:(half + 1) * D], rows[:, c, t * P:(t + 1) * P],
                                               w[2][:, c, :], start=(c == 0 and n == 0), stop=(c == FC - 1 and n == 2))
                mm.then_inc(o_ps, 1)

            def shared_hidden(g):
                pe.wait_ge(z1_lo_ok, g + 1)
                for c in range(FC):
                    for m, b, sig, free in ((0, 2, mid3_ps, act3_ok), (1, 4, sw3_ps, h3_ok)):
                        if not isinstance(g, int) or g * FC + c >= 2:
                            pe.wait_ge(free, g * FC + (c - 1))
                        for n, (w, rows) in enumerate(((shared_hi, z1_hi), (shared_lo, z1_hi), (shared_hi, z1_lo))):
                            for k in range(DC):
                                mm = pe.matmul(bank[b + c % 2][:, :], w[m][:, k, c * P:(c + 1) * P], rows[:, k, :],
                                               start=(n == 0 and k == 0), stop=(n == 2 and k == DC - 1))
                        mm.then_inc(sig, 1)

            def phase3(g, par):
                z1_T(g, par)
                if isinstance(g, int) and g == 0:
                    pe.wait_ge(y2_ok, TILES)
                    pe.wait_ge(shared_lo_ok, 6)
                if not (isinstance(g, int) and g == 0):
                    shared_out(g - 1)
                shared_hidden(g)

            groups(pe, phase3, 2)
            shared_out(GROUPS - 1)

        @block.scalar
        def _(act):
            def probs(g):
                act.wait_ge(s_ok, g + 1)
                at_least(act, pT_ps, g)
                at_least(act, rinv_ok, g)
                for t in range(NT):
                    a = act.activation(p_sb[:, t, :], s_sb[:, t, :], ACT.Exp, bias=nmax[:, t:t + 1], scale=-1.0,
                                       accum_out=rsum[:, t:t + 1])
                a.then_inc(p_ok, 1)

            def probs_T(g):
                act.wait_ge(pT_ps, g + 1)
                at_least(act, pv_ps, g * 2)
                act.activation(pT[:, :, :].rearrange("p t k -> p (t k)"), bank[2][:, :], ACT.Copy).then_inc(pT_ok, 1)

            def x1_T(g):
                act.wait_ge(x1T_ps, g + 1)
                act.activation(x1T[:, 0, :], bank[5][:, :], ACT.Copy).then_inc(x1T_act, 1)

            def gate_exp(g):
                act.wait_ge(logit_ok, g + 1)
                at_least(act, en1_ok, g)
                act.activation(en[:, :, :], logit[:, :, :], ACT.Exp, scale=-1.0).then_inc(en_ok, 1)

            def split_expert(g, raw=w_raw):
                act.wait_ge(expert_in, g * 48 + 48)
                act.activation(w_hi[:, ds(g, 1), :].rearrange("p a n -> p (a n)"), raw[:, :], ACT.Copy).then_inc(w_hi_ok, 1)

            def norm_apply1(g, par):
                act.wait_ge(shift_ok[0], g + 1)
                for t in range(NT // 2):
                    a = act.activation(x1row[par][:, t, 0:D], x1row[par][:, t, 0:D], ACT.Identity,
                                       bias=shift[:, t:t + 1], scale=rs[:, t:t + 1])
                a.then_inc(x1_act, 1)

            def x_hi(g, k):
                act.wait_ge(xT_ps, g * DC + (k + 1))
                act.activation(xT_hi[:, k, :], bank[k][:, :], ACT.Copy).then_inc(x_hi_ok, 1)

            def stage(g, par, prev, more):
                if prev:
                    probs(g - 1)
                if prev == 2:
                    gate_exp(g - 2)
                for c in range(DC):
                    act.wait_ge(q_ps, g * 2 + (c + 1))
                    a = act.activation(qT[:, c, :], bank[3 + c][:, :], ACT.Identity, bias=bq_sb[:, c:c + 1])
                    if prev and c == 0:
                        probs_T(g - 1)
                a.then_inc(q_ok, 1)
                if prev == 2:
                    split_expert(g - 2)
                for c in range(DC):
                    act.wait_ge(k_ps, g * 2 + (c + 1))
                    a = act.activation(kT[:, c, :], bank[c][:, :], ACT.Identity, bias=bk_sb[:, c:c + 1])
                a.then_inc(k_ok, 1)
                act.wait_ge(v_ps, g + 1)
                for c in range(2):
                    a = act.activation(v_sb[:, 2 * c:2 * c + 2, :].rearrange("p t e -> p (t e)"), bank[3 + c][:, :], ACT.Copy)
                a.then_inc(v_ok, 1)
                if prev:
                    norm_apply1(g - 1, 1 - par)
                if more:
                    x_hi(g + 1, 0)
                if prev:
                    x1_T(g - 1)
                if more:
                    x_hi(g + 1, 1)

            for i in range(3):
                c = slice(i * DC * D, (i + 1) * DC * D)
                act.wait_ge(attn_in[i], 16)
                act.activation(flat(w_qkv_hi[:, :, :])[:, c], w_raw[:, c], ACT.Copy).then_inc(qkv_hi_ok, 1)
            x_hi(0, 0)
            x_hi(0, 1)
            act.wait_ge(const_in, 16 * 7)
            stages(act, stage)
            last = GROUPS - 1
            probs(last)
            probs_T(last)
            gate_exp(last - 1)
            split_expert(last - 1)
            norm_apply1(last, 1)
            x1_T(last)
            gate_exp(last)
            split_expert(last, w_raw_last)

            def rows_hi(t, r):
                act.wait_ge(xsT_ps, t + 1)
                act.activation(xs_hi[r % 2][:, :, :].rearrange("p k c -> p (k c)"), bank[0][:, 0:D], ACT.Copy).then_inc(xs_hi_ok, 1)

            def silu(t, r):
                act.wait_ge(mid_ps, t + 1)
                act.wait_ge(gate_ok, t + 1)
                at_least(act, h_ok, t)
                act.activation(act2, bank[1][:, :], ACT.Silu, scale=gate[r % 2][:, 0:1]).then_inc(act_ok, 1)

            def hidden_hi(t, r):
                act.wait_ge(hT_ps, t + 1)
                act.activation(h_hi[:, :, :].rearrange("p c k -> p (c k)"), bank[3][:, :], ACT.Copy).then_inc(h_hi_ok, 1)
                act.wait_ge(h_hi_ok, t + 1)
                act.activation(h_b.rearrange("p c k -> p (c k)"), f32(h_hi[:, :, :].rearrange("p c k -> p (c k)")),
                               ACT.Copy).then_inc(h_b_ok, 1)

            def copy_out(t, r):
                act.wait_ge(y_ps, t + 1)
                if not isinstance(t, int) or t >= RING:
                    act.wait_ge(y_stored[r], (t - r) * (16 // RING))
                act.activation(y2[r], bank[4 + r % 2][:, 0:D], ACT.Copy).then_inc(y2_ok, 1)

            def tile(t, r, prev, ahead):
                if ahead:
                    rows_hi(t + 1, (r + 1) % RING)
                silu(t, r)
                if prev:
                    hidden_hi(t - 1, (r - 1) % RING)
                    copy_out(t - 1, (r - 1) % RING)

            rows_hi(0, 0)
            for t in range(2 * RING):
                tile(t, t % RING, t > 0, True)
            with act.Fori(2, TAIL // RING) as i:
                for r in range(RING):
                    tile(i * RING + r, r, True, True)
            for t in range(TAIL, TILES):
                tile(t, t % RING, True, t < TILES - 1)
            hidden_hi(TILES - 1, (TILES - 1) % RING)
            copy_out(TILES - 1, (TILES - 1) % RING)

            def shared_act(g):
                act.wait_ge(z1T_ps, g + 1)
                for k in range(DC):
                    a = act.activation(z1_hi[:, k, :], bank[k][:, :], ACT.Copy)
                a.then_inc(z1_hi_ok, 1)
                if not (isinstance(g, int) and g < 2):
                    norm_apply(g - 2)
                for c in range(FC):
                    act.wait_ge(mid3_ps, g * FC + (c + 1))
                    if not isinstance(g, int) or g * FC + c >= 2:
                        act.wait_ge(h3_ok, g * FC + (c - 1))
                    act.activation(act3[c % 2], bank[2 + c % 2][:, :], ACT.Silu).then_inc(act3_ok, 1)
                    if c > 0:
                        shared_h_hi(g, c - 1)
                shared_h_hi(g, FC - 1)

            def shared_h_hi(g, c):
                act.wait_ge(h3_ok, g * FC + (c + 1))
                act.activation(h3_hi[:, c, :], h3[c % 2], ACT.Copy).then_inc(h3_hi_ok, 1)

            def norm_apply(g, z=z_sb, tiles=NT):
                act.wait_ge(shift_ok[1], g + 1)
                at_least(act, o_stored, g * 16)
                for t in range(tiles):
                    a = act.activation(o_sb[:, t, :], z[:, t, :], ACT.Identity, bias=shift[:, t:t + 1], scale=rs[:, t:t + 1])
                a.then_inc(o_ok, 1)

            shared_act(0)
            shared_act(1)
            shared_act(2)
            with act.Fori(3, GROUPS) as g:
                shared_act(g)
            norm_apply(GROUPS - 2)
            norm_apply(GROUPS - 1, z1[1], NT // 2)

        @block.vector
        def _(dve):
            def x_lo(g):
                for k in range(DC):
                    dve.wait_ge(x_hi_ok, g * DC + (k + 1))
                    i = dve.tensor_tensor(xT_lo[:, k, :], bank[k][:, :], f32(xT_hi[:, k, :]), ALU.subtract)
                i.then_inc(x_lo_ok, 1)

            for i in range(3):
                c = slice(i * DC * D, (i + 1) * DC * D)
                dve.wait_ge(qkv_hi_ok, i + 1)
                dve.tensor_tensor(flat(w_qkv_lo[:, :, :])[:, c], w_raw[:, c], f32(flat(w_qkv_hi[:, :, :])[:, c]), ALU.subtract)\
                   .then_inc(qkv_lo_ok, 1)
            x_lo(0)
            dve.wait_ge(const_in, 16 * 7)
            dve.tensor_copy(trib[:, :, :], tri_sb).then_inc(tri_ok, 1)
            dve.sem_inc(added_ok, 2)

            def norm_stats(which, n, src):
                for t in range(NT):
                    i = dve.bn_stats(stats[:, t, :], src[:, t, :])
                i.then_inc(stats_ok[which], 1)
                wait_apart(dve, stats_ok[which], n)
                for t in range(NT):
                    i = dve.bn_aggr(mv[:, t, :], stats[:, t, :])
                i.then_inc(mv_ok[which], 1)

            def norm_root(which, n):
                dve.wait_ge(mv_ok[which], n)
                dve.tensor_scalar(veps[:, :], mv[:, :, 1], EPS, None, ALU.add).then_inc(veps_ok[which], 1)
                dve.wait_ge(veps_ok[which], n)
                dve.tensor_scalar(halfi[:, :], veps[:, :].bitcast(I32), 1, None, ALU.logical_shift_right).then_inc(half_ok[which], 1)
                dve.wait_ge(half_ok[which], n)
                dve.tensor_scalar(rs[:, :].bitcast(I32), halfi[:, :], -1.0, float(RSQRT_MAGIC), ALU.mult, ALU.add)\
                   .then_inc(rs_ok[which][0], 1)
                for s in range(NEWTON):
                    dve.wait_ge(rs_ok[which][s], n)
                    dve.tensor_tensor(rs_a[:, :], rs[:, :], rs[:, :], ALU.mult).then_inc(rsa_ok[which][s], 1)
                    dve.wait_ge(rsa_ok[which][s], n)
                    dve.scalar_tensor_tensor(out=rs_b[:, :], in0=rs_a[:, :], scalar=-0.5, in1=veps[:, :],
                                             op0=ALU.mult, op1=ALU.mult).then_inc(rsb_ok[which][s], 1)
                    dve.wait_ge(rsb_ok[which][s], n)
                    dve.scalar_tensor_tensor(out=rs[:, :], in0=rs_b[:, :], scalar=1.5, in1=rs[:, :],
                                             op0=ALU.add, op1=ALU.mult).then_inc(rs_ok[which][s + 1], 1)
                dve.wait_ge(rs_ok[which][NEWTON], n)
                dve.scalar_tensor_tensor(out=shift[:, :], in0=mv[:, :, 0], scalar=-1.0, in1=rs[:, :],
                                         op0=ALU.mult, op1=ALU.mult).then_inc(shift_ok[which], 1)

            def attn_sum(g, par):
                dve.wait_ge(rinv_ok, g + 1)
                dve.wait_ge(x_bias_ok, g + 1)
                if not isinstance(g, int) or g >= 2:
                    dve.wait_ge(scattered[par], (g - par) * (8 * TOP_K * NT))
                    dve.wait_ge(x1_stored[par], (g - par) * 8)
                for t in range(NT):
                    if t % 2 == 0:
                        dve.wait_ge(pv_ps, g * 2 + (t // 2 + 1))
                    i = dve.scalar_tensor_tensor(out=x1row[par][:, t, 0:D], in0=bank[5 + t // 2][:, (t % 2) * D:(t % 2 + 1) * D],
                                                 scalar=rinv[:, t:t + 1], in1=x_sb[par][:, t, :], op0=ALU.mult, op1=ALU.add)
                i.then_inc(y_ok, 1)
                dve.wait_ge(y_ok, g + 1)
                norm_stats(0, g + 1, x1row[par][:, :, 0:D])
                norm_root(0, g + 1)
                dve.wait_ge(shift_ok[0], g + 1)
                for t in range(NT // 2, NT):
                    i = dve.tensor_scalar(x1row[par][:, t, 0:D], x1row[par][:, t, 0:D], rs[:, t:t + 1], shift[:, t:t + 1],
                                          ALU.mult, ALU.add)
                i.then_inc(x1_dve, 1)

            def x1_T(g):
                dve.wait_ge(x1T_ps, g + 1)
                dve.tensor_copy(x1T[:, 1, :], bank[6][:, :]).then_inc(x1T_dve, 1)

            def choose(g, par):
                dve.wait_ge(logit_ps, g + 1)
                at_least(dve, en_ok, g)
                dve.tensor_copy(logit[:, :, :].rearrange("p t e -> p (t e)"), bank[7][:, 0:NT * E]).then_inc(logit_ok, 1)
                wait_apart(dve, logit_ok, g + 1)
                for t in range(NT):
                    i = dve.max(top[:, t, :], logit[:, t, :])
                i.then_inc(top_ok, 1)
                wait_apart(dve, top_ok, g + 1)
                for t in range(NT):
                    i = dve.max_index(topi[:, t, :], top[:, t, :], logit[:, t, :])
                i.then_inc(topi_ok, 1)
                dve.wait_ge(topi_ok, g + 1)
                dve.tensor_copy(topf[:, :, :], topi[:, :, 0:TOP_K].rearrange("p t k -> p k t")).then_inc(topf_ok, 1)
                dve.wait_ge(topf_ok, g + 1)
                sel_g = sel[:, ds(g, 1), :, :].rearrange("p a j e -> p (a j) e")
                dve.tensor_tensor(sel_g,
                                  exp_sb[:, 0, :].unsqueeze(1).to_broadcast([P, TOP_K * NT, E]),
                                  topf[:, :, :].rearrange("p k t -> p (k t)").unsqueeze(2).to_broadcast([P, TOP_K * NT, E]),
                                  ALU.is_equal).then_inc(sel_ok, 1)
                dve.wait_ge(sel_ok, g + 1)
                at_least(dve, rank_ps, g)
                dve.tensor_tensor(chosen[:, :, :], sel_g[:, 0:NT, :], sel_g[:, NT:2 * NT, :], ALU.add).then_inc(chosen_ok, 1)

            def gates(g, par):
                dve.wait_ge(en_ok, g + 1)
                dve.tensor_scalar(en[:, :, :], en[:, :, :], 1.0, None, ALU.add).then_inc(en1_ok, 1)
                dve.wait_ge(en1_ok, g + 1)
                dve.reciprocal(x1row[par][:, :, D:ROW], en[:, :, :]).then_inc(gates_ok, 1)

            def place_rows(g, par):
                dve.wait_ge(rank_ps, g + 1)
                at_least(dve, place2_ok, g)
                dve.tensor_tensor(place[:, :, :], bank[7][:, 64:64 + NT * E].rearrange("p (t e) -> p t e", t=NT),
                                  count[:, :].unsqueeze(1).to_broadcast([P, NT, E]), ALU.add).then_inc(place_ok, 1)
                dve.wait_ge(place_ok, g + 1)
                dve.tensor_tensor(count[:, :], bank[7][:, 128:128 + E], count[:, :], ALU.add).then_inc(count_ok, 1)
                sel_g = sel[:, ds(g, 1), :, :].rearrange("p a j e -> p (a j) e")
                for k in range(TOP_K):
                    i = dve.tensor_tensor(place2[:, k, :, :], sel_g[:, k * NT:(k + 1) * NT, :], place[:, :, :], ALU.mult)
                i.then_inc(place2_ok, 1)
                dve.wait_ge(place2_ok, g + 1)
                slot_g = slot_f[:, ds(g, 1), :].rearrange("p a j -> p (a j)")
                dve.tensor_reduce(slot_g, place2[:, :, :, :].rearrange("p k t e -> p (k t) e"), AX.X, ALU.add)\
                   .then_inc(slotf_ok, 1)
                dve.wait_ge(slotf_ok, g + 1)
                dve.tensor_scalar(slot_i[:, par, :, :].rearrange("p k t -> p (k t)"), slot_g, 0.0, None,
                                  ALU.add).then_inc(slot_ok, 1)
                dve.wait_ge(count_ok, g + 1)

            def scores(g):
                wait_apart(dve, s_ps, g + 1)
                at_least(dve, pT_ps, g)
                for t in range(NT):
                    i = dve.tensor_tensor_reduce(s_sb[:, t, :], bank[2][:, t * P:(t + 1) * P], mask_sb[:, :], -1.0, BIG,
                                                 ALU.add, ALU.min, nmax[:, t:t + 1])
                i.then_inc(s_ok, 1)

            def stage(g, par, prev, more):
                dve.wait_ge(x_lo_ok, g + 1)
                if prev == 2:
                    choose(g - 2, par)
                if prev:
                    dve.wait_ge(p_ok, g)
                    dve.reciprocal(rinv[:, :], rsum[:, :]).then_inc(rinv_ok, 1)
                if prev == 2:
                    place_rows(g - 2, par)
                    gates(g - 2, par)
                if prev:
                    attn_sum(g - 1, 1 - par)
                scores(g)
                if prev:
                    x1_T(g - 1)
                if more:
                    x_lo(g + 1)

            dve.tensor_copy(count[:, :], exp_sb[:, 1, :]).then_inc(start_ok, 1)
            dve.wait_ge(start_ok, 1)
            stages(dve, stage)
            last = GROUPS - 1
            dve.wait_ge(p_ok, GROUPS)
            dve.reciprocal(rinv[:, :], rsum[:, :]).then_inc(rinv_ok, 1)
            choose(last - 1, 0)
            attn_sum(last, 1)
            place_rows(last - 1, 0)
            gates(last - 1, 0)
            x1_T(last)
            choose(last, 1)
            place_rows(last, 1)
            gates(last, 1)

            steps = [0]

            def step(i):
                steps[0] += 1
                i.then_inc(t_step, 1)
                dve.wait_ge(t_step, steps[0])

            dve.wait_ge(t_iota, 2)
            dve.wait_ge(count_ok, GROUPS)
            dve.tensor_copy(end_i[:, :], count[:, :]).then_inc(t_pad, 1)
            step(dve.tensor_tensor(tiles_f[:, 0, 0:E], count[:, :], exp_sb[:, 1, :], ALU.subtract))
            step(dve.tensor_scalar(cnt_i[:, :], tiles_f[:, 0, 0:E], float(P - 1), None, ALU.add))
            step(dve.tensor_scalar(tiles_i[:, :], cnt_i[:, :], P.bit_length() - 1, None, ALU.logical_shift_right))
            step(dve.tensor_copy(hop[:, :], tiles_i[:, :]))
            end = [tiles_f[:, 0, 0:E], tiles_f[:, 1, 0:E]]
            step(dve.tensor_copy(end[0], hop[:, :]))
            n = 0
            s = 1
            while s < E:
                step(dve.tensor_copy(end[1 - n][:, 0:s], end[n][:, 0:s]))
                step(dve.tensor_tensor(end[1 - n][:, s:E], end[n][:, s:E], end[n][:, 0:E - s], ALU.add))
                n = 1 - n
                s *= 2
            ends = end[n]
            step(dve.tensor_tensor(base_d[:, :], ends, hop[:, :], ALU.subtract))
            step(dve.scalar_tensor_tensor(out=base_d[:, :], in0=base_d[:, :], scalar=float(P), in1=exp_sb[:, 1, :],
                                          op0=ALU.mult, op1=ALU.subtract))
            step(dve.memset(past[:, :, 0], 1.0))
            step(dve.tensor_tensor(past[:, :, 1:E + 1], tile_no[:, :].unsqueeze(2).to_broadcast([P, TILES, E]),
                                   ends.unsqueeze(1).to_broadcast([P, TILES, E]), ALU.is_ge))
            step(dve.tensor_reduce(tile_e, past[0:1, :, 1:E + 1], AX.X, ALU.add))
            step(dve.tensor_scalar(tile_e, tile_e, float(E - 1), None, ALU.min))
            step(dve.tensor_copy(tile_ei[:, 0:1], tile_e[:, 0:1]))
            step(dve.scalar_tensor_tensor(out=tile_ei[:, 1:TILES], in0=tile_e[:, 0:TILES - 1], scalar=float(E),
                                          in1=tile_e[:, 1:TILES], op0=ALU.mult, op1=ALU.add))
            step(dve.tensor_scalar(hop[:, :], hop[:, :], -1.0, float(QBLOCKS), ALU.mult, ALU.add))
            step(dve.tensor_tensor(walk[0:1, :, :], past[0:1, :, 1:E + 1],
                                   hop[0:1, :].unsqueeze(1).to_broadcast([1, TILES, E]), ALU.mult))
            step(dve.tensor_reduce(tile_b, walk[0:1, :, :], AX.X, ALU.add))
            step(dve.tensor_tensor(tile_b, tile_b, tile_no[0:1, :], ALU.add))
            dve.tensor_scalar(tile_bi, tile_b, float(E * QBLOCKS), None, ALU.min).then_inc(tables_ok, 1)
            step(dve.tensor_tensor(onehot, past[:, :, 0:E], past[:, :, 1:E + 1], ALU.subtract))
            step(dve.tensor_tensor(ysel[:, :, :], sel[:, :, :, :].rearrange("p g j e -> p (g j) e"),
                                   base_d[:, :].unsqueeze(1).to_broadcast([P, GROUPS * TOP_K * NT, E]), ALU.mult))
            yslot = s_sb[:, 0, :]
            step(dve.tensor_reduce(yslot, ysel[:, :, :], AX.X, ALU.add))
            dve.tensor_tensor(yslot_i, yslot,
                              slot_f[:, :, :].rearrange("p g j -> p (g j)"), ALU.add).then_inc(yslot_ok, 1)

            def gate_of(t, r):
                dve.wait_ge(xs_in[r], 16 * (t // RING + 1) if isinstance(t, int) else (t - r) * (16 // RING) + 16)
                at_least(dve, gate_ok, t)
                dve.tensor_tensor(gate_j[:, :], xs[r][:, D:ROW], onehot[:, ds(t, 1), :].rearrange("p a e -> p (a e)"),
                                  ALU.mult).then_inc(gatej_ok, 1)
                dve.wait_ge(gatej_ok, t + 1)
                dve.tensor_reduce(gate[r % 2][:, 0:1], gate_j[:, :], AX.X, ALU.add).then_inc(gate_ok, 1)

            def rows_lo(t, r):
                dve.wait_ge(xs_hi_ok, t + 1)
                dve.tensor_tensor(xs_lo[r % 2][:, :, :].rearrange("p k c -> p (k c)"), bank[0][:, 0:D],
                                  f32(xs_hi[r % 2][:, :, :].rearrange("p k c -> p (k c)")), ALU.subtract)
                dve.tensor_copy(xs_b[r % 2][:, :, :].rearrange("p k c -> p (k c)"),
                                f32(xs_hi[r % 2][:, :, :].rearrange("p k c -> p (k c)"))).then_inc(xs_lo_ok, 1)

            def hidden_lo(t, r):
                dve.wait_ge(h_hi_ok, t + 1)
                dve.tensor_tensor(h_lo[:, :, :].rearrange("p c k -> p (c k)"), bank[3][:, :],
                                  f32(h_hi[:, :, :].rearrange("p c k -> p (c k)")), ALU.subtract).then_inc(h_lo_ok, 1)

            def product(t, r):
                dve.wait_ge(act_ok, t + 1)
                dve.wait_ge(sw_ps, t + 1)
                dve.wait_ge(gate_ok, t + 1)
                at_least(dve, hT_ps, t)
                dve.scalar_tensor_tensor(out=h2, in0=bank[2][:, :], scalar=gate[r % 2][:, 0:1],
                                         in1=act2, op0=ALU.mult, op1=ALU.mult).then_inc(h_ok, 1)

            def tile(t, r, prev, ahead):
                if ahead:
                    gate_of(t + 1, (r + 1) % RING)
                    rows_lo(t + 1, (r + 1) % RING)
                if prev:
                    hidden_lo(t - 1, (r - 1) % RING)
                product(t, r)

            gate_of(0, 0)
            rows_lo(0, 0)
            for t in range(RING):
                tile(t, t, t > 0, True)
            with dve.Fori(1, TAIL // RING) as i:
                for r in range(RING):
                    tile(i * RING + r, r, True, True)
            for t in range(TAIL, TILES):
                tile(t, t % RING, True, t < TILES - 1)
            hidden_lo(TILES - 1, (TILES - 1) % RING)

            def add_experts(g, par):
                dve.wait_ge(pair_ok, g + 1)
                dve.wait_ge(z1_in[par], (g - par) * 8 + 16)
                at_least(dve, o_ok, g)
                dve.tensor_tensor(z_sb[:, :, :], z1[par], yg[par][:, 0:NT, :], ALU.add).then_inc(added_ok, 1)

            def add_last_experts():
                dve.wait_ge(pair_ok, GROUPS)
                dve.wait_ge(z1T_ps, GROUPS)
                dve.tensor_tensor(z1[1], z1[1], yg[1][:, 0:NT, :], ALU.add).then_inc(added_ok, 1)

            def apply_last():
                dve.wait_ge(shift_ok[1], GROUPS)
                dve.wait_ge(o_stored, (GROUPS - 1) * 16)
                for t in range(NT // 2, NT):
                    i = dve.tensor_scalar(o_sb[:, t, :], z1[1][:, t, :], rs[:, t:t + 1], shift[:, t:t + 1], ALU.mult, ALU.add)
                i.then_inc(o_half_ok, 1)

            def add_shared(g, z):
                dve.wait_ge(added_ok, g + 3)
                dve.wait_ge(o_ps, g + 1)
                for c in range(2):
                    i = dve.tensor_tensor(z[:, 2 * c:2 * c + 2, :], bank[6 + c][:, :].rearrange("p (t d) -> p t d", t=2),
                                          z[:, 2 * c:2 * c + 2, :], ALU.add)
                i.then_inc(summed_ok, 1)

            def stats_of_sum(g, z):
                dve.wait_ge(summed_ok, g + 1)
                norm_stats(1, g + 1, z)

            def z1_lo_of(g):
                dve.wait_ge(z1_hi_ok, g + 1)
                for k in range(DC):
                    i = dve.tensor_tensor(z1_lo[:, k, :], bank[k][:, :], f32(z1_hi[:, k, :]), ALU.subtract)
                i.then_inc(z1_lo_ok, 1)

            def shared_product(g, c):
                dve.wait_ge(act3_ok, g * FC + (c + 1))
                dve.wait_ge(sw3_ps, g * FC + (c + 1))
                if not isinstance(g, int) or g * FC + c >= 2:
                    dve.wait_ge(h3_lo_ok, g * FC + (c - 1))
                dve.tensor_tensor(h3[c % 2], bank[4 + c % 2][:, :], act3[c % 2], ALU.mult).then_inc(h3_ok, 1)

            def shared_lo_of(g, c):
                dve.wait_ge(h3_hi_ok, g * FC + (c + 1))
                dve.tensor_tensor(h3_lo[:, c, :], h3[c % 2], f32(h3_hi[:, c, :]), ALU.subtract).then_inc(h3_lo_ok, 1)

            def phase3(g, par, prev):
                z1_lo_of(g)
                if prev:
                    add_experts(g - 1, 1 - par)
                    add_shared(g - 1, z_sb)
                for c in range(FC):
                    shared_product(g, c)
                    if prev and c == 0:
                        stats_of_sum(g - 1, z_sb)
                    if c < 2:
                        shared_lo_of(g, c)
                shared_lo_of(g, 2)
                shared_lo_of(g, 3)
                if prev:
                    norm_root(1, g)

            phase3(0, 0, False)
            phase3(1, 1, True)
            with dve.Fori(0, (GROUPS - 2) // 2) as i:
                for u in range(2):
                    phase3(i * 2 + (2 + u), u, True)
            add_last_experts()
            add_shared(GROUPS - 1, z1[1])
            stats_of_sum(GROUPS - 1, z1[1])
            dve.wait_ge(o_ok, GROUPS - 1)
            norm_root(1, GROUPS)
            apply_last()


OUT_SHAPE = (16, 512, 256)


def kernel(L0_attn_x, L0_attn_Wq, L0_attn_bq, L0_attn_Wk, L0_attn_bk, L0_attn_Wv, L0_attn_bv, L0_ffn_router_DE,
           L0_ffn_w_in_shared_FD, L0_ffn_w_out_shared_DF, L0_ffn_w_swiglu_FD, L0_ffn_w_in_eDF, L0_ffn_w_swiglu_eDF,
           L0_ffn_w_out_eFD):
    import numpy as np
    import concourse.bacc as bacc
    from concourse.bass_utils import run_bass_kernel_spmd

    blocks = np.arange(P) // BLOCK
    feeds = {
        "x": L0_attn_x, "wqT": np.transpose(L0_attn_Wq), "wkT": np.transpose(L0_attn_Wk), "wvT": np.transpose(L0_attn_Wv),
        "bq": np.asarray(L0_attn_bq).reshape(DC, P).T, "bk": np.asarray(L0_attn_bk).reshape(DC, P).T, "bv": np.broadcast_to(np.asarray(L0_attn_bv)[None, :], (P, D)),
        "router": L0_ffn_router_DE, "w_in_shT": np.transpose(L0_ffn_w_in_shared_FD),
        "w_sw_shT": np.transpose(L0_ffn_w_swiglu_FD), "w_out_shT": np.transpose(L0_ffn_w_out_shared_DF),
        "w_in": L0_ffn_w_in_eDF, "w_sw": L0_ffn_w_swiglu_eDF, "w_out": L0_ffn_w_out_eFD,
        "ident": np.eye(P, dtype=np.float32),
        "mask": np.where(blocks[:, None] == blocks[None, :], 0.0, OFF_BLOCK).astype(np.float32),
        "tri": np.stack([np.triu(np.ones((P, P), np.float32), 1), np.ones((P, P), np.float32)], 1),
        "experts": np.broadcast_to(np.stack([np.arange(E), np.arange(E) * QROWS]).astype(np.float32)[None], (P, 2, E)),
    }
    nc = bacc.Bacc("TRN2", target_bir_lowering=False, num_devices=1)
    arrays, args = {}, {}
    for name, a in feeds.items():
        a = np.ascontiguousarray(a)
        arrays[f"in_{name}"] = a
        args[name] = nc.dram_tensor(f"in_{name}", a.shape, mybir.dt.from_np(a.dtype), kind="ExternalInput").ap()
    args["out"] = nc.dram_tensor("out_0", OUT_SHAPE, F32, kind="ExternalOutput").ap()
    build(nc, **args)
    return run_bass_kernel_spmd(nc, [arrays], core_ids=[0]).results[0]["out_0"]
```
